# Optimizing a Trainium2 kernel written in Bass

```python
import numpy as np
import jax
import jax.numpy as jnp

def _softmax(x, axis=-1):
    return jax.nn.softmax(x, axis=axis)

def _gelu(x):
    return jax.nn.gelu(x, approximate=True)

def _silu(x):
    return jax.nn.silu(x)

def _sigmoid(x):
    return jax.nn.sigmoid(x)

def _layernorm(x, axis=-1, eps=1e-05):
    m = jnp.mean(x, axis=axis, keepdims=True)
    v = jnp.var(x, axis=axis, keepdims=True)
    return (x - m) / jnp.sqrt(v + eps)

def _scatter_add(tgt, idx, src, axis=0):
    return tgt.at[idx].add(src)

def _segment_sum(src, seg, n):
    return jax.ops.segment_sum(src, seg, n)
kernel_name = 'mk_adj_preln_d4_adj_r2_0491ed'

def setup_inputs(seed: int=0):
    np.random.seed(seed)
    _w = jnp.asarray

    def _rec_inputs():
        import jax
        import jax.numpy as jnp
        _gk = jax.random.key(seed)
        x = -0.0005207 + 1.001 * jax.random.normal(jax.random.fold_in(_gk, 1), (64, 128, 128), jnp.float32)
        _a = jax.random.bernoulli(jax.random.fold_in(_gk, 2), 0.03125, (64, 128, 128))
        _a = jnp.logical_or(_a, jnp.swapaxes(_a, -1, -2))
        _a = jnp.logical_or(_a, jnp.eye(128, dtype=bool))
        _af = _a.astype(jnp.float32)
        _af = _af * jax.random.uniform(jax.random.fold_in(_gk, 3), (64, 128, 128), jnp.float32, 0.05, 1)
        adj = _af
        return (x, adj)
    x, adj = _rec_inputs()

    def _L0_gnn_setup():
        import jax, jax.numpy as jnp
        import numpy as np
        B, N, DIN, DOUT = (8, 1024, 128, 128)
        key = jax.random.key(seed)
        k1, k2, k3, k4 = jax.random.split(key, 4)
        x = jax.random.normal(k1, (B, N, DIN), dtype=jnp.float32)
        adj = jax.random.uniform(k2, (B, N, N), dtype=jnp.float32)
        W = jax.random.normal(k3, (DIN, DOUT), dtype=jnp.float32) / np.sqrt(DIN)
        b = jax.random.normal(k4, (DOUT,), dtype=jnp.float32) * 0.01
        return {'x': x, 'adj': adj, 'W': W, 'b': b}
    _L0_gnn_all = _L0_gnn_setup()
    _L0_gnn_in = {k: v for k, v in _L0_gnn_all.items() if k in ('W', 'b')}
    del _L0_gnn_all

    def _L1_gnn_setup():
        import jax, jax.numpy as jnp
        import numpy as np
        B, N, NAB, NF, NG = (8, 128, 128, 128, 64)
        CUTOFF = 5.0
        LN2 = float(np.log(2.0))

        def ssp(x):
            return jax.nn.softplus(x) - LN2
        key = jax.random.key(seed)
        ks = jax.random.split(key, 12)
        r = jax.random.normal(ks[0], (B, N, NAB), dtype=jnp.float32)
        e = jax.random.uniform(ks[1], (B, N, N), dtype=jnp.float32) * CUTOFF
        A = (jax.random.uniform(ks[2], (B, N, N)) < 0.3).astype(jnp.float32)
        s = 0.05
        W1 = jax.random.normal(ks[3], (NF, NG), dtype=jnp.float32) * s
        b1 = jnp.zeros((NF,), jnp.float32)
        W2 = jax.random.normal(ks[4], (NF, NF), dtype=jnp.float32) * s
        b2 = jnp.zeros((NF,), jnp.float32)
        Wa = jax.random.normal(ks[5], (NF, NAB), dtype=jnp.float32) * s
        Wd1 = jax.random.normal(ks[6], (NAB, NF), dtype=jnp.float32) * s
        bd1 = jnp.zeros((NAB,), jnp.float32)
        Wd2 = jax.random.normal(ks[7], (NAB, NAB), dtype=jnp.float32) * s
        bd2 = jnp.zeros((NAB,), jnp.float32)
        return {'r': r, 'e': e, 'A': A, 'W1': W1, 'b1': b1, 'W2': W2, 'b2': b2, 'Wa': Wa, 'Wd1': Wd1, 'bd1': bd1, 'Wd2': Wd2, 'bd2': bd2}
    _L1_gnn_all = _L1_gnn_setup()
    _L1_gnn_in = {k: v for k, v in _L1_gnn_all.items() if k in ('W1', 'b1', 'W2', 'b2', 'Wa', 'Wd1', 'bd1', 'Wd2', 'bd2')}
    del _L1_gnn_all

    def _L2_gnn_setup():
        import jax, jax.numpy as jnp
        import numpy as np
        B, N, H = (8, 1024, 128)
        key = jax.random.key(seed)
        ks = jax.random.split(key, 8)
        s = 1.0 / np.sqrt(H)
        return {'h': jax.random.normal(ks[0], (B, N, H), dtype=jnp.float32), 'A': jax.random.uniform(ks[1], (B, N, N), dtype=jnp.float32), 'W1': jax.random.normal(ks[2], (H, H), dtype=jnp.float32) * s, 'b1': jnp.zeros((H,), dtype=jnp.float32), 'W2': jax.random.normal(ks[3], (H, H), dtype=jnp.float32) * s, 'b2': jnp.zeros((H,), dtype=jnp.float32), 'W_ih': jax.random.normal(ks[4], (3 * H, H), dtype=jnp.float32) * s, 'W_hh': jax.random.normal(ks[5], (3 * H, H), dtype=jnp.float32) * s, 'b_ih': jnp.zeros((3 * H,), dtype=jnp.float32), 'b_hh': jnp.zeros((3 * H,), dtype=jnp.float32)}
    _L2_gnn_all = _L2_gnn_setup()
    _L2_gnn_in = {k: v for k, v in _L2_gnn_all.items() if k in ('W1', 'b1', 'W2', 'b2', 'W_ih', 'W_hh', 'b_ih', 'b_hh')}
    del _L2_gnn_all

    def _L3_gnn_setup():
        import jax, jax.numpy as jnp
        import numpy as np
        B, N, D, OUT = (4, 256, 128, 128)
        key = jax.random.key(seed)
        k1, k2, k3, k4 = jax.random.split(key, 4)
        x = jax.random.normal(k1, (B, N, D), dtype=jnp.float32)
        adj = (jax.random.uniform(k2, (B, N, N)) < 0.5).astype(jnp.float32)
        W = jax.random.normal(k3, (2 * D, OUT), dtype=jnp.float32) * (1.0 / np.sqrt(2 * D))
        b = jax.random.normal(k4, (OUT,), dtype=jnp.float32) * 0.01
        return {'x': x, 'adj': adj, 'W': W, 'b': b}
    _L3_gnn_all = _L3_gnn_setup()
    _L3_gnn_in = {k: v for k, v in _L3_gnn_all.items() if k in ('W', 'b')}
    del _L3_gnn_all
    return {'x': x, 'adj': adj, 'L0_gnn_W': _L0_gnn_in['W'], 'L0_gnn_b': _L0_gnn_in['b'], 'L1_gnn_W1': _L1_gnn_in['W1'], 'L1_gnn_b1': _L1_gnn_in['b1'], 'L1_gnn_W2': _L1_gnn_in['W2'], 'L1_gnn_b2': _L1_gnn_in['b2'], 'L1_gnn_Wa': _L1_gnn_in['Wa'], 'L1_gnn_Wd1': _L1_gnn_in['Wd1'], 'L1_gnn_bd1': _L1_gnn_in['bd1'], 'L1_gnn_Wd2': _L1_gnn_in['Wd2'], 'L1_gnn_bd2': _L1_gnn_in['bd2'], 'L2_gnn_W1': _L2_gnn_in['W1'], 'L2_gnn_b1': _L2_gnn_in['b1'], 'L2_gnn_W2': _L2_gnn_in['W2'], 'L2_gnn_b2': _L2_gnn_in['b2'], 'L2_gnn_W_ih': _L2_gnn_in['W_ih'], 'L2_gnn_W_hh': _L2_gnn_in['W_hh'], 'L2_gnn_b_ih': _L2_gnn_in['b_ih'], 'L2_gnn_b_hh': _L2_gnn_in['b_hh'], 'L3_gnn_W': _L3_gnn_in['W'], 'L3_gnn_b': _L3_gnn_in['b']}

def reference(x, adj, L0_gnn_W, L0_gnn_b, L1_gnn_W1, L1_gnn_b1, L1_gnn_W2, L1_gnn_b2, L1_gnn_Wa, L1_gnn_Wd1, L1_gnn_bd1, L1_gnn_Wd2, L1_gnn_bd2, L2_gnn_W1, L2_gnn_b1, L2_gnn_W2, L2_gnn_b2, L2_gnn_W_ih, L2_gnn_W_hh, L2_gnn_b_ih, L2_gnn_b_hh, L3_gnn_W, L3_gnn_b):
    import jax
    import jax.numpy as jnp

    def _L0_gnn_ref(x, adj, W, b):
        import jax, jax.numpy as jnp
        import numpy as np
        B, N, DIN, DOUT = (8, 1024, 128, 128)
        degree = jnp.sum(adj, axis=2)
        d_norm = 1.0 / jnp.sqrt(degree + 1e-08)
        adj_norm = d_norm[:, :, None] * adj * d_norm[:, None, :]
        support = jnp.einsum('bnm,bmd->bnd', adj_norm, x)
        return support @ W + b

    def _L1_gnn_ref(r, e, A, W1, b1, W2, b2, Wa, Wd1, bd1, Wd2, bd2):
        import jax, jax.numpy as jnp
        import numpy as np
        B, N, NAB, NF, NG = (8, 128, 128, 128, 64)
        CUTOFF = 5.0
        LN2 = float(np.log(2.0))

        def ssp(x):
            return jax.nn.softplus(x) - LN2
        offsets = jnp.linspace(0.0, CUTOFF, NG, dtype=jnp.float32)
        width = offsets[1] - offsets[0]
        coeff = -0.5 / (width * width)
        diff = e[:, :, :, None] - offsets
        g = jnp.exp(coeff * diff * diff)
        h = ssp(jnp.einsum('bijg,fg->bijf', g, W1) + b1)
        Wf = jnp.einsum('bijf,gf->bijg', h, W2) + b2
        rf = jnp.einsum('bjd,fd->bjf', r, Wa)
        Am = A[:, :, :, None]
        Wf = Wf * Am
        y = jnp.einsum('bjf,bijf->bif', rf, Wf * Am)
        y = ssp(jnp.einsum('bif,df->bid', y, Wd1) + bd1)
        y = jnp.einsum('bid,ed->bie', y, Wd2) + bd2
        return y

    def _L2_gnn_ref(h, A, W1, b1, W2, b2, W_ih, W_hh, b_ih, b_hh):
        import jax, jax.numpy as jnp
        import numpy as np
        B, N, H = (8, 1024, 128)
        m = jax.nn.relu(jnp.einsum('bnh,oh->bno', h, W1) + b1)
        m = jax.nn.relu(jnp.einsum('bnh,oh->bno', m, W2) + b2)
        msg = jax.nn.relu(jnp.einsum('bnm,bmh->bnh', A, m))
        gx = jnp.einsum('bnh,oh->bno', msg, W_ih) + b_ih
        gh = jnp.einsum('bnh,oh->bno', h, W_hh) + b_hh
        gx_r, gx_z, gx_n = jnp.split(gx, 3, axis=-1)
        gh_r, gh_z, gh_n = jnp.split(gh, 3, axis=-1)
        r = jax.nn.sigmoid(gx_r + gh_r)
        z = jax.nn.sigmoid(gx_z + gh_z)
        n = jnp.tanh(gx_n + r * gh_n)
        return (1.0 - z) * n + z * h

    def _L3_gnn_ref(x, adj, W, b):
        import jax, jax.numpy as jnp
        import numpy as np
        B, N, D, OUT = (4, 256, 128, 128)
        d = x.shape[-1]
        W1, W2 = (W[:d], W[d:])
        p = jnp.einsum('bnd,do->bno', x, W1 - W2)
        q = jnp.einsum('bnd,do->bno', x, W2)
        pre = p[:, :, None, :] + q[:, None, :, :] + b
        h = jax.nn.relu(pre) * adj[..., None]
        return jnp.max(h, axis=2)
    h = jnp.maximum(_layernorm(x, axis=-1), 0.0)
    x = x + _L0_gnn_ref(h, adj, L0_gnn_W, L0_gnn_b)
    h = jnp.maximum(_layernorm(x, axis=-1), 0.0)
    x = x + _L1_gnn_ref(h, adj, adj, L1_gnn_W1, L1_gnn_b1, L1_gnn_W2, L1_gnn_b2, L1_gnn_Wa, L1_gnn_Wd1, L1_gnn_bd1, L1_gnn_Wd2, L1_gnn_bd2)
    h = jnp.maximum(_layernorm(x, axis=-1), 0.0)
    x = x + _L2_gnn_ref(h, adj, L2_gnn_W1, L2_gnn_b1, L2_gnn_W2, L2_gnn_b2, L2_gnn_W_ih, L2_gnn_W_hh, L2_gnn_b_ih, L2_gnn_b_hh)
    h = jnp.maximum(_layernorm(x, axis=-1), 0.0)
    x = x + _L3_gnn_ref(h, adj, L3_gnn_W, L3_gnn_b)
    return x

_drawn_inputs = setup_inputs


def setup_inputs(seed=0):
    import zlib

    import numpy as np

    out = dict(_drawn_inputs(seed))
    spreads = {'L1_gnn_b1': (0.0, 0.8),
     'L1_gnn_b2': (0.0, 0.542),
     'L1_gnn_bd1': (0.0, 1.334),
     'L1_gnn_bd2': (0.0, 0.603),
     'L2_gnn_b1': (0.0, 0.69),
     'L2_gnn_b2': (0.0, 0.699),
     'L2_gnn_b_ih': (0.0, 1.492),
     'L2_gnn_b_hh': (0.0, 2.0)}
    factors = {'L0_gnn_b': 6.502,
     'L1_gnn_W1': 8.0,
     'L1_gnn_W2': 8.0,
     'L1_gnn_Wa': 3.624,
     'L1_gnn_Wd1': 3.511,
     'L3_gnn_b': 64.0,
     'L2_gnn_W_hh': 2.997}
    for name, (base, spread) in spreads.items():
        noise = np.random.default_rng([zlib.crc32(name.encode()), seed]).standard_normal(out[name].shape)
        drawn = base * np.exp(spread * noise) if base else spread * noise
        out[name] = jnp.asarray(drawn.astype(out[name].dtype))
    for name, factor in factors.items():
        out[name] = (out[name] * factor).astype(out[name].dtype)
    return out
```

```python
from contextlib import ExitStack

import numpy as np

import concourse.bass as bass
from concourse import mybir

F32 = mybir.dt.float32
BF16 = mybir.dt.bfloat16
I32 = mybir.dt.int32
ALU = mybir.AluOpType
ACT = mybir.ActivationFunctionType
AX = mybir.AxisListType

B, N, D = 64, 128, 128
NG = 64
GB = 4
G = B // GB
GC = GB * D
NS = 24
NR = -(-N // NS)
CH = 8
NC = NS // CH
CC = CH * N
HC = CC // 2
STEPS = B * NC
UNROLL = 2 * NC
NBK = NS // 4
NO_SLOT = 200.0
CUTOFF = 5.0
WIDTH = np.float32(CUTOFF) / np.float32(NG - 1)
COEFF = float(np.float32(-0.5) / (WIDTH * WIDTH))
LN2 = float(np.log(2.0))
SOFT_MAX = 20.0
LN_EPS = 1e-5
DEG_EPS = 1e-8
WA, W1, W2, WD1, WD2, M1, M2, IH, HH = 0, 1, 2, 3, 4, 5, 6, 7, 10
NW = 13


def due(value, base=0):
    return 0 if isinstance(value, int) and value <= 0 else value + base


def active(h, n):
    return not isinstance(h, int) or 0 <= h < n


def group_steps(eng, body, depth):
    head = 4
    for t in range(head):
        body(t, t % 2)
    with eng.Fori(0, (G - head) // 2) as i:
        for u in range(2):
            body(i * 2 + (head + u), u)
    for t in range(G, G + depth):
        body(t, t % 2)


def chunk_steps(eng, step, depth):
    for k in range(UNROLL):
        step(0, k, k)
    with eng.Fori(1, STEPS // UNROLL) as m:
        for k in range(UNROLL):
            step(m, k, m * UNROLL + k)
    for k in range(depth):
        step(STEPS // UNROLL, k, STEPS + k)


def graph_steps(eng, body, depth):
    for t in range(4):
        body(t, t % 2)
    with eng.Fori(0, (B - 4) // 2) as i:
        for u in range(2):
            body(i * 2 + (4 + u), u)
    for t in range(B, B + depth):
        body(t, t % 2)


def build(nc, io):
    ctx = ExitStack()
    with ctx:
        def sb(name, shape, dt=F32):
            return ctx.enter_context(nc.sbuf_tensor(name, shape, dt))

        def sem(name):
            return ctx.enter_context(nc.semaphore(name))

        X = sb("X", [128, B * D])
        AT = sb("AT", [128, B * N])
        YR = sb("YR", [128, 2, B * N])
        Y, R = YR[:, 0, :], YR[:, 1, :]
        RANK = sb("RANK", [128, B * N], BF16)
        IOTA = sb("IOTA", [128, NS * N], BF16)
        WT = sb("WT", [128, NW, 128])
        W0 = sb("W0", [128, 128])
        W3 = sb("W3", [128, 2, 128])
        ident = sb("ident", [128, 128])
        identb = sb("identb", [128, 128], BF16)
        after = sb("after", [128, 128], BF16)
        ones = sb("ones", [128, NG])
        ROWB = sb("ROWB", [128, 4, 128])
        COLB = sb("COLB", [128, 16])
        STAT = sb("STAT", [128, 3, B])
        STATB = sb("STATB", [128, 2, GB * 8 + 16])
        ONE = sb("ONE", [1, 128])
        MX = sb("MX", [128, 24])
        FLAG = sb("FLAG", [1, 8], I32)
        WORK = sb("WORK", [128, 14000])
        PS = ctx.enter_context(nc.psum_tensor("PS", [128, 8 * 512], F32))
        acD = nc.dram_tensor("ac_slots", (NR, B, NS, N), F32, kind="Internal").ap()

        b1c, b2c, bd1c, m1c = (COLB[:, k:k + 1] for k in range(4))
        brz = COLB[:, 4:6]
        bin_, bhn = COLB[:, 6:7], COLB[:, 9:10]
        offc = COLB[:, 10:11]
        bih, bhh = COLB[:, 4:7], COLB[:, 7:10]
        DEG, LNS, LNB = STAT[:, 0, :], STAT[:, 1, :], STAT[:, 2, :]

        def bank(k, n=1):
            return PS[:, k * 512:(k + n) * 512]

        class Carve:
            def __init__(self):
                self.at = 0

            def __call__(self, words, dt=F32):
                a = WORK[:, self.at:self.at + words]
                self.at += words
                assert self.at <= 14000, self.at
                return a if dt == F32 else a.bitcast(dt)

        def gsl(t, k=GC):
            return bass.ds(t * k, k)

        def by4(ap):
            return ap.rearrange("p (b n) -> p b n", b=GB)

        s_passed = sem("wait_passed")
        s_phase = sem("phase")
        s_gen = sem("general_round")
        s_w = sem("weights_loaded")
        s_x = sem("x_loaded")
        s_gp = sem("gpsimd_constants")
        s_prep = sem("prep_dve")
        s_wt = sem("weights_transposed")
        s_wtc = sem("weights_copied")
        s_rowb = sem("row_biases_summed")
        s_adj = [sem("adj_loaded0"), sem("adj_loaded1")]
        s_deg = sem("degrees_read")
        s_tp = sem("adj_transposed")
        s_at = sem("at_stored")
        s_mask = sem("mask_made")
        s_rank = sem("rank_counted")
        s_rks = sem("rank_stored")
        s_d0 = sem("degree_root")
        s_bn = sem("ln_stats")
        s_var = sem("ln_var")
        s_rs = sem("ln_scale")
        s_h = sem("h_ready")
        s_hu = sem("h_used")
        s_p2 = [sem(f"l0_{n}") for n in ("support", "support_copied", "out", "x", "xb")]
        s_p3 = [sem(f"l1in_{n}") for n in ("t", "tc", "rf", "rfc")]
        s_oh = sem("onehot_made")
        s_pa = sem("weighted_made")
        s_pa2 = sem("weighted2_made")
        s_rf = sem("rf_copied")
        s_z = sem("z_gathered")
        s_zc = sem("z_copied")
        s_sq = sem("square_made")
        s_g = sem("gauss_made")
        s_acd = sem("ac_saved")
        s_pre = sem("pre_made")
        s_min = sem("pre_capped")
        s_ex = sem("exp_made")
        s_ln = sem("log_made")
        s_sp = sem("softplus_made")
        s_gp2 = sem("gather_made")
        s_gc = sem("gather_copied")
        s_wf = sem("filter_made")
        s_hm = sem("message_made")
        s_red = sem("message_summed")
        s_ya = sem("general_added")
        s_io = sem("iota_moved")
        s_p5 = [sem(f"l1out_{n}") for n in ("t1", "cap", "exp", "log", "sp", "t2", "x", "xb")]
        s_p6 = [sem(f"l2m_{n}") for n in ("ht", "htc", "m1", "m1c", "m2", "m2c", "msg", "msgc")]
        s_p8 = [sem(f"l2g_{n}") for n in ("rz", "n", "sig", "rh", "pre", "tanh", "dif", "zd", "new", "t", "x")]
        s_p9 = [sem(f"l3in_{n}") for n in ("t", "tc", "pq", "p", "q")]
        s_l3 = {n: sem(f"l3_{n}") for n in ("ac0", "ac1", "act", "ac", "oh", "c1", "r1", "c2", "c3",
                                            "z", "acc", "fold", "x")}
        s_gl = {n: sem(f"l3g_{n}") for n in ("ac", "act", "acs", "sh", "oh", "c1", "r1", "c2", "c3", "z",
                                             "acc", "fold", "x")}
        s_out = sem("out_stored")
        s_flag = sem("flag_made")

        def leave_round(eng, r):
            eng.drain().then_inc(s_gen, 1)
            eng.wait_ge(s_gen, due(r * 5))
            eng.sem_inc(s_passed, 1)

        c = Carve()
        NATW = c(NW * 128).rearrange("p (w n) -> p w n", w=NW)
        W3N = c(256).rearrange("p (w n) -> p w n", w=2)
        ROWN = c(512)
        MLN2 = c(128)
        ADJ = [c(GC), c(GC)]
        MASK = [c(GC // 2, BF16), c(GC // 2, BF16)]
        SUMW2 = c(1)
        PINF = c(64)

        c = Carve()
        HB = [c(GC), c(GC)]
        TB = [c(GC), c(GC)]
        XB = [c(GC), c(GC)]
        UB = [c(GC), c(GC)]
        VB = [c(GC), c(GC)]
        RZ = [c(2 * GC), c(2 * GC)]
        NB_ = [c(GC), c(GC)]

        c = Carve()
        OH = [c(CC // 2, BF16), c(CC // 2, BF16)]
        PA = [c(CC), c(CC)]
        PA2 = [c(CC), c(CC)]
        ZC = c(HC)
        GA = [c(HC), c(HC)]
        SP = [c(CC), c(CC)]
        GS = [c(CC), c(CC)]
        HS = c((CH + 2) * N).rearrange("p (s i) -> p s i", i=N)
        RF = [c(128), c(128)]

        c = Carve()
        OH3 = [c(NS * N // 2, BF16).rearrange("p (s i) -> p s i", i=N) for _ in range(2)]
        PARTS = [c(3 * D, BF16).rearrange("p (k w n) -> p k w n", k=3, w=2) for _ in range(2)]
        REM = [c(2 * D).rearrange("p (w n) -> p w n", w=2) for _ in range(2)]
        ACT_ = [c(N), c(N)]
        AC = [c(NS), c(NS)]
        ACC = [c(GC).rearrange("p (s o) -> p s o", o=D) for _ in range(2)]
        SHR = c(N // 2, BF16)
        SHV = c(1)

        def general_rounds(eng, one_round, last_dma=False):
            many = eng.value_load(FLAG[0:1, 0:1], min_val=0, max_val=1)
            with eng.If(many > 0):
                with eng.Fori(1, NR) as r:
                    one_round(r)
                    if last_dma:
                        eng.wait_ge(s_acd, due((r + 1) * (16 * STEPS)))
                        eng.sem_inc(s_passed, 1)
                    leave_round(eng, r)

        block = ctx.enter_context(nc.Block())

        @block.sync
        def _(sp):
            natural = [io["L1_gnn_Wa"], None, io["L1_gnn_W2"], io["L1_gnn_Wd1"], io["L1_gnn_Wd2"],
                       io["L2_gnn_W1"], io["L2_gnn_W2"]]
            for k, w in enumerate(natural):
                if w is not None:
                    sp.dma_start(NATW[:, k, :], w).then_inc(s_w, 16)
            for h in range(2):
                sp.dma_start(NATW[:, W1, h * NG:(h + 1) * NG], io["L1_gnn_W1"]).then_inc(s_w, 16)
            for k in range(3):
                sp.dma_start(NATW[:, IH + k, :], io["L2_gnn_W_ih"][k * 128:(k + 1) * 128, :]).then_inc(s_w, 16)
                sp.dma_start(NATW[:, HH + k, :], io["L2_gnn_W_hh"][k * 128:(k + 1) * 128, :]).then_inc(s_w, 16)
            sp.dma_start(W0[:, :], io["L0_gnn_W"]).then_inc(s_w, 16)
            for k in range(2):
                sp.dma_start(W3N[:, k, :], io["L3_gnn_W"][k * 128:(k + 1) * 128, :]).then_inc(s_w, 16)
            for k, n in enumerate(("L0_gnn_b", "L1_gnn_bd2", "L3_gnn_b", "L2_gnn_b2")):
                sp.dma_start(ROWN[0:1, k * 128:(k + 1) * 128],
                             io[n].rearrange("(a n) -> a n", a=1)).then_inc(s_w, 16)
            for k, n in enumerate(("L1_gnn_b1", "L1_gnn_b2", "L1_gnn_bd1", "L2_gnn_b1")):
                sp.dma_start(COLB[:, k:k + 1], io[n].rearrange("(p a) -> p a", a=1)).then_inc(s_w, 16)
            for k in range(3):
                for n, at in (("L2_gnn_b_ih", 4), ("L2_gnn_b_hh", 7)):
                    sp.dma_start(COLB[:, at + k:at + k + 1],
                                 io[n][k * 128:(k + 1) * 128].rearrange("(p a) -> p a", a=1)).then_inc(s_w, 16)

            def load_adj(t, u):
                if not active(t, G):
                    return
                sp.wait_ge(s_deg, due(t - 1))
                sp.wait_ge(s_tp, due(t - 1))
                sp.dma_start(by4(ADJ[u]), io["adj"][bass.ds(t * GB, GB), :, :]
                             .rearrange("b i j -> i b j")).then_inc(s_adj[u], 16)
            group_steps(sp, load_adj, 0)
            sp.drain().then_inc(s_phase, 1)
            sp.wait_ge(s_phase, 5)
            sp.drain().then_inc(s_phase, 1)
            sp.wait_ge(s_phase, 10)
            sp.drain().then_inc(s_phase, 1)
            sp.wait_ge(s_phase, 15)

            def save_ac(r, base):
                def step(m, k, t):
                    h = t - 1
                    if not active(h, STEPS):
                        return
                    b, ch = m * 2 + (k - 1) // NC, (k - 1) % NC
                    sp.wait_ge(s_zc, due(h + 1, base))
                    dst = acD[r] if isinstance(r, int) else acD[bass.ds(r, 1)].rearrange("a b s i -> (a b) s i")
                    dst = dst[bass.ds(b, 1) if not isinstance(b, int) else slice(b, b + 1),
                              ch * CH:(ch + 1) * CH, :]
                    sp.dma_start(dst.rearrange("a (h s) i -> (a h) (s i)", h=2),
                                 ZC[0:NG + 1:NG, :]).then_inc(s_acd, 16)
                return step
            chunk_steps(sp, save_ac(0, 0), 1)
            sp.wait_ge(s_acd, 16 * STEPS)
            sp.drain().then_inc(s_phase, 1)
            sp.wait_ge(s_phase, 20)
            general_rounds(sp, lambda r: chunk_steps(sp, save_ac(r, r * STEPS), 1), last_dma=True)
            sp.drain().then_inc(s_phase, 1)
            sp.wait_ge(s_phase, 25)
            sp.drain().then_inc(s_phase, 1)
            sp.wait_ge(s_phase, 30)
            sp.drain().then_inc(s_phase, 1)
            sp.wait_ge(s_phase, 35)
            sp.drain().then_inc(s_phase, 1)
            sp.wait_ge(s_phase, 40)
            sp.drain().then_inc(s_phase, 1)
            sp.wait_ge(s_phase, 45)

            many = sp.value_load(FLAG[0:1, 0:1], min_val=0, max_val=1)
            with sp.If(many > 0):
                with sp.Fori(0, B) as b:
                    with sp.Fori(0, NR) as r:
                        sp.wait_ge(s_gl["act"], due(b * NR + r + 1))
                        sp.dma_start(ACT_[0][0:NS, :], acD.rearrange("r b s i -> (r b) s i")[bass.ds(r * B + b, 1)]
                                     .rearrange("a s i -> (a s) i")).then_inc(s_gl["ac"], 16)
            with sp.Else():
                def load_ac(t, u):
                    if active(t, B):
                        sp.wait_ge(s_l3["act"], due(t - 1))
                        src = acD[0][bass.ds(t, 1)] if not isinstance(t, int) else acD[0][t:t + 1]
                        sp.dma_start(ACT_[u][0:NS, :], src.rearrange("a s i -> (a s) i"))\
                          .then_inc(s_l3[f"ac{u}"], 16)
                graph_steps(sp, load_ac, 0)
            sp.drain().then_inc(s_phase, 1)
            sp.wait_ge(s_phase, 50)
            for k in range(G):
                sp.dma_start(io["out"][k * GB:(k + 1) * GB].rearrange("b n d -> n b d"),
                             by4(X[:, k * GC:(k + 1) * GC])).then_inc(s_out, 16)
            sp.wait_ge(s_out, 16 * G)

        @block.gpsimd
        def _(pool):
            nc.gpsimd.memset(ident[:, :], 0.0).then_inc(s_gp, 1)
            nc.gpsimd.memset(identb[:, :], 0.0).then_inc(s_gp, 1)
            nc.gpsimd.memset(after[:, :], 0.0).then_inc(s_gp, 1)
            nc.gpsimd.memset(ones[:, :], 1.0).then_inc(s_gp, 1)
            nc.gpsimd.memset(MLN2[:, :], -LN2).then_inc(s_gp, 1)
            nc.gpsimd.memset(PINF[:, :], -0.5).then_inc(s_gp, 1)
            nc.gpsimd.memset(MX[:, :], 0.0).then_inc(s_gp, 1)
            nc.gpsimd.memset(COLB[:, 11:16], -0.5).then_inc(s_gp, 1)
            nc.gpsimd.memset(ONE[:, :], 1.0).then_inc(s_gp, 1)
            pool.wait_ge(s_gp, 9)
            nc.gpsimd.affine_select(out=ident[:, :], in_=ident[:, :], compare_op=ALU.not_equal, fill=1.0,
                                    base=0, pattern=[[-1, 128]], channel_multiplier=1).then_inc(s_gp, 1)
            nc.gpsimd.affine_select(out=identb[:, :], in_=identb[:, :], compare_op=ALU.not_equal, fill=1.0,
                                    base=0, pattern=[[-1, 128]], channel_multiplier=1).then_inc(s_gp, 1)
            nc.gpsimd.affine_select(out=after[:, :], in_=after[:, :], compare_op=ALU.is_ge, fill=1.0,
                                    base=0, pattern=[[1, 128]], channel_multiplier=-1).then_inc(s_gp, 1)
            nc.gpsimd.iota(IOTA[:, :].rearrange("p (s i) -> p s i", i=N), pattern=[[1, NS], [0, N]], base=0,
                           channel_multiplier=0, allow_small_or_imprecise_dtypes=True).then_inc(s_gp, 1)
            for h in range(2):
                pool.wait_ge(s_gp, 13 + h)
                nc.gpsimd.iota(offc[h * NG:(h + 1) * NG, :], pattern=[[0, 1]], base=0, channel_multiplier=1,
                               allow_small_or_imprecise_dtypes=True).then_inc(s_gp, 1)
            pool.wait_ge(s_gp, 15)
            pool.wait_ge(s_d0, 1)
            nc.gpsimd.tensor_tensor(DEG, DEG, PINF, ALU.pow).then_inc(s_d0, 1)
            pool.drain().then_inc(s_phase, 1)
            pool.wait_ge(s_phase, 5)

            def ln_root(layer, add_bias=None):
                base = layer * G

                def step(t, u):
                    if active(t, G):
                        pool.wait_ge(s_var, due(t + 1, base))
                        v = LNS[:, bass.ds(t * GB, GB)]
                        nc.gpsimd.tensor_tensor(v, v, COLB[:, 11:15], ALU.pow).then_inc(s_rs, 1)
                    if add_bias is not None:
                        add_bias(t, u)
                return step

            def xb0(t, u):
                if active(t, G):
                    pool.wait_ge(s_p2[3], due(t - 1))
                    nc.gpsimd.tensor_tensor(by4(XB[u]), by4(X[:, gsl(t)]),
                                            ROWB[:, 0:1, :].to_broadcast([128, GB, 128]), ALU.add)\
                      .then_inc(s_p2[4], 1)
            group_steps(pool, ln_root(0, xb0), 0)
            pool.drain().then_inc(s_phase, 1)
            pool.wait_ge(s_phase, 10)
            group_steps(pool, ln_root(1), 0)
            pool.drain().then_inc(s_phase, 1)
            pool.wait_ge(s_phase, 15)

            def weigh(base, rbase):
                def step(m, k, t):
                    if not active(t, STEPS):
                        return
                    b, ch, u = m * 2 + k // NC, k % NC, k % 2
                    if ch == 0:
                        pool.wait_ge(s_gp2, due(t - NC, base))
                        nc.gpsimd.tensor_copy(RF[(k // NC) % 2], R[:, gsl(b, 128)]).then_inc(s_rf, 1)
                    at = AT[:, gsl(b, N)].rearrange("p (a i) -> p a i", a=1).to_broadcast([128, CH, N])
                    pa = PA[u].rearrange("p (s i) -> p s i", i=N)
                    pool.wait_ge(s_oh, due(t + 1, base))
                    pool.wait_ge(s_z, due(t - 1, base))
                    pool.sem_inc(s_passed, 1)
                    nc.gpsimd.tensor_tensor(pa, OH[u].rearrange("p (s i) -> p s i", i=N), at, ALU.mult)\
                      .then_inc(s_pa, 1)
                    pool.wait_ge(s_pa, due(t + 1, base))
                    pool.wait_ge(s_gp2, due(t - 1, base))
                    nc.gpsimd.tensor_tensor(PA2[u], PA[u], PA[u], ALU.mult).then_inc(s_pa2, 1)
                return step
            chunk_steps(pool, weigh(0, 0), 0)
            pool.drain().then_inc(s_phase, 1)
            pool.wait_ge(s_phase, 20)
            general_rounds(pool, lambda r: chunk_steps(pool, weigh(r * STEPS, r * B), 0))
            pool.drain().then_inc(s_phase, 1)
            pool.wait_ge(s_phase, 25)

            def xb1(t, u):
                if active(t, G):
                    pool.wait_ge(s_p5[6], due(t - 1))
                    nc.gpsimd.tensor_tensor(by4(XB[u]), by4(X[:, gsl(t)]),
                                            ROWB[:, 1:2, :].to_broadcast([128, GB, 128]), ALU.add)\
                      .then_inc(s_p5[7], 1)
            group_steps(pool, xb1, 0)
            pool.drain().then_inc(s_phase, 1)
            pool.wait_ge(s_phase, 30)
            group_steps(pool, ln_root(2), 0)
            pool.drain().then_inc(s_phase, 1)
            pool.wait_ge(s_phase, 35)

            def blend(t, u):
                h = t - 1
                if active(h, G):
                    v = 1 - u
                    ht = R[:, gsl(h)]
                    pool.wait_ge(s_p8[5], due(h + 1))
                    pool.wait_ge(s_p8[9], due(h - 1))
                    nc.gpsimd.tensor_tensor(UB[v], ht, NB_[v], ALU.subtract).then_inc(s_p8[6], 1)
                    pool.wait_ge(s_p8[6], due(h + 1))
                    nc.gpsimd.tensor_tensor(UB[v], UB[v], RZ[v][:, GC:2 * GC], ALU.mult).then_inc(s_p8[7], 1)
                    pool.wait_ge(s_p8[7], due(h + 1))
                    nc.gpsimd.tensor_tensor(UB[v], UB[v], NB_[v], ALU.add).then_inc(s_p8[8], 1)
            group_steps(pool, blend, 1)
            pool.drain().then_inc(s_phase, 1)
            pool.wait_ge(s_phase, 40)
            group_steps(pool, ln_root(3), 0)
            pool.drain().then_inc(s_phase, 1)
            pool.wait_ge(s_phase, 45)

            pool.drain().then_inc(s_phase, 1)
            pool.wait_ge(s_phase, 50)

        @block.vector
        def _(dve):
            dve.wait_ge(s_gp, 15)
            nc.vector.tensor_scalar(offc, offc, -float(WIDTH), None, ALU.mult).then_inc(s_prep, 1)
            dve.wait_ge(s_w, 16 * 31)
            nc.vector.tensor_tensor(COLB[:, 4:6], COLB[:, 4:6], COLB[:, 7:9], ALU.add).then_inc(s_prep, 1)
            nc.vector.reduce_sum(SUMW2, NATW[:, W2, :], AX.X).then_inc(s_prep, 1)
            nc.vector.tensor_tensor(W3[:, 0, :], W3N[:, 0, :], W3N[:, 1, :], ALU.subtract).then_inc(s_prep, 1)
            nc.vector.tensor_copy(W3[:, 1, :], W3N[:, 1, :]).then_inc(s_prep, 1)
            dve.wait_ge(s_prep, 5)
            nc.vector.scalar_tensor_tensor(b2c, SUMW2, -LN2, b2c, ALU.mult, ALU.add).then_inc(s_prep, 1)

            def ranks(t, u):
                if active(t, G):
                    dve.wait_ge(s_adj[u], (t - u) * 8 + 16)
                    nc.vector.reduce_sum(DEG[:, bass.ds(t * GB, GB)], by4(ADJ[u]), AX.X).then_inc(s_deg, 1)
                    dve.wait_ge(s_at, due(t + 1))
                    dve.wait_ge(s_rank, due(t - 1))
                    nc.vector.tensor_scalar(MASK[u], AT[:, gsl(t)], 0.0, None, ALU.not_equal).then_inc(s_mask, 1)
                    nc.vector.tensor_scalar(RANK[:, gsl(t)], AT[:, gsl(t)], 0.0, NO_SLOT,
                                            ALU.is_equal, ALU.mult).then_inc(s_mask, 1)
                h = t - 1
                if active(h, G):
                    dve.wait_ge(s_rank, due(h + 1))
                    dve.wait_ge(s_mask, due(h * 2 + 2))
                    nc.vector.tensor_tensor(RANK[:, gsl(h)], RANK[:, gsl(h)], bank(2 + (1 - u)), ALU.add)\
                      .then_inc(s_rks, 1)
                    nc.vector.reduce_max(MX[0:1, bass.ds(h, 1)], PS[0:1, (3 - u) * 512:(4 - u) * 512], AX.X)\
                      .then_inc(s_rks, 1)
            group_steps(dve, ranks, 1)
            dve.wait_ge(s_deg, G)
            nc.vector.tensor_scalar(DEG, DEG, DEG_EPS, None, ALU.add).then_inc(s_d0, 1)
            dve.wait_ge(s_rks, 2 * G)
            nc.vector.reduce_max(MX[0:1, G:G + 1], MX[0:1, 0:G], AX.X).then_inc(s_flag, 1)
            dve.wait_ge(s_flag, 1)
            nc.vector.tensor_scalar(FLAG[0:1, 0:1], MX[0:1, G:G + 1], float(NS) - 0.5, None, ALU.is_gt)\
              .then_inc(s_flag, 1)
            dve.drain().then_inc(s_phase, 1)
            dve.wait_ge(s_phase, 5)

            def ln_stats(layer, t, u):
                base = layer * G
                st = STATB[:, u, 0:GB * 6].rearrange("p (b k) -> p b k", k=6)
                mv = STATB[:, u, GB * 6:GB * 8].rearrange("p (b k) -> p b k", k=2)
                for q in range(GB):
                    nc.vector.bn_stats(st[:, q, :], X[:, bass.ds(t * GC + q * D, D)]).then_inc(s_bn, 1)
                dve.wait_ge(s_bn, due(t * (2 * GB + 1) + GB, layer * G * (2 * GB + 1)))
                dve.sem_inc(s_passed, 1)
                for q in range(GB):
                    nc.vector.bn_aggr(mv[:, q, :], st[:, q, :]).then_inc(s_bn, 1)
                dve.wait_ge(s_bn, due(t * (2 * GB + 1) + 2 * GB, layer * G * (2 * GB + 1)))
                v = LNS[:, bass.ds(t * GB, GB)]
                nc.vector.tensor_scalar(v, mv[:, :, 1], LN_EPS, None, ALU.add).then_inc(s_var, 1)
                nc.vector.tensor_scalar(LNB[:, bass.ds(t * GB, GB)], mv[:, :, 0], -1.0, None, ALU.mult)\
                  .then_inc(s_bn, 1)

            def ln_shift(layer, t):
                dve.wait_ge(s_rs, due(t + 1, layer * G))
                dve.wait_ge(s_bn, due((t + 1) * (2 * GB + 1), layer * G * (2 * GB + 1)))
                v, s = LNS[:, bass.ds(t * GB, GB)], LNB[:, bass.ds(t * GB, GB)]
                if layer == 0:
                    nc.vector.tensor_tensor(v, v, DEG[:, bass.ds(t * GB, GB)], ALU.mult).then_inc(s_prep, 1)
                    dve.wait_ge(s_prep, due(t + 7))
                nc.vector.tensor_tensor(s, s, v, ALU.mult).then_inc(s_hu, 1)

            dve.wait_ge(s_x, 16 * G)

            def layer0(t, u):
                if active(t, G):
                    ln_stats(0, t, u)
                    ln_shift(0, t)
                h = t - 1
                if active(h, G):
                    dve.wait_ge(s_p2[2], due(h + 1))
                    dve.wait_ge(s_p2[4], due(h + 1))
                    for q in range(GB):
                        last = nc.vector.scalar_tensor_tensor(
                            X[:, bass.ds(h * GC + q * D, D)], bank(2 + (1 - u))[:, q * D:(q + 1) * D],
                            DEG[:, bass.ds(h * GB + q, 1)], XB[1 - u][:, q * D:(q + 1) * D],
                            ALU.mult, ALU.add)
                    last.then_inc(s_p2[3], 1)
            group_steps(dve, layer0, 1)
            dve.drain().then_inc(s_phase, 1)
            dve.wait_ge(s_phase, 10)

            def norm1(t, u):
                if active(t, G):
                    ln_stats(1, t, u)
                    ln_shift(1, t)
            group_steps(dve, norm1, 0)
            dve.drain().then_inc(s_phase, 1)
            dve.wait_ge(s_phase, 15)

            def edges1(base, general):
                def step(m, k, t):
                    u = k % 2
                    b, ch = m * 2 + k // NC, k % NC
                    if active(t, STEPS):
                        dve.wait_ge(s_pa, due(t - 1, base))
                        nc.vector.tensor_tensor(
                            OH[u].rearrange("p (s i) -> p s i", i=N),
                            RANK[:, gsl(b, N)].rearrange("p (a i) -> p a i", a=1).to_broadcast([128, CH, N]),
                            IOTA[:, ch * CC:(ch + 1) * CC].rearrange("p (s i) -> p s i", i=N),
                            ALU.is_equal).then_inc(s_oh, 1)
                    h = t - 2
                    if active(h, STEPS):
                        dve.wait_ge(s_pre, due(h + 1, base))
                        dve.wait_ge(s_wf, due(h - 1, base))
                        nc.vector.tensor_scalar(SP[u], bank(2, 2), b1c, SOFT_MAX, ALU.add, ALU.min)\
                          .then_inc(s_min, 1)
                    e = t - 4
                    if active(e, STEPS):
                        ech = (k - 4) % NC
                        eb = m * 2 + (k - 4) // NC
                        eu = k % 2
                        dve.wait_ge(s_wf, due(e + 1, base))
                        dve.wait_ge(s_gc, due(e + 1, base))
                        dve.wait_ge(s_red, due(e, base))
                        nc.vector.scalar_tensor_tensor(
                            HS[:, 1:CH + 1, :], bank(4, 2).rearrange("p (s i) -> p s i", i=N), b2c,
                            GS[eu].rearrange("p (s i) -> p s i", i=N), ALU.add, ALU.mult).then_inc(s_hm, 1)
                        dve.wait_ge(s_hm, due(e + 1, base))
                        if ech == 0:
                            src = HS[:, 1:CH + 1, :]
                        elif ech % 2 == 1:
                            src = HS[:, 0:CH + 1, :]
                        else:
                            src = HS[:, 1:CH + 2, :]
                        if ech == NC - 1 and not general:
                            dst = Y[:, gsl(eb, N)]
                        else:
                            dst = HS[:, 0 if ech % 2 == 0 else CH + 1, :]
                        nc.vector.reduce_sum(dst, src.rearrange("p s i -> p i s"), AX.X).then_inc(s_red, 1)
                        if ech == NC - 1 and general:
                            dve.wait_ge(s_red, due(e + 1, base))
                            nc.vector.tensor_tensor(Y[:, gsl(eb, N)], Y[:, gsl(eb, N)], dst, ALU.add)\
                              .then_inc(s_ya, 1)
                    if active(h, STEPS):
                        dve.wait_ge(s_ln, due(h + 1, base))
                        nc.vector.scalar_tensor_tensor(SP[u], bank(2, 2), b1c, SP[u], ALU.add, ALU.max)\
                          .then_inc(s_sp, 1)
                return step
            chunk_steps(dve, edges1(0, False), 4)
            dve.drain().then_inc(s_phase, 1)
            dve.wait_ge(s_phase, 20)
            many = dve.value_load(FLAG[0:1, 0:1], min_val=0, max_val=1)
            with dve.If(many > 0):
                with dve.Fori(1, NR) as r:
                    nc.vector.tensor_scalar(IOTA[:, :], IOTA[:, :], float(NS), None, ALU.add).then_inc(s_io, 1)
                    dve.wait_ge(s_io, r)
                    chunk_steps(dve, edges1(r * STEPS, True), 4)
                    leave_round(dve, r)
            dve.drain().then_inc(s_phase, 1)
            dve.wait_ge(s_phase, 25)

            def nodes1(t, u):
                if active(t, G):
                    dve.wait_ge(s_p5[0], due(t + 1))
                    dve.wait_ge(s_p5[5], due(t - 1))
                    nc.vector.tensor_scalar(TB[u], bank(u), bd1c, SOFT_MAX, ALU.add, ALU.min).then_inc(s_p5[1], 1)
                h = t - 1
                if active(h, G):
                    v = 1 - u
                    dve.wait_ge(s_p5[3], due(h + 1))
                    nc.vector.scalar_tensor_tensor(TB[v], bank(v), bd1c, TB[v], ALU.add, ALU.max)\
                      .then_inc(s_p5[4], 1)
                e = t - 2
                if active(e, G):
                    dve.wait_ge(s_p5[5], due(e + 1))
                    dve.wait_ge(s_p5[7], due(e + 1))
                    nc.vector.tensor_tensor(X[:, gsl(e)], bank(2 + u), XB[u], ALU.add).then_inc(s_p5[6], 1)
            group_steps(dve, nodes1, 2)
            dve.drain().then_inc(s_phase, 1)
            dve.wait_ge(s_phase, 30)

            def norm2(t, u):
                if active(t, G):
                    ln_stats(2, t, u)
                    ln_shift(2, t)
            group_steps(dve, norm2, 0)
            dve.drain().then_inc(s_phase, 1)
            dve.wait_ge(s_phase, 35)

            def gates(t, u):
                h = t - 1
                if active(t, G):
                    dve.wait_ge(s_p8[2], due(t + 1))
                    dve.wait_ge(s_p8[1], due(t + 1))
                    dve.wait_ge(s_p8[5], due(t - 1))
                    nc.vector.scalar_tensor_tensor(VB[u], bank(3), bhn, RZ[u][:, 0:GC], ALU.add, ALU.mult)\
                      .then_inc(s_p8[3], 1)
                    dve.wait_ge(s_p8[3], due(t + 1))
                    nc.vector.tensor_tensor(VB[u], VB[u], bank(2), ALU.add).then_inc(s_p8[4], 1)
                if active(h, G):
                    dve.wait_ge(s_p8[9], due(h + 1))
                    nc.vector.tensor_tensor(X[:, gsl(h)], bank(4 + (1 - u)), X[:, gsl(h)], ALU.add)\
                      .then_inc(s_p8[10], 1)
            group_steps(dve, gates, 1)
            dve.drain().then_inc(s_phase, 1)
            dve.wait_ge(s_phase, 40)

            def norm3(t, u):
                if active(t, G):
                    ln_stats(3, t, u)
                    ln_shift(3, t)
                h = t - 1
                if active(h, G):
                    dve.wait_ge(s_p9[2], due(h + 1))
                    pq = bank(4 if u else 6, 2).rearrange("p (b w n) -> p b w n", b=GB, w=2)
                    nc.vector.tensor_tensor(by4(Y[:, gsl(h)]), pq[:, :, 0, :],
                                            ROWB[:, 2:3, :].to_broadcast([128, GB, 128]), ALU.add)\
                      .then_inc(s_p9[3], 1)
                    nc.vector.tensor_copy(by4(R[:, gsl(h)]), pq[:, :, 1, :]).then_inc(s_p9[4], 1)
            group_steps(dve, norm3, 1)
            dve.drain().then_inc(s_phase, 1)
            dve.wait_ge(s_phase, 45)

            many = dve.value_load(FLAG[0:1, 0:1], min_val=0, max_val=1)
            with dve.If(many > 0):
                for n in ("act", "acs", "z", "acc"):
                    dve.sem_inc(s_gl[n], 1)
                nc.vector.memset(SHV[:, :], -float(NS) * (NR - 1)).then_inc(s_gl["sh"], 1)
                nc.vector.tensor_scalar(IOTA[:, :], IOTA[:, :], -float(NS) * (NR - 1), None, ALU.add)\
                  .then_inc(s_gl["sh"], 1)
                with dve.Fori(0, B) as b:
                    dve.wait_ge(s_gl["sh"], due(b * (2 * NR + 1) + 2))
                    nc.vector.tensor_scalar(SHV[:, :], SHV[:, :], float(NS) * NR, None, ALU.add)\
                      .then_inc(s_gl["sh"], 1)
                    y2 = YR[:, :, gsl(b, 128)]
                    dve.wait_ge(s_gl["z"], due(b * (NR * NBK) + 1))
                    nc.vector.tensor_copy(PARTS[0][:, 0], y2).then_inc(s_gl["c1"], 1)
                    dve.wait_ge(s_gl["c1"], due(b + 1))
                    nc.vector.tensor_tensor(REM[0], y2, PARTS[0][:, 0], ALU.subtract).then_inc(s_gl["r1"], 1)
                    dve.wait_ge(s_gl["r1"], due(b + 1))
                    nc.vector.tensor_copy(PARTS[0][:, 1], REM[0]).then_inc(s_gl["c2"], 1)
                    dve.wait_ge(s_gl["c2"], due(b + 1))
                    nc.vector.tensor_tensor(PARTS[0][:, 2], REM[0], PARTS[0][:, 1], ALU.subtract)\
                      .then_inc(s_gl["c3"], 1)
                    nc.vector.memset(ACC[0], 0.0).then_inc(s_gl["fold"], 1)
                    with dve.Fori(0, NR) as r:
                        n = b * NR + r
                        dve.wait_ge(s_gl["sh"], due(b * (2 * NR + 1) + r * 2 + 3))
                        nc.vector.tensor_scalar(SHV[:, :], SHV[:, :], -float(NS), None, ALU.add)\
                          .then_inc(s_gl["sh"], 1)
                        dve.wait_ge(s_gl["sh"], due(b * (2 * NR + 1) + r * 2 + 4))
                        nc.vector.tensor_scalar(SHR[:, :], RANK[:, gsl(b, N)], SHV[:, 0:1], None, ALU.add)\
                          .then_inc(s_gl["sh"], 1)
                        dve.wait_ge(s_gl["sh"], due(b * (2 * NR + 1) + r * 2 + 5))
                        dve.wait_ge(s_gl["z"], due(n * NBK + 1))
                        nc.vector.tensor_tensor(
                            OH3[0], SHR[:, :].rearrange("p (a i) -> p a i", a=1).to_broadcast([128, NS, N]),
                            IOTA[:, :].rearrange("p (s i) -> p s i", i=N), ALU.is_equal)\
                          .then_inc(s_gl["oh"], 1)
                        dve.wait_ge(s_gl["act"], due(n + 2))
                        dve.wait_ge(s_gl["acc"], due(n * NBK + 1))
                        nc.vector.tensor_scalar(AC[0], bank(6)[:, 0:NS], 0.0, None, ALU.max)\
                          .then_inc(s_gl["acs"], 1)
                        dve.wait_ge(s_gl["acs"], due(n + 2))
                        dve.wait_ge(s_gl["fold"], due(b * 3 + 1))
                        for kb in range(NBK):
                            dve.wait_ge(s_gl["z"], due(n * NBK + kb + 2))
                            dve.wait_ge(s_gl["acc"], due(n * NBK + kb + 1))
                            for q in range(4):
                                s = kb * 4 + q
                                last = nc.vector.scalar_tensor_tensor(
                                    ACC[0][:, q, :], bank(kb % 2)[:, q * D:(q + 1) * D], AC[0][:, s:s + 1],
                                    ACC[0][:, q, :], ALU.mult, ALU.max)
                            last.then_inc(s_gl["acc"], 1)
                    dve.wait_ge(s_gl["acc"], due((b + 1) * (NR * NBK) + 1))
                    nc.vector.tensor_tensor(ACC[0][:, 0:2, :], ACC[0][:, 0:2, :], ACC[0][:, 2:4, :], ALU.max)\
                      .then_inc(s_gl["fold"], 1)
                    dve.wait_ge(s_gl["fold"], due(b * 3 + 2))
                    nc.vector.tensor_tensor(ACC[0][:, 0, :], ACC[0][:, 0, :], ACC[0][:, 1, :], ALU.max)\
                      .then_inc(s_gl["fold"], 1)
                    dve.wait_ge(s_gl["fold"], due(b * 3 + 3))
                    nc.vector.tensor_tensor(X[:, gsl(b, D)], X[:, gsl(b, D)], ACC[0][:, 0, :], ALU.add)\
                      .then_inc(s_gl["x"], 1)
            with dve.Else():
                def edges3(t, u):
                    if active(t, B):
                        dve.wait_ge(s_l3["z"], due((t - 1) * NBK))
                        nc.vector.tensor_tensor(
                            OH3[u], RANK[:, gsl(t, N)].rearrange("p (a i) -> p a i", a=1)
                            .to_broadcast([128, NS, N]), IOTA[:, :].rearrange("p (s i) -> p s i", i=N),
                            ALU.is_equal).then_inc(s_l3["oh"], 1)
                        y2 = YR[:, :, gsl(t, 128)]
                        dve.wait_ge(s_l3["c1"], due(t + 1))
                        dve.wait_ge(s_l3["c2"], due(t - 1))
                        nc.vector.tensor_tensor(REM[u], y2, PARTS[u][:, 0], ALU.subtract).then_inc(s_l3["r1"], 1)
                        dve.wait_ge(s_l3["act"], due(t + 1))
                        nc.vector.tensor_scalar(AC[u], bank(6 + u)[:, 0:NS], 0.0, None, ALU.max)\
                          .then_inc(s_l3["ac"], 1)
                        dve.wait_ge(s_l3["c2"], due(t + 1))
                        nc.vector.tensor_tensor(PARTS[u][:, 2], REM[u], PARTS[u][:, 1], ALU.subtract)\
                          .then_inc(s_l3["c3"], 1)
                    h = t - 1
                    if active(h, B):
                        v = 1 - u
                        a = ACC[v]
                        dve.wait_ge(s_l3["ac"], due(h + 1))
                        for kb in range(NBK):
                            dve.wait_ge(s_l3["z"], due(h * NBK + kb + 1))
                            if kb:
                                dve.wait_ge(s_l3["acc"], due(h * NBK + kb))
                            for q in range(4):
                                s = kb * 4 + q
                                z = bank(kb % 6)[:, q * D:(q + 1) * D]
                                if kb == 0:
                                    last = nc.vector.tensor_scalar(a[:, q, :], z, AC[v][:, s:s + 1], 0.0,
                                                                   ALU.mult, ALU.max)
                                else:
                                    last = nc.vector.scalar_tensor_tensor(
                                        a[:, q, :], z, AC[v][:, s:s + 1], a[:, q, :], ALU.mult, ALU.max)
                            last.then_inc(s_l3["acc"], 1)
                        dve.wait_ge(s_l3["acc"], due((h + 1) * NBK))
                        nc.vector.tensor_tensor(a[:, 0:2, :], a[:, 0:2, :], a[:, 2:4, :], ALU.max)\
                          .then_inc(s_l3["fold"], 1)
                        dve.wait_ge(s_l3["fold"], due(h * 2 + 1))
                        nc.vector.tensor_tensor(a[:, 0, :], a[:, 0, :], a[:, 1, :], ALU.max)\
                          .then_inc(s_l3["fold"], 1)
                        dve.wait_ge(s_l3["fold"], due(h * 2 + 2))
                        nc.vector.tensor_tensor(X[:, gsl(h, D)], X[:, gsl(h, D)], a[:, 0, :], ALU.add)\
                          .then_inc(s_l3["x"], 1)
                graph_steps(dve, edges3, 1)
            dve.drain().then_inc(s_phase, 1)
            dve.wait_ge(s_phase, 50)

        @block.scalar
        def _(act):
            nc.scalar.preload_act_table_set("natural_log_exp_and_others")
            for k in range(G):
                act.dma_start(by4(X[:, k * GC:(k + 1) * GC]),
                              io["x"][k * GB:(k + 1) * GB].rearrange("b n d -> n b d")).then_inc(s_x, 16)
            for k in range(0, NW, GB):
                n = min(GB, NW - k)
                act.wait_ge(s_wt, k // GB + 1)
                nc.scalar.copy(WT[:, k:k + n, :], bank(k // GB)[:, 0:n * 128]
                               .rearrange("p (w n) -> p w n", w=n)).then_inc(s_wtc, 1)
            act.wait_ge(s_rowb, 1)
            nc.scalar.copy(ROWB[:, :, :], bank(4).rearrange("p (w n) -> p w n", w=4)).then_inc(s_wtc, 1)

            def store_at(t, u):
                if active(t, G):
                    act.wait_ge(s_tp, due(t + 1))
                    nc.scalar.copy(AT[:, gsl(t)], bank(u)).then_inc(s_at, 1)
            group_steps(act, store_at, 0)
            act.drain().then_inc(s_phase, 1)
            act.wait_ge(s_phase, 5)

            def ln_apply(layer, t, u, free_sem, per):
                act.wait_ge(s_hu, due(t + 1, layer * G))
                act.wait_ge(free_sem, due((t - 1) * per))
                for q in range(GB):
                    last = nc.scalar.activation(
                        HB[u][:, q * D:(q + 1) * D], X[:, bass.ds(t * GC + q * D, D)], ACT.Relu,
                        bias=LNB[:, bass.ds(t * GB + q, 1)], scale=LNS[:, bass.ds(t * GB + q, 1)])
                last.then_inc(s_h, 1)

            def layer0(t, u):
                if active(t, G):
                    ln_apply(0, t, u, s_p2[0], 1)
                h = t - 1
                if active(h, G):
                    act.wait_ge(s_p2[0], due(h + 1))
                    act.wait_ge(s_p2[2], due(h - 1))
                    nc.scalar.copy(TB[1 - u], bank(1 - u)).then_inc(s_p2[1], 1)
            group_steps(act, layer0, 1)
            act.drain().then_inc(s_phase, 1)
            act.wait_ge(s_phase, 10)

            def into1(t, u):
                if active(t, G):
                    ln_apply(1, t, u, s_p3[0], 1)
                h = t - 1
                if active(h, G):
                    act.wait_ge(s_p3[0], due(h + 1))
                    act.wait_ge(s_p3[2], due(h - 1))
                    nc.scalar.copy(TB[1 - u], bank(1 - u)).then_inc(s_p3[1], 1)
                    act.wait_ge(s_p3[2], due(h + 1))
                    nc.scalar.copy(R[:, gsl(h)], bank(2 + (1 - u))).then_inc(s_p3[3], 1)
            group_steps(act, into1, 1)
            act.drain().then_inc(s_phase, 1)
            act.wait_ge(s_phase, 15)

            def edges1(base):
                def step(m, k, t):
                    h = t - 1
                    if active(h, STEPS):
                        u = (k - 1) % 2
                        act.wait_ge(s_z, due(h + 1, base))
                        act.wait_ge(s_acd, due(h * 16, base * 16))
                        act.wait_ge(s_pre, due(h - 1, base))
                        nc.scalar.copy(ZC, bank(u)).then_inc(s_zc, 1)
                        nc.scalar.activation(GA[u], bank(u), ACT.Square, bias=offc).then_inc(s_sq, 1)
                        act.wait_ge(s_sq, due(h + 1, base))
                        nc.scalar.activation(GA[u], GA[u], ACT.Exp, scale=COEFF).then_inc(s_g, 1)
                    e = t - 2
                    if active(e, STEPS):
                        v = k % 2
                        act.wait_ge(s_min, due(e + 1, base))
                        nc.scalar.activation(SP[v], SP[v], ACT.Exp).then_inc(s_ex, 1)
                        act.wait_ge(s_ex, due(e + 1, base))
                        nc.scalar.activation(SP[v], SP[v], ACT.Ln, bias=1.0).then_inc(s_ln, 1)
                        act.wait_ge(s_gp2, due(e + 1, base))
                        act.wait_ge(s_hm, due(e - 1, base))
                        nc.scalar.copy(GS[v], bank(6, 2)).then_inc(s_gc, 1)
                return step
            chunk_steps(act, edges1(0), 2)
            act.drain().then_inc(s_phase, 1)
            act.wait_ge(s_phase, 20)
            general_rounds(act, lambda r: chunk_steps(act, edges1(r * STEPS), 2))
            act.drain().then_inc(s_phase, 1)
            act.wait_ge(s_phase, 25)

            def nodes1(t, u):
                if active(t, G):
                    act.wait_ge(s_p5[1], due(t + 1))
                    nc.scalar.activation(TB[u], TB[u], ACT.Exp).then_inc(s_p5[2], 1)
                    act.wait_ge(s_p5[2], due(t + 1))
                    nc.scalar.activation(TB[u], TB[u], ACT.Ln, bias=1.0).then_inc(s_p5[3], 1)
            group_steps(act, nodes1, 0)
            act.drain().then_inc(s_phase, 1)
            act.wait_ge(s_phase, 30)

            def messages(t, u):
                v = 1 - u
                if active(t, G):
                    ln_apply(2, t, u, s_p6[0], 1)
                h = t - 1
                if active(h, G):
                    act.wait_ge(s_p6[0], due(h + 1))
                    nc.scalar.copy(R[:, gsl(h)], bank(v)).then_inc(s_p6[1], 1)
                    act.wait_ge(s_p6[2], due(h + 1))
                    act.wait_ge(s_p6[4], due(h - 1))
                    nc.scalar.activation(TB[v], bank(2 + v), ACT.Relu, bias=m1c).then_inc(s_p6[3], 1)
                    act.wait_ge(s_p6[4], due(h + 1))
                    act.wait_ge(s_p6[6], due(h - 1))
                    nc.scalar.activation(UB[v], bank(4 + v), ACT.Relu).then_inc(s_p6[5], 1)
                e = t - 2
                if active(e, G):
                    act.wait_ge(s_p6[6], due(e + 1))
                    nc.scalar.activation(Y[:, gsl(e)], bank(6 + u), ACT.Relu).then_inc(s_p6[7], 1)
            group_steps(act, messages, 2)
            act.drain().then_inc(s_phase, 1)
            act.wait_ge(s_phase, 35)

            def gates(t, u):
                if active(t, G):
                    act.wait_ge(s_p8[0], due(t + 1))
                    act.wait_ge(s_p8[8], due(t - 1))
                    for k in range(2):
                        last = nc.scalar.activation(RZ[u][:, k * GC:(k + 1) * GC], bank(k), ACT.Sigmoid,
                                                    bias=brz[:, k:k + 1])
                    last.then_inc(s_p8[2], 1)
                    act.wait_ge(s_p8[4], due(t + 1))
                    nc.scalar.activation(NB_[u], VB[u], ACT.Tanh, bias=bin_).then_inc(s_p8[5], 1)
            group_steps(act, gates, 0)
            act.drain().then_inc(s_phase, 1)
            act.wait_ge(s_phase, 40)

            def into3(t, u):
                if active(t, G):
                    ln_apply(3, t, u, s_p9[0], 1)
                h = t - 1
                if active(h, G):
                    act.wait_ge(s_p9[0], due(h + 1))
                    act.wait_ge(s_p9[2], due(h - 1))
                    nc.scalar.copy(TB[1 - u], bank(1 - u)).then_inc(s_p9[1], 1)
            group_steps(act, into3, 1)
            act.drain().then_inc(s_phase, 1)
            act.wait_ge(s_phase, 45)

            many = act.value_load(FLAG[0:1, 0:1], min_val=0, max_val=1)
            with act.If(many > 0):
                act.nop()
            with act.Else():
                def parts(t, u):
                    if active(t, B):
                        act.wait_ge(s_l3["z"], due((t - 1) * NBK))
                        nc.scalar.copy(PARTS[u][:, 0], YR[:, :, gsl(t, 128)]).then_inc(s_l3["c1"], 1)
                        act.wait_ge(s_l3["r1"], due(t + 1))
                        nc.scalar.copy(PARTS[u][:, 1], REM[u]).then_inc(s_l3["c2"], 1)
                graph_steps(act, parts, 0)
            act.drain().then_inc(s_phase, 1)
            act.wait_ge(s_phase, 50)

        @block.tensor
        def _(pe):
            mm = nc.tensor.matmul
            pe.wait_ge(s_gp, 15)
            pe.wait_ge(s_w, 16 * 31)
            for k in range(0, NW, GB):
                for q in range(k, min(k + GB, NW)):
                    last = nc.tensor.transpose(bank(k // GB)[:, (q - k) * 128:(q - k + 1) * 128],
                                               NATW[:, q, :], ident[:, :])
                last.then_inc(s_wt, 1)
            pe.wait_ge(s_wtc, 2)
            pe.wait_ge(s_prep, 1)
            mm(bank(4), ONE[0:1, :], ROWN[0:1, :], start=True, stop=True, skip_group_check=True)
            mm(bank(4)[:, 128:256], MLN2, WT[:, WD2, :], start=False, stop=True, skip_group_check=True)\
                .then_inc(s_rowb, 1)
            pe.wait_ge(s_wtc, 5)

            def ranks(t, u):
                if active(t, G):
                    pe.wait_ge(s_adj[u], (t - u) * 8 + 16)
                    pe.wait_ge(s_at, due(t - 1))
                    for q in range(GB):
                        last = nc.tensor.transpose(bank(u)[:, q * N:(q + 1) * N], ADJ[u][:, q * N:(q + 1) * N],
                                                   ident[:, :])
                    last.then_inc(s_tp, 1)
                h = t - 1
                if active(h, G):
                    v = 1 - u
                    pe.wait_ge(s_mask, due(h * 2 + 1))
                    pe.wait_ge(s_rks, due((h - 1) * 2))
                    mm(bank(2 + v), after[:, :], MASK[v], start=True, stop=True).then_inc(s_rank, 1)
            group_steps(pe, ranks, 1)
            pe.drain().then_inc(s_phase, 1)
            pe.wait_ge(s_phase, 5)

            def layer0(t, u):
                h = t - 1
                if active(h, G):
                    v = 1 - u
                    pe.wait_ge(s_h, due(h + 1))
                    pe.wait_ge(s_p2[1], due(h - 1))
                    for q in range(GB):
                        last = mm(bank(v)[:, q * N:(q + 1) * N], HB[v][:, q * D:(q + 1) * D],
                                  AT[:, bass.ds(h * GC + q * N, N)], start=(q == 0), stop=True, skip_group_check=True)
                    last.then_inc(s_p2[0], 1)
                    pe.wait_ge(s_p2[1], due(h + 1))
                    pe.wait_ge(s_p2[3], due(h - 1))
                    for q in range(GB):
                        last = mm(bank(2 + v)[:, q * D:(q + 1) * D], TB[v][:, q * N:(q + 1) * N], W0[:, :],
                                  start=(q == 0), stop=True, skip_group_check=True)
                    last.then_inc(s_p2[2], 1)
            group_steps(pe, layer0, 1)
            pe.drain().then_inc(s_phase, 1)
            pe.wait_ge(s_phase, 10)

            def transpose_h(v, out, ready, count):
                for q in range(GB):
                    last = nc.tensor.transpose(out[:, q * N:(q + 1) * N], HB[v][:, q * D:(q + 1) * D], ident[:, :])
                last.then_inc(ready, 1)

            def into1(t, u):
                h = t - 1
                if active(h, G):
                    v = 1 - u
                    pe.wait_ge(s_h, due(h + 1, G))
                    pe.wait_ge(s_p3[1], due(h - 1))
                    transpose_h(v, bank(v), s_p3[0], 1)
                    pe.wait_ge(s_p3[1], due(h + 1))
                    pe.wait_ge(s_p3[3], due(h - 1))
                    for q in range(GB):
                        last = mm(bank(2 + v)[:, q * D:(q + 1) * D], TB[v][:, q * N:(q + 1) * N], WT[:, WA, :],
                                  start=(q == 0), stop=True, skip_group_check=True)
                    last.then_inc(s_p3[2], 1)
            group_steps(pe, into1, 1)
            pe.drain().then_inc(s_phase, 1)
            pe.wait_ge(s_phase, 15)

            def edges1(base, rbase):
                def step(m, k, t):
                    h = t - 1
                    if active(h, STEPS):
                        u = (k - 1) % 2
                        pe.wait_ge(s_pa, due(h + 1, base))
                        pe.wait_ge(s_sq, due(h - 1, base))
                        mm(PS[0:NG, u * 512:(u + 1) * 512], ones[:, :], PA[u][:, 0:HC], start=True, stop=True)
                        mm(PS[NG:128, u * 512:(u + 1) * 512], ones[:, :], PA[u][:, HC:CC], start=True, stop=True)\
                            .then_inc(s_z, 1)
                    e = t - 2
                    if active(e, STEPS):
                        v = k % 2
                        ch = (k - 2) % NC
                        gb = ((k - 2) // NC) % 2
                        b = m * 2 + (k - 2) // NC
                        pe.wait_ge(s_g, due(e + 1, base))
                        pe.wait_ge(s_sp, due(e, base))
                        for q in range(2):
                            last = mm(bank(2 + q), WT[q * NG:(q + 1) * NG, W1, :],
                                      GA[v][q * NG:(q + 1) * NG, :], start=True, stop=True)
                        last.then_inc(s_pre, 1)
                        pe.wait_ge(s_pa2, due(e + 1, base))
                        pe.wait_ge(s_gc, due(e, base))
                        if ch == 0:
                            pe.wait_ge(s_rf, due(b + 1, rbase))
                        for q in range(2):
                            last = mm(bank(6 + q), RF[gb], PA2[v][:, q * HC:(q + 1) * HC], start=True, stop=True)
                        last.then_inc(s_gp2, 1)
                    f = t - 3
                    if active(f, STEPS):
                        w = (k - 3) % 2
                        pe.wait_ge(s_sp, due(f + 1, base))
                        pe.wait_ge(s_hm, due(f, base))
                        for q in range(2):
                            last = mm(bank(4 + q), WT[:, W2, :], SP[w][:, q * HC:(q + 1) * HC],
                                      start=True, stop=True)
                        last.then_inc(s_wf, 1)
                return step
            chunk_steps(pe, edges1(0, 0), 3)
            pe.drain().then_inc(s_phase, 1)
            pe.wait_ge(s_phase, 20)
            general_rounds(pe, lambda r: chunk_steps(pe, edges1(r * STEPS, r * B), 3))
            pe.drain().then_inc(s_phase, 1)
            pe.wait_ge(s_phase, 25)

            def nodes1(t, u):
                if active(t, G):
                    pe.wait_ge(s_p5[4], due(t - 1))
                    mm(bank(u), WT[:, WD1, :], Y[:, gsl(t)], start=True, stop=True).then_inc(s_p5[0], 1)
                h = t - 2
                if active(h, G):
                    pe.wait_ge(s_p5[4], due(h + 1))
                    pe.wait_ge(s_p5[6], due(h - 1))
                    for q in range(GB):
                        last = mm(bank(2 + u)[:, q * D:(q + 1) * D], TB[u][:, q * N:(q + 1) * N], WT[:, WD2, :],
                                  start=(q == 0), stop=True, skip_group_check=True)
                    last.then_inc(s_p5[5], 1)
            group_steps(pe, nodes1, 2)
            pe.drain().then_inc(s_phase, 1)
            pe.wait_ge(s_phase, 30)

            def messages(t, u):
                h = t - 1
                if active(h, G):
                    v = 1 - u
                    pe.wait_ge(s_h, due(h + 1, 2 * G))
                    pe.wait_ge(s_p6[1], due(h - 1))
                    transpose_h(v, bank(v), s_p6[0], 1)
                    pe.wait_ge(s_p6[1], due(h + 1))
                    pe.wait_ge(s_p6[3], due(h - 1))
                    mm(bank(2 + v), WT[:, M1, :], R[:, gsl(h)], start=True, stop=True).then_inc(s_p6[2], 1)
                    pe.wait_ge(s_p6[3], due(h + 1))
                    pe.wait_ge(s_p6[5], due(h - 1))
                    for q in range(GB):
                        mm(bank(4 + v)[:, q * D:(q + 1) * D], TB[v][:, q * N:(q + 1) * N], WT[:, M2, :],
                           start=(q == 0), stop=True, skip_group_check=True)
                    mm(bank(4 + v), ONE[0:1, :], ROWB[0:1, 3:4, :].to_broadcast([1, GB, 128]), start=False, stop=True,
                       skip_group_check=True).then_inc(s_p6[4], 1)
                    pe.wait_ge(s_p6[5], due(h + 1))
                    pe.wait_ge(s_p6[7], due(h - 1))
                    for q in range(GB):
                        last = mm(bank(6 + v)[:, q * N:(q + 1) * N], UB[v][:, q * D:(q + 1) * D],
                                  AT[:, bass.ds(h * GC + q * N, N)], start=(q == 0), stop=True, skip_group_check=True)
                    last.then_inc(s_p6[6], 1)
            group_steps(pe, messages, 1)
            pe.drain().then_inc(s_phase, 1)
            pe.wait_ge(s_phase, 35)

            def gates(t, u):
                if active(t, G):
                    msg, ht = Y[:, gsl(t)], R[:, gsl(t)]
                    pe.wait_ge(s_p8[2], due(t))
                    for k in range(2):
                        mm(bank(k), WT[:, IH + k, :], msg, start=True, stop=False)
                        last = mm(bank(k), WT[:, HH + k, :], ht, start=False, stop=True)
                    last.then_inc(s_p8[0], 1)
                    pe.wait_ge(s_p8[4], due(t))
                    mm(bank(2), WT[:, IH + 2, :], msg, start=True, stop=True)
                    mm(bank(3), WT[:, HH + 2, :], ht, start=True, stop=True).then_inc(s_p8[1], 1)
                h = t - 1
                if active(h, G):
                    v = 1 - u
                    pe.wait_ge(s_p8[8], due(h + 1))
                    pe.wait_ge(s_p8[10], due(h - 1))
                    for q in range(GB):
                        last = nc.tensor.transpose(bank(4 + v)[:, q * N:(q + 1) * N],
                                                   UB[v][:, q * D:(q + 1) * D], ident[:, :])
                    last.then_inc(s_p8[9], 1)
            group_steps(pe, gates, 1)
            pe.drain().then_inc(s_phase, 1)
            pe.wait_ge(s_phase, 40)

            def into3(t, u):
                h = t - 1
                if active(h, G):
                    v = 1 - u
                    pe.wait_ge(s_h, due(h + 1, 3 * G))
                    pe.wait_ge(s_p9[1], due(h - 1))
                    transpose_h(v, bank(v), s_p9[0], 1)
                    pe.wait_ge(s_p9[1], due(h + 1))
                    pe.wait_ge(s_p9[4], due(h - 1))
                    pq = bank(6 if v else 4, 2)
                    for q in range(GB):
                        last = mm(pq[:, q * 256:(q + 1) * 256], TB[v][:, q * N:(q + 1) * N], W3[:, :, :],
                                  start=(q % 2 == 0), stop=True, skip_group_check=True)
                    last.then_inc(s_p9[2], 1)
            group_steps(pe, into3, 1)
            pe.drain().then_inc(s_phase, 1)
            pe.wait_ge(s_phase, 45)

            def slots(parts, oh, zb, kb):
                for k in range(3):
                    mm(zb, identb[:, :], parts[:, k, 0:1, :].to_broadcast([128, 4, D]), start=(k == 0), stop=True,
                       skip_group_check=True)
                for q in range(4):
                    for k in range(3):
                        last = mm(zb[:, q * D:(q + 1) * D], oh[:, kb * 4 + q, :], parts[:, k, 1, :],
                                  start=False, stop=True, skip_group_check=True)
                return last

            many = pe.value_load(FLAG[0:1, 0:1], min_val=0, max_val=1)
            with pe.If(many > 0):
                with pe.Fori(0, B) as b:
                    with pe.Fori(0, NR) as r:
                        n = b * NR + r
                        pe.wait_ge(s_gl["ac"], due(n * 16 + 16))
                        pe.wait_ge(s_gl["acs"], due(n + 1))
                        pe.sem_inc(s_passed, 1)
                        nc.tensor.transpose(bank(6)[:, 0:NS], ACT_[0][0:NS, :], ident[0:NS, 0:NS])\
                            .then_inc(s_gl["act"], 1)
                        pe.wait_ge(s_gl["oh"], due(n + 1))
                        pe.wait_ge(s_gl["c3"], due(b + 1))
                        for kb in range(NBK):
                            pe.wait_ge(s_gl["acc"], due(n * NBK + max(kb - 1, 0) + 1))
                            slots(PARTS[0], OH3[0], bank(kb % 2), kb).then_inc(s_gl["z"], 1)
            with pe.Else():
                def edges3(t, u):
                    if active(t, B):
                        pe.wait_ge(s_l3[f"ac{u}"], (t - u) * 8 + 16)
                        pe.wait_ge(s_l3["ac"], due(t - 1))
                        pe.sem_inc(s_passed, 1)
                        nc.tensor.transpose(bank(6 + u)[:, 0:NS], ACT_[u][0:NS, :], ident[0:NS, 0:NS])\
                            .then_inc(s_l3["act"], 1)
                    h = t - 1
                    if active(h, B):
                        v = 1 - u
                        pe.wait_ge(s_l3["oh"], due(h + 1))
                        pe.wait_ge(s_l3["c3"], due(h + 1))
                        for kb in range(NBK):
                            pe.wait_ge(s_l3["acc"], due((h - 1) * NBK + kb + 1))
                            slots(PARTS[v], OH3[v], bank(kb), kb).then_inc(s_l3["z"], 1)
                graph_steps(pe, edges3, 1)
            pe.drain().then_inc(s_phase, 1)
            pe.wait_ge(s_phase, 50)


_INS = ['x', 'adj', 'L0_gnn_W', 'L0_gnn_b', 'L1_gnn_W1', 'L1_gnn_b1', 'L1_gnn_W2', 'L1_gnn_b2', 'L1_gnn_Wa',
        'L1_gnn_Wd1', 'L1_gnn_bd1', 'L1_gnn_Wd2', 'L1_gnn_bd2', 'L2_gnn_W1', 'L2_gnn_b1', 'L2_gnn_W2',
        'L2_gnn_b2', 'L2_gnn_W_ih', 'L2_gnn_W_hh', 'L2_gnn_b_ih', 'L2_gnn_b_hh', 'L3_gnn_W', 'L3_gnn_b']


def kernel(**inputs):
    import concourse.bacc as bacc
    from concourse.bass_utils import run_bass_kernel_spmd

    nc = bacc.Bacc("TRN2", target_bir_lowering=False, num_devices=1, dynamic_dma_scratch_size=1024)
    arrays, io = {}, {}
    for name in _INS:
        a = np.ascontiguousarray(inputs[name])
        arrays[name + "_dram"] = a
        io[name] = nc.dram_tensor(name + "_dram", a.shape, mybir.dt.from_np(a.dtype), kind="ExternalInput").ap()
    io["out"] = nc.dram_tensor("out_dram", (B, N, D), F32, kind="ExternalOutput").ap()
    build(nc, io)
    r = run_bass_kernel_spmd(nc, [arrays], core_ids=[0])
    return r.results[0]["out_dram"]
```

```python
from contextlib import ExitStack

import numpy as np

import concourse.bass as bass
from concourse import mybir

F32 = mybir.dt.float32
BF16 = mybir.dt.bfloat16
I32 = mybir.dt.int32
ALU = mybir.AluOpType
ACT = mybir.ActivationFunctionType
AX = mybir.AxisListType

B, N, D = 64, 128, 128
NG = 64
GB = 4
G = B // GB
GC = GB * D
NS = 20
NR = -(-N // NS)
BPG = NS // 4
CC = 2 * GC
HC = GC
UNROLL = GB * BPG // 2
STEPS = G * UNROLL
NO_SLOT = 200.0
CUTOFF = 5.0
WIDTH = np.float32(CUTOFF) / np.float32(NG - 1)
COEFF = float(np.float32(-0.5) / (WIDTH * WIDTH))
LN2 = float(np.log(2.0))
SOFT_MAX = 20.0
EXP_MAX = float(np.exp(SOFT_MAX))
LN_EPS = 1e-5
DEG_EPS = 1e-8
WA, W1, W2, WD1, WD2, M1, M2, IH, HH = 0, 1, 2, 3, 4, 5, 6, 7, 10
NW = 13
LOADS = 26


def due(value, base=0):
    return 0 if isinstance(value, int) and value <= 0 else value + base


def active(h, n):
    return not isinstance(h, int) or 0 <= h < n


def group_steps(eng, body, depth, head=6):
    for t in range(head):
        body(t, t % 2)
    with eng.Fori(0, (G - head) // 2) as i:
        for u in range(2):
            body(i * 2 + (head + u), u)
    for t in range(G, G + depth):
        body(t, t % 2)


def chunk_steps(eng, step, depth):
    for k in range(UNROLL):
        step(0, k, k)
    with eng.Fori(1, G) as m:
        for k in range(UNROLL):
            step(m, k, m * UNROLL + k)
    for k in range(depth):
        step(G, k, STEPS + k)


def graph_steps(eng, body, depth):
    for t in range(4):
        body(t, t % 2)
    with eng.Fori(0, (B - 4) // 2) as i:
        for u in range(2):
            body(i * 2 + (4 + u), u)
    for t in range(B, B + depth):
        body(t, t % 2)


def place(m, k):
    j = 2 * k
    return m * GB + j // BPG, 4 * (j % BPG), j % BPG == BPG - 1


def carries():
    side = [None] * UNROLL
    for k in reversed(range(UNROLL)):
        _, slot, split = place(0, k)
        if slot or split:
            after_ = side[k + 1] if k + 1 < UNROLL else None
            side[k] = 0 if split else 9 if after_ == 0 else 0
    return side


CARRY = carries()


def build(nc, io):
    ctx = ExitStack()
    with ctx:
        def sb(name, shape, dt=F32):
            return ctx.enter_context(nc.sbuf_tensor(name, shape, dt))

        def sem(name):
            return ctx.enter_context(nc.semaphore(name))

        X = sb("X", [128, B * D])
        AT = sb("AT", [128, B * N])
        YR = sb("YR", [128, 2, B * N])
        Y, R = YR[:, 0, :], YR[:, 1, :]
        RANK = sb("RANK", [128, B * N], BF16)
        IOTA = sb("IOTA", [128, (NS + 4) * N], BF16)
        WT = sb("WT", [128, NW, 128])
        W0 = sb("W0", [128, 128])
        W3 = sb("W3", [128, 2, 128])
        ident = sb("ident", [128, 128])
        identb = sb("identb", [128, 128], BF16)
        upto = sb("upto", [128, 128], BF16)
        ones = sb("ones", [128, NG])
        ROWB = sb("ROWB", [128, 4, 128])
        COLB = sb("COLB", [128, 16])
        STAT = sb("STAT", [128, 3, B])
        STATB = sb("STATB", [128, 2, GB * 8 + 16])
        ONE = sb("ONE", [1, 128])
        MX = sb("MX", [128, 24])
        FLAG = sb("FLAG", [1, 8], I32)
        WORK = sb("WORK", [128, 14000])
        PS = ctx.enter_context(nc.psum_tensor("PS", [128, 8 * 512], F32))
        acD = nc.dram_tensor("ac_slots", (NR * STEPS, 2, HC), F32, kind="Internal").ap()
        ac_rows = acD.rearrange("c h w -> (c h w)").rearrange("(g s i) -> g s i", s=NS, i=N)

        b1c, b2c, bd1c, m1c = (COLB[:, k:k + 1] for k in range(4))
        brz = COLB[:, 4:6]
        bin_, bhn = COLB[:, 6:7], COLB[:, 9:10]
        offc = COLB[:, 10:11]
        bih, bhh = COLB[:, 4:7], COLB[:, 7:10]
        DEG, LNS, LNB = STAT[:, 0, :], STAT[:, 1, :], STAT[:, 2, :]

        def bank(k, n=1):
            return PS[:, k * 512:(k + n) * 512]

        class Carve:
            def __init__(self):
                self.at = 0

            def __call__(self, words, dt=F32):
                a = WORK[:, self.at:self.at + words]
                self.at += words
                assert self.at <= 14000, self.at
                return a if dt == F32 else a.bitcast(dt)

        def gsl(t, k=GC):
            return bass.ds(t * k, k)

        def by4(ap):
            return ap.rearrange("p (b n) -> p b n", b=GB)

        s_passed = sem("wait_passed")
        s_phase = sem("phase")
        s_gen = sem("general_round")
        s_w = sem("weights_loaded")
        s_x = sem("x_loaded")
        s_gp = sem("gpsimd_constants")
        s_prep = sem("prep_dve")
        s_wt = sem("weights_transposed")
        s_wtc = sem("weights_copied")
        s_rowb = sem("row_biases_summed")
        s_adj = [sem("adj_loaded0"), sem("adj_loaded1")]
        s_deg = sem("degrees_read")
        s_tp = sem("adj_transposed")
        s_at = sem("at_stored")
        s_mask = sem("mask_made")
        s_rank = sem("rank_counted")
        s_rks = sem("rank_stored")
        s_d0 = sem("degree_root")
        s_bn = sem("ln_stats")
        s_var = sem("ln_var")
        s_rs = sem("ln_scale")
        s_h = sem("h_ready")
        s_hu = sem("h_used")
        s_p2 = [sem(f"l0_{n}") for n in ("support", "support_copied", "out", "x", "xb")]
        s_p3 = [sem(f"l1in_{n}") for n in ("t", "tc", "rf", "rfc")]
        s_oh = sem("onehot_made")
        s_pa = sem("weighted_made")
        s_pa2 = sem("weighted2_made")
        s_rf = sem("rf_copied")
        s_z = sem("z_gathered")
        s_zc = sem("z_copied")
        s_sq = sem("square_made")
        s_g = sem("gauss_made")
        s_acd = sem("ac_saved")
        s_pre = sem("pre_made")
        s_min = sem("pre_capped")
        s_ex = sem("exp_made")
        s_ln = sem("log_made")
        s_sp = sem("softplus_made")
        s_gp2 = sem("gather_made")
        s_gc = sem("gather_copied")
        s_wf = sem("filter_made")
        s_hm = sem("message_made")
        s_red = sem("message_summed")
        s_fin = sem("first_graph_summed")
        s_ya = sem("general_added")
        s_io = sem("iota_moved")
        s_p5 = [sem(f"l1out_{n}") for n in ("t1", "cap", "exp", "log", "sp", "t2", "x", "xb")]
        s_p6 = [sem(f"l2m_{n}") for n in ("ht", "htc", "m1", "m1c", "m2", "m2c", "msg", "msgc")]
        s_p8 = [sem(f"l2g_{n}") for n in ("rz", "n", "sig", "rh", "pre", "tanh", "dif", "zd", "new", "t", "x")]
        s_p9 = [sem(f"l3in_{n}") for n in ("t", "tc", "pq", "p", "q")]
        s_l3 = {n: sem(f"l3_{n}") for n in ("ac0", "ac1", "act", "ac", "oh", "c1", "r1", "c2", "c3",
                                            "z", "acc", "fold", "x")}
        s_l3r = sem("l3_relu")
        s_l3p = sem("l3_remainders")
        s_gl = {n: sem(f"l3g_{n}") for n in ("ac", "act", "acs", "sh", "oh", "c1", "r1", "c2", "c3", "z",
                                             "acc", "fold", "x")}
        s_out = sem("out_stored")
        s_flag = sem("flag_made")

        def leave_round(eng, r):
            eng.drain().then_inc(s_gen, 1)
            eng.wait_ge(s_gen, due(r * 5))
            eng.sem_inc(s_passed, 1)

        c = Carve()
        NATW = c(NW * 128).rearrange("p (w n) -> p w n", w=NW)
        W3N = c(256).rearrange("p (w n) -> p w n", w=2)
        ROWN = c(512)
        MLN2 = c(128)
        ADJ = [c(GC), c(GC)]
        MASK = [c(GC // 2, BF16), c(GC // 2, BF16)]
        SUMW2 = c(1)
        PINF = c(64)

        c = Carve()
        HB = [c(GC), c(GC)]
        TB = [c(GC), c(GC)]
        XB = [c(GC), c(GC)]
        UB = [c(GC), c(GC)]
        VB = [c(GC), c(GC)]
        RZ = [c(2 * GC), c(2 * GC)]
        NB_ = [c(GC), c(GC)]

        c = Carve()
        OH = [c(CC // 2, BF16), c(CC // 2, BF16)]
        PA = [c(CC), c(CC)]
        PA2 = [c(CC), c(CC)]
        ZC = c(HC)
        GA = [c(HC), c(HC)]
        SP = [c(CC), c(CC)]
        GS = [c(CC), c(CC)]
        HS = c(10 * N).rearrange("p (s i) -> p s i", i=N)
        YT = c(N)
        RF = [c(128), c(128)]

        c = Carve()
        OH3 = [c(NS * N // 2, BF16).rearrange("p (s i) -> p s i", i=N) for _ in range(2)]
        PARTS = [c(3 * D, BF16).rearrange("p (k w n) -> p k w n", k=3, w=2) for _ in range(2)]
        REM = [c(2 * D).rearrange("p (w n) -> p w n", w=2) for _ in range(2)]
        ACT_ = [c(N), c(N)]
        AC = [c(NS), c(NS)]
        ACC = [c(GC).rearrange("p (s o) -> p s o", o=D) for _ in range(2)]
        MSG = [[c(GC).rearrange("p (s o) -> p s o", o=D) for _ in range(BPG - 1)] for _ in range(2)]
        SHR = c(N // 2, BF16)
        SHV = c(1)

        def spread(ap, b, split):
            if split:
                return ap[:, bass.ds(b * N, 2 * N)].rearrange("p (g a i) -> p g a i", g=2, a=1)\
                    .to_broadcast([128, 2, 4, N])
            return ap[:, gsl(b, N)].rearrange("p (a i) -> p a i", a=1).to_broadcast([128, 8, N])

        def spread_rank(b):
            return RANK[:, gsl(b, N)].rearrange("p (a i) -> p a i", a=1).to_broadcast([128, NS, N])

        def slots_of(ap, split):
            return ap.rearrange("p (g s i) -> p g s i", g=2, i=N) if split else \
                ap.rearrange("p (s i) -> p s i", i=N)

        def general_rounds(eng, one_round, last_dma=False):
            many = eng.value_load(FLAG[0:1, 0:1], min_val=0, max_val=1)
            with eng.If(many > 0):
                with eng.Fori(1, NR) as r:
                    one_round(r)
                    if last_dma:
                        eng.wait_ge(s_acd, due((r + 1) * (16 * STEPS)))
                        eng.sem_inc(s_passed, 1)
                    leave_round(eng, r)

        block = ctx.enter_context(nc.Block())

        @block.sync
        def _(sp):
            def load_adj(t, u):
                if not active(t, G):
                    return
                sp.wait_ge(s_deg, due(t - 1))
                sp.wait_ge(s_tp, due(t - 1))
                sp.dma_start(by4(ADJ[u]), io["adj"][bass.ds(t * GB, GB), :, :]
                             .rearrange("b i j -> i b j")).then_inc(s_adj[u], 16)
            group_steps(sp, load_adj, 0)
            sp.drain().then_inc(s_phase, 1)
            sp.wait_ge(s_phase, 5)
            sp.drain().then_inc(s_phase, 1)
            sp.wait_ge(s_phase, 10)
            sp.drain().then_inc(s_phase, 1)
            sp.wait_ge(s_phase, 15)

            def save_ac(base):
                def step(m, k, t):
                    h = t - 1
                    if not active(h, STEPS):
                        return
                    sp.wait_ge(s_zc, due(h + 1, base))
                    sp.dma_start(acD[bass.ds(h + base, 1)].rearrange("c h w -> (c h) w"),
                                 ZC[0:NG + 1:NG, :]).then_inc(s_acd, 16)
                return step
            chunk_steps(sp, save_ac(0), 1)
            sp.wait_ge(s_acd, 16 * STEPS)
            sp.drain().then_inc(s_phase, 1)
            sp.wait_ge(s_phase, 20)
            general_rounds(sp, lambda r: chunk_steps(sp, save_ac(r * STEPS), 1), last_dma=True)
            sp.drain().then_inc(s_phase, 1)
            sp.wait_ge(s_phase, 25)
            sp.drain().then_inc(s_phase, 1)
            sp.wait_ge(s_phase, 30)
            sp.drain().then_inc(s_phase, 1)
            sp.wait_ge(s_phase, 35)
            sp.drain().then_inc(s_phase, 1)
            sp.wait_ge(s_phase, 40)
            sp.drain().then_inc(s_phase, 1)
            sp.wait_ge(s_phase, 45)

            many = sp.value_load(FLAG[0:1, 0:1], min_val=0, max_val=1)
            with sp.If(many > 0):
                with sp.Fori(0, B) as b:
                    with sp.Fori(0, NR) as r:
                        sp.wait_ge(s_gl["act"], due(b * NR + r + 1))
                        sp.dma_start(ACT_[0][0:NS, :], ac_rows[bass.ds(r * B + b, 1)]
                                     .rearrange("a s i -> (a s) i")).then_inc(s_gl["ac"], 16)
            with sp.Else():
                def load_ac(t, u):
                    if active(t, B):
                        sp.wait_ge(s_l3["act"], due(t - 1))
                        sp.dma_start(ACT_[u][0:NS, :], ac_rows[bass.ds(t, 1)].rearrange("a s i -> (a s) i"))\
                          .then_inc(s_l3[f"ac{u}"], 16)
                graph_steps(sp, load_ac, 0)
            sp.drain().then_inc(s_phase, 1)
            sp.wait_ge(s_phase, 50)
            for k in range(G):
                sp.dma_start(io["out"][k * GB:(k + 1) * GB].rearrange("b n d -> n b d"),
                             by4(X[:, k * GC:(k + 1) * GC])).then_inc(s_out, 16)
            sp.wait_ge(s_out, 16 * G)

        @block.gpsimd
        def _(pool):
            nc.gpsimd.memset(ident[:, :], 0.0).then_inc(s_gp, 1)
            nc.gpsimd.memset(identb[:, :], 0.0).then_inc(s_gp, 1)
            nc.gpsimd.memset(upto[:, :], 0.0).then_inc(s_gp, 1)
            nc.gpsimd.memset(ones[:, :], 1.0).then_inc(s_gp, 1)
            nc.gpsimd.memset(MLN2[:, :], -LN2).then_inc(s_gp, 1)
            nc.gpsimd.memset(PINF[:, :], -0.5).then_inc(s_gp, 1)
            nc.gpsimd.memset(MX[:, :], 0.0).then_inc(s_gp, 1)
            nc.gpsimd.memset(COLB[:, 11:16], -0.5).then_inc(s_gp, 1)
            nc.gpsimd.memset(ONE[:, :], 1.0).then_inc(s_gp, 1)
            pool.wait_ge(s_gp, 9)
            nc.gpsimd.affine_select(out=ident[:, :], in_=ident[:, :], compare_op=ALU.not_equal, fill=1.0,
                                    base=0, pattern=[[-1, 128]], channel_multiplier=1).then_inc(s_gp, 1)
            nc.gpsimd.affine_select(out=identb[:, :], in_=identb[:, :], compare_op=ALU.not_equal, fill=1.0,
                                    base=0, pattern=[[-1, 128]], channel_multiplier=1).then_inc(s_gp, 1)
            nc.gpsimd.affine_select(out=upto[:, :], in_=upto[:, :], compare_op=ALU.is_gt, fill=1.0,
                                    base=0, pattern=[[1, 128]], channel_multiplier=-1).then_inc(s_gp, 1)
            for at, n in ((0, NS), (NS, 4)):
                nc.gpsimd.iota(IOTA[:, at * N:(at + n) * N].rearrange("p (s i) -> p s i", i=N),
                               pattern=[[1, n], [0, N]], base=1, channel_multiplier=0,
                               allow_small_or_imprecise_dtypes=True).then_inc(s_gp, 1)
            for h in range(2):
                pool.wait_ge(s_gp, 14 + h)
                nc.gpsimd.iota(offc[h * NG:(h + 1) * NG, :], pattern=[[0, 1]], base=0, channel_multiplier=1,
                               allow_small_or_imprecise_dtypes=True).then_inc(s_gp, 1)
            pool.wait_ge(s_gp, 16)
            pool.wait_ge(s_d0, 1)
            nc.gpsimd.tensor_tensor(DEG, DEG, PINF, ALU.pow).then_inc(s_d0, 1)
            pool.drain().then_inc(s_phase, 1)
            pool.wait_ge(s_phase, 5)

            def ln_root(layer, add_bias=None):
                base = layer * G

                def step(t, u):
                    if active(t, G):
                        pool.wait_ge(s_var, due(t + 1, base))
                        v = LNS[:, bass.ds(t * GB, GB)]
                        nc.gpsimd.tensor_tensor(v, v, COLB[:, 11:15], ALU.pow).then_inc(s_rs, 1)
                    if add_bias is not None:
                        add_bias(t, u)
                return step

            def xb0(t, u):
                if active(t, G):
                    pool.wait_ge(s_p2[3], due(t - 1))
                    nc.gpsimd.tensor_tensor(by4(XB[u]), by4(X[:, gsl(t)]),
                                            ROWB[:, 0:1, :].to_broadcast([128, GB, 128]), ALU.add)\
                      .then_inc(s_p2[4], 1)
            group_steps(pool, ln_root(0, xb0), 0)
            pool.drain().then_inc(s_phase, 1)
            pool.wait_ge(s_phase, 10)
            group_steps(pool, ln_root(1), 0)
            pool.drain().then_inc(s_phase, 1)
            pool.wait_ge(s_phase, 15)

            def weigh(base, rbase):
                def step(m, k, t):
                    if not active(t, STEPS):
                        return
                    u = k % 2
                    b, slot, split = place(m, k)
                    if slot == 0 or split:
                        b2, q = (b + 1, 2 * k // BPG + 1) if split else (b, 2 * k // BPG)
                        pool.wait_ge(s_gp2, due((b2 - 1) * BPG, base * 2))
                        pool.sem_inc(s_passed, 1)
                        nc.gpsimd.tensor_copy(RF[q % 2], R[:, gsl(b2, 128)]).then_inc(s_rf, 1)
                    pool.wait_ge(s_oh, due(t + 1, base))
                    pool.wait_ge(s_z, due(t - 1, base))
                    pool.sem_inc(s_passed, 1)
                    nc.gpsimd.tensor_tensor(slots_of(PA[u], split), slots_of(OH[u], split),
                                            spread(AT, b, split), ALU.mult).then_inc(s_pa, 1)
                    pool.wait_ge(s_pa, due(t + 1, base))
                    pool.wait_ge(s_gp2, due(2 * (t - 1), base * 2))
                    nc.gpsimd.tensor_tensor(PA2[u], PA[u], PA[u], ALU.mult).then_inc(s_pa2, 1)
                return step
            chunk_steps(pool, weigh(0, 0), 0)
            pool.drain().then_inc(s_phase, 1)
            pool.wait_ge(s_phase, 20)
            general_rounds(pool, lambda r: chunk_steps(pool, weigh(r * STEPS, r * B), 0))
            pool.drain().then_inc(s_phase, 1)
            pool.wait_ge(s_phase, 25)

            def xb1(t, u):
                if active(t, G):
                    pool.wait_ge(s_p5[6], due(t - 1))
                    nc.gpsimd.tensor_tensor(by4(XB[u]), by4(X[:, gsl(t)]),
                                            ROWB[:, 1:2, :].to_broadcast([128, GB, 128]), ALU.add)\
                      .then_inc(s_p5[7], 1)
            group_steps(pool, xb1, 0)
            pool.drain().then_inc(s_phase, 1)
            pool.wait_ge(s_phase, 30)
            group_steps(pool, ln_root(2), 0)
            pool.drain().then_inc(s_phase, 1)
            pool.wait_ge(s_phase, 35)

            def blend(t, u):
                h = t - 1
                if active(h, G):
                    v = 1 - u
                    ht = R[:, gsl(h)]
                    pool.wait_ge(s_p8[5], due(h + 1))
                    pool.wait_ge(s_p8[9], due(h - 1))
                    nc.gpsimd.tensor_tensor(UB[v], ht, NB_[v], ALU.subtract).then_inc(s_p8[6], 1)
                    pool.wait_ge(s_p8[6], due(h + 1))
                    nc.gpsimd.tensor_tensor(UB[v], UB[v], RZ[v][:, GC:2 * GC], ALU.mult).then_inc(s_p8[7], 1)
                    pool.wait_ge(s_p8[7], due(h + 1))
                    nc.gpsimd.tensor_tensor(UB[v], UB[v], NB_[v], ALU.add).then_inc(s_p8[8], 1)
            group_steps(pool, blend, 1)
            pool.drain().then_inc(s_phase, 1)
            pool.wait_ge(s_phase, 40)
            group_steps(pool, ln_root(3), 0)
            pool.drain().then_inc(s_phase, 1)
            pool.wait_ge(s_phase, 45)

            many = pool.value_load(FLAG[0:1, 0:1], min_val=0, max_val=1)
            with pool.If(many > 0):
                pool.nop()
            with pool.Else():
                def remainders(t, u):
                    if active(t, B):
                        y2 = YR[:, :, gsl(t, 128)]
                        pool.wait_ge(s_l3["c1"], due(t + 1))
                        pool.wait_ge(s_l3["c2"], due(t - 1))
                        pool.sem_inc(s_passed, 1)
                        nc.gpsimd.tensor_tensor(REM[u], y2, PARTS[u][:, 0], ALU.subtract).then_inc(s_l3["r1"], 1)
                        pool.wait_ge(s_l3["c2"], due(t + 1))
                        nc.gpsimd.tensor_tensor(PARTS[u][:, 2], REM[u], PARTS[u][:, 1], ALU.subtract)\
                          .then_inc(s_l3["c3"], 1)
                graph_steps(pool, remainders, 0)
            pool.drain().then_inc(s_phase, 1)
            pool.wait_ge(s_phase, 50)

        @block.vector
        def _(dve):
            dve.wait_ge(s_gp, 16)
            def ranks(t, u):
                if active(t, G):
                    dve.wait_ge(s_adj[u], (t - u) * 8 + 16)
                    nc.vector.reduce_sum(DEG[:, bass.ds(t * GB, GB)], by4(ADJ[u]), AX.X).then_inc(s_deg, 1)
                    dve.wait_ge(s_at, due(t + 1))
                    dve.wait_ge(s_rank, due(t - 1))
                    nc.vector.tensor_scalar(MASK[u], AT[:, gsl(t)], 0.0, None, ALU.not_equal).then_inc(s_mask, 1)
                    nc.vector.tensor_scalar(RANK[:, gsl(t)], AT[:, gsl(t)], 0.0, NO_SLOT,
                                            ALU.is_equal, ALU.mult).then_inc(s_mask, 1)
                h = t - 1
                if active(h, G):
                    dve.wait_ge(s_rank, due(h + 1))
                    dve.wait_ge(s_mask, due(h * 2 + 2))
                    nc.vector.tensor_tensor(RANK[:, gsl(h)], RANK[:, gsl(h)], bank(2 + (1 - u)), ALU.add)\
                      .then_inc(s_rks, 1)
                    nc.vector.reduce_max(MX[0:1, bass.ds(h, 1)], PS[0:1, (3 - u) * 512:(4 - u) * 512], AX.X)\
                      .then_inc(s_rks, 1)
            group_steps(dve, ranks, 1)
            nc.vector.tensor_scalar(offc, offc, -float(WIDTH), None, ALU.mult).then_inc(s_prep, 1)
            dve.wait_ge(s_w, 16 * LOADS)
            nc.vector.tensor_tensor(COLB[:, 4:6], COLB[:, 4:6], COLB[:, 7:9], ALU.add).then_inc(s_prep, 1)
            nc.vector.reduce_sum(SUMW2, NATW[:, W2, :], AX.X).then_inc(s_prep, 1)
            nc.vector.tensor_tensor(W3[:, 0, :], W3N[:, 0, :], W3N[:, 1, :], ALU.subtract).then_inc(s_prep, 1)
            nc.vector.tensor_copy(W3[:, 1, :], W3N[:, 1, :]).then_inc(s_prep, 1)
            dve.wait_ge(s_prep, 5)
            nc.vector.scalar_tensor_tensor(b2c, SUMW2, -LN2, b2c, ALU.mult, ALU.add).then_inc(s_prep, 1)
            dve.wait_ge(s_deg, G)
            nc.vector.tensor_scalar(DEG, DEG, DEG_EPS, None, ALU.add).then_inc(s_d0, 1)
            dve.wait_ge(s_rks, 2 * G)
            nc.vector.reduce_max(MX[0:1, G:G + 1], MX[0:1, 0:G], AX.X).then_inc(s_flag, 1)
            dve.wait_ge(s_flag, 1)
            nc.vector.tensor_scalar(FLAG[0:1, 0:1], MX[0:1, G:G + 1], float(NS) + 0.5, None, ALU.is_gt)\
              .then_inc(s_flag, 1)
            dve.drain().then_inc(s_phase, 1)
            dve.wait_ge(s_phase, 5)

            def ln_stats(layer, t, u):
                base = layer * G
                st = STATB[:, u, 0:GB * 6].rearrange("p (b k) -> p b k", k=6)
                mv = STATB[:, u, GB * 6:GB * 8].rearrange("p (b k) -> p b k", k=2)
                for q in range(GB):
                    nc.vector.bn_stats(st[:, q, :], X[:, bass.ds(t * GC + q * D, D)]).then_inc(s_bn, 1)
                dve.wait_ge(s_bn, due(t * (2 * GB + 1) + GB, layer * G * (2 * GB + 1)))
                dve.sem_inc(s_passed, 1)
                for q in range(GB):
                    nc.vector.bn_aggr(mv[:, q, :], st[:, q, :]).then_inc(s_bn, 1)
                dve.wait_ge(s_bn, due(t * (2 * GB + 1) + 2 * GB, layer * G * (2 * GB + 1)))
                v = LNS[:, bass.ds(t * GB, GB)]
                nc.vector.tensor_scalar(v, mv[:, :, 1], LN_EPS, None, ALU.add).then_inc(s_var, 1)
                nc.vector.tensor_scalar(LNB[:, bass.ds(t * GB, GB)], mv[:, :, 0], -1.0, None, ALU.mult)\
                  .then_inc(s_bn, 1)

            def ln_shift(layer, t):
                dve.wait_ge(s_rs, due(t + 1, layer * G))
                dve.wait_ge(s_bn, due((t + 1) * (2 * GB + 1), layer * G * (2 * GB + 1)))
                v, s = LNS[:, bass.ds(t * GB, GB)], LNB[:, bass.ds(t * GB, GB)]
                if layer == 0:
                    nc.vector.tensor_tensor(v, v, DEG[:, bass.ds(t * GB, GB)], ALU.mult).then_inc(s_prep, 1)
                    dve.wait_ge(s_prep, due(t + 7))
                nc.vector.tensor_tensor(s, s, v, ALU.mult).then_inc(s_hu, 1)

            dve.wait_ge(s_x, 16 * 4)

            def layer0(t, u):
                if active(t, G):
                    ln_stats(0, t, u)
                if active(t - 1, G):
                    ln_shift(0, t - 1)
                h = t - 3
                if active(h, G):
                    dve.wait_ge(s_p2[2], due(h + 1))
                    dve.wait_ge(s_p2[4], due(h + 1))
                    for q in range(GB):
                        last = nc.vector.scalar_tensor_tensor(
                            X[:, bass.ds(h * GC + q * D, D)], bank(2 + (1 - u))[:, q * D:(q + 1) * D],
                            DEG[:, bass.ds(h * GB + q, 1)], XB[1 - u][:, q * D:(q + 1) * D],
                            ALU.mult, ALU.add)
                    last.then_inc(s_p2[3], 1)
            group_steps(dve, layer0, 3)
            dve.drain().then_inc(s_phase, 1)
            dve.wait_ge(s_phase, 10)

            def norm1(t, u):
                if active(t, G):
                    ln_stats(1, t, u)
                if active(t - 1, G):
                    ln_shift(1, t - 1)
            group_steps(dve, norm1, 1)
            dve.drain().then_inc(s_phase, 1)
            dve.wait_ge(s_phase, 15)

            def sum_slots(dst, lo, hi):
                return nc.vector.reduce_sum(dst, HS[:, lo:hi, :].rearrange("p s i -> p i s"), AX.X)

            def edges1(base, rbase, general):
                def step(m, k, t):
                    u = k % 2
                    if active(t, STEPS):
                        b, slot, split = place(m, k)
                        dve.wait_ge(s_pa, due(t - 1, base))
                        nc.vector.tensor_tensor(slots_of(OH[u], split), spread(RANK, b, split),
                                                slots_of(IOTA[:, slot * N:(slot + 8) * N], split),
                                                ALU.is_equal).then_inc(s_oh, 1)
                    e = t - 4
                    if active(e, STEPS):
                        ek = (k - 4) % UNROLL
                        eb, eslot, esplit = place(m if k >= 4 else m - 1, ek)
                        dve.wait_ge(s_wf, due(e + 1, base))
                        dve.wait_ge(s_gc, due(2 * (e + 1), base * 2))
                        dve.wait_ge(s_red, due(e, base))
                        nc.vector.scalar_tensor_tensor(
                            HS[:, 1:9, :], bank(4, 2).rearrange("p (s i) -> p s i", i=N), b2c,
                            GS[u].rearrange("p (s i) -> p s i", i=N), ALU.add, ALU.mult).then_inc(s_hm, 1)
                        dve.wait_ge(s_hm, due(e + 1, base))
                        into, out = CARRY[ek], CARRY[ek + 1] if ek + 1 < UNROLL else None
                        whole = YT if general else Y[:, gsl(eb, N)]
                        lo, hi = (0 if into == 0 else 1), (10 if into == 9 else 9)
                        if esplit:
                            last = sum_slots(whole, lo, 5)
                            last.then_inc(s_fin, 1)
                            sum_slots(HS[:, out, :], 5, 9).then_inc(s_red, 1)
                        elif out is None or eslot + 8 == NS:
                            sum_slots(whole, lo, hi).then_inc(s_red, 1)
                        else:
                            sum_slots(HS[:, out, :], lo, hi).then_inc(s_red, 1)
                        if general and (esplit or eslot + 8 == NS):
                            dve.wait_ge(s_red, due(e + 1, base))
                            if esplit:
                                dve.wait_ge(s_fin, due(1 + 2 * (m if k >= 4 else m - 1) + (ek >= UNROLL // 2),
                                                       rbase))
                            nc.vector.tensor_tensor(Y[:, gsl(eb, N)], Y[:, gsl(eb, N)], YT, ALU.add)\
                              .then_inc(s_ya, 1)
                    h = t - 2
                    if active(h, STEPS):
                        pre = bank(2 if u == 0 else 6, 2)
                        dve.wait_ge(s_ex, due(h + 1, base))
                        nc.vector.tensor_scalar(SP[u], SP[u], EXP_MAX, None, ALU.min).then_inc(s_min, 1)
                        dve.wait_ge(s_ln, due(h + 1, base))
                        nc.vector.scalar_tensor_tensor(SP[u], pre, b1c, SP[u], ALU.add, ALU.max)\
                          .then_inc(s_sp, 1)
                return step
            chunk_steps(dve, edges1(0, 0, False), 4)
            dve.drain().then_inc(s_phase, 1)
            dve.wait_ge(s_phase, 20)
            many = dve.value_load(FLAG[0:1, 0:1], min_val=0, max_val=1)
            with dve.If(many > 0):
                with dve.Fori(1, NR) as r:
                    nc.vector.tensor_scalar(IOTA[:, :], IOTA[:, :], float(NS), None, ALU.add).then_inc(s_io, 1)
                    dve.wait_ge(s_io, r)
                    chunk_steps(dve, edges1(r * STEPS, (r * 2) * G, True), 4)
                    leave_round(dve, r)
            dve.drain().then_inc(s_phase, 1)
            dve.wait_ge(s_phase, 25)

            def nodes1(t, u):
                if active(t, G):
                    dve.wait_ge(s_p5[0], due(t + 1))
                    dve.wait_ge(s_p5[5], due(t - 1))
                    nc.vector.tensor_scalar(TB[u], bank(u), bd1c, SOFT_MAX, ALU.add, ALU.min).then_inc(s_p5[1], 1)
                h = t - 1
                if active(h, G):
                    v = 1 - u
                    dve.wait_ge(s_p5[3], due(h + 1))
                    nc.vector.scalar_tensor_tensor(TB[v], bank(v), bd1c, TB[v], ALU.add, ALU.max)\
                      .then_inc(s_p5[4], 1)
                e = t - 2
                if active(e, G):
                    dve.wait_ge(s_p5[5], due(e + 1))
                    dve.wait_ge(s_p5[7], due(e + 1))
                    nc.vector.tensor_tensor(X[:, gsl(e)], bank(2 + u), XB[u], ALU.add).then_inc(s_p5[6], 1)
            group_steps(dve, nodes1, 2)
            dve.drain().then_inc(s_phase, 1)
            dve.wait_ge(s_phase, 30)

            def norm2(t, u):
                if active(t, G):
                    ln_stats(2, t, u)
                if active(t - 1, G):
                    ln_shift(2, t - 1)
                h = t - 4
                if active(h, G):
                    dve.wait_ge(s_p6[4], due(h + 1))
                    dve.wait_ge(s_p6[6], due(h - 1))
                    nc.vector.tensor_scalar(UB[u], bank(4 + u), 0.0, None, ALU.max).then_inc(s_p6[5], 1)
            group_steps(dve, norm2, 4)
            dve.drain().then_inc(s_phase, 1)
            dve.wait_ge(s_phase, 35)

            def gates(t, u):
                h = t - 1
                if active(t, G):
                    dve.wait_ge(s_p8[2], due(t + 1))
                    dve.wait_ge(s_p8[1], due(t + 1))
                    dve.wait_ge(s_p8[5], due(t - 1))
                    nc.vector.scalar_tensor_tensor(VB[u], bank(3), bhn, RZ[u][:, 0:GC], ALU.add, ALU.mult)\
                      .then_inc(s_p8[3], 1)
                    dve.wait_ge(s_p8[3], due(t + 1))
                    nc.vector.tensor_tensor(VB[u], VB[u], bank(2), ALU.add).then_inc(s_p8[4], 1)
                if active(h, G):
                    dve.wait_ge(s_p8[9], due(h + 1))
                    nc.vector.tensor_tensor(X[:, gsl(h)], bank(4 + (1 - u)), X[:, gsl(h)], ALU.add)\
                      .then_inc(s_p8[10], 1)
            group_steps(dve, gates, 1)
            dve.drain().then_inc(s_phase, 1)
            dve.wait_ge(s_phase, 40)

            def norm3(t, u):
                if active(t, G):
                    ln_stats(3, t, u)
                if active(t - 1, G):
                    ln_shift(3, t - 1)
                h = t - 3
                if active(h, G):
                    dve.wait_ge(s_p9[2], due(h + 1))
                    pq = bank(4 if u else 6, 2).rearrange("p (b w n) -> p b w n", b=GB, w=2)
                    nc.vector.tensor_tensor(by4(Y[:, gsl(h)]), pq[:, :, 0, :],
                                            ROWB[:, 2:3, :].to_broadcast([128, GB, 128]), ALU.add)\
                      .then_inc(s_p9[3], 1)
            group_steps(dve, norm3, 3)
            dve.drain().then_inc(s_phase, 1)
            dve.wait_ge(s_phase, 45)

            many = dve.value_load(FLAG[0:1, 0:1], min_val=0, max_val=1)
            with dve.If(many > 0):
                for n in ("act", "acs", "z", "acc"):
                    dve.sem_inc(s_gl[n], 1)
                nc.vector.memset(SHV[:, :], -float(NS) * (NR - 1)).then_inc(s_gl["sh"], 1)
                nc.vector.tensor_scalar(IOTA[:, :], IOTA[:, :], -float(NS) * (NR - 1), None, ALU.add)\
                  .then_inc(s_gl["sh"], 1)
                with dve.Fori(0, B) as b:
                    dve.wait_ge(s_gl["sh"], due(b * (2 * NR + 1) + 2))
                    nc.vector.tensor_scalar(SHV[:, :], SHV[:, :], float(NS) * NR, None, ALU.add)\
                      .then_inc(s_gl["sh"], 1)
                    y2 = YR[:, :, gsl(b, 128)]
                    dve.wait_ge(s_gl["z"], due(b * (NR * BPG) + 1))
                    nc.vector.tensor_copy(PARTS[0][:, 0], y2).then_inc(s_gl["c1"], 1)
                    dve.wait_ge(s_gl["c1"], due(b + 1))
                    nc.vector.tensor_tensor(REM[0], y2, PARTS[0][:, 0], ALU.subtract).then_inc(s_gl["r1"], 1)
                    dve.wait_ge(s_gl["r1"], due(b + 1))
                    nc.vector.tensor_copy(PARTS[0][:, 1], REM[0]).then_inc(s_gl["c2"], 1)
                    dve.wait_ge(s_gl["c2"], due(b + 1))
                    nc.vector.tensor_tensor(PARTS[0][:, 2], REM[0], PARTS[0][:, 1], ALU.subtract)\
                      .then_inc(s_gl["c3"], 1)
                    nc.vector.memset(ACC[0], 0.0).then_inc(s_gl["fold"], 1)
                    with dve.Fori(0, NR) as r:
                        n = b * NR + r
                        dve.wait_ge(s_gl["sh"], due(b * (2 * NR + 1) + r * 2 + 3))
                        nc.vector.tensor_scalar(SHV[:, :], SHV[:, :], -float(NS), None, ALU.add)\
                          .then_inc(s_gl["sh"], 1)
                        dve.wait_ge(s_gl["sh"], due(b * (2 * NR + 1) + r * 2 + 4))
                        nc.vector.tensor_scalar(SHR[:, :], RANK[:, gsl(b, N)], SHV[:, 0:1], None, ALU.add)\
                          .then_inc(s_gl["sh"], 1)
                        dve.wait_ge(s_gl["sh"], due(b * (2 * NR + 1) + r * 2 + 5))
                        dve.wait_ge(s_gl["z"], due(n * BPG + 1))
                        nc.vector.tensor_tensor(
                            OH3[0], SHR[:, :].rearrange("p (a i) -> p a i", a=1).to_broadcast([128, NS, N]),
                            IOTA[:, 0:NS * N].rearrange("p (s i) -> p s i", i=N), ALU.is_equal)\
                          .then_inc(s_gl["oh"], 1)
                        dve.wait_ge(s_gl["act"], due(n + 2))
                        dve.wait_ge(s_gl["acc"], due(n * BPG + 1))
                        nc.vector.tensor_scalar(AC[0], bank(6)[:, 0:NS], 0.0, None, ALU.max)\
                          .then_inc(s_gl["acs"], 1)
                        dve.wait_ge(s_gl["acs"], due(n + 2))
                        dve.wait_ge(s_gl["fold"], due(b * 3 + 1))
                        for kb in range(BPG):
                            dve.wait_ge(s_gl["z"], due(n * BPG + kb + 2))
                            dve.wait_ge(s_gl["acc"], due(n * BPG + kb + 1))
                            for q in range(4):
                                s = kb * 4 + q
                                last = nc.vector.scalar_tensor_tensor(
                                    ACC[0][:, q, :], bank(kb % 2)[:, q * D:(q + 1) * D], AC[0][:, s:s + 1],
                                    ACC[0][:, q, :], ALU.mult, ALU.max)
                            last.then_inc(s_gl["acc"], 1)
                    dve.wait_ge(s_gl["acc"], due((b + 1) * (NR * BPG) + 1))
                    nc.vector.tensor_tensor(ACC[0][:, 0:2, :], ACC[0][:, 0:2, :], ACC[0][:, 2:4, :], ALU.max)\
                      .then_inc(s_gl["fold"], 1)
                    dve.wait_ge(s_gl["fold"], due(b * 3 + 2))
                    nc.vector.tensor_tensor(ACC[0][:, 0, :], ACC[0][:, 0, :], ACC[0][:, 1, :], ALU.max)\
                      .then_inc(s_gl["fold"], 1)
                    dve.wait_ge(s_gl["fold"], due(b * 3 + 3))
                    nc.vector.tensor_tensor(X[:, gsl(b, D)], X[:, gsl(b, D)], ACC[0][:, 0, :], ALU.add)\
                      .then_inc(s_gl["x"], 1)
            with dve.Else():
                def edges3(t, u):
                    if active(t, B):
                        dve.wait_ge(s_l3["z"], due((t - 1) * BPG))
                        nc.vector.tensor_tensor(OH3[u], spread_rank(t), IOTA[:, 0:NS * N]
                                                .rearrange("p (s i) -> p s i", i=N), ALU.is_equal)\
                          .then_inc(s_l3["oh"], 1)
                        dve.wait_ge(s_l3["act"], due(t + 1))
                        dve.wait_ge(s_l3r, due((t - 1) * (BPG - 1)))
                        nc.vector.tensor_scalar(AC[u], bank(6 + u)[:, 0:NS], 0.0, None, ALU.max)\
                          .then_inc(s_l3["ac"], 1)
                    h = t - 1
                    if active(h, B):
                        v = 1 - u
                        a, msg = ACC[v], MSG[v]
                        for kb in range(1, BPG - 1):
                            dve.wait_ge(s_l3r, due(h * (BPG - 1) + kb + 1))
                            if kb > 1:
                                dve.wait_ge(s_l3["acc"], due(h * (BPG - 1) + kb - 1))
                            nc.vector.tensor_tensor(a, msg[0] if kb == 1 else a, msg[kb], ALU.max)\
                              .then_inc(s_l3["acc"], 1)
                        dve.wait_ge(s_l3["z"], due(h * BPG + BPG))
                        dve.wait_ge(s_l3["acc"], due(h * (BPG - 1) + BPG - 2))
                        for q in range(4):
                            s = (BPG - 1) * 4 + q
                            last = nc.vector.scalar_tensor_tensor(
                                a[:, q, :], bank(BPG - 1)[:, q * D:(q + 1) * D], AC[v][:, s:s + 1], a[:, q, :],
                                ALU.mult, ALU.max)
                        last.then_inc(s_l3["acc"], 1)
                        dve.wait_ge(s_l3["acc"], due((h + 1) * (BPG - 1)))
                        nc.vector.tensor_tensor(a[:, 0:2, :], a[:, 0:2, :], a[:, 2:4, :], ALU.max)\
                          .then_inc(s_l3["fold"], 1)
                        dve.wait_ge(s_l3["fold"], due(h * 2 + 1))
                        nc.vector.tensor_tensor(a[:, 0, :], a[:, 0, :], a[:, 1, :], ALU.max)\
                          .then_inc(s_l3["fold"], 1)
                        dve.wait_ge(s_l3["fold"], due(h * 2 + 2))
                        nc.vector.tensor_tensor(X[:, gsl(h, D)], X[:, gsl(h, D)], a[:, 0, :], ALU.add)\
                          .then_inc(s_l3["x"], 1)
                graph_steps(dve, edges3, 1)
            dve.drain().then_inc(s_phase, 1)
            dve.wait_ge(s_phase, 50)

        @block.scalar
        def _(act):
            nc.scalar.preload_act_table_set("natural_log_exp_and_others")
            natural = [io["L1_gnn_Wa"], None, io["L1_gnn_W2"], io["L1_gnn_Wd1"], io["L1_gnn_Wd2"],
                       io["L2_gnn_W1"], io["L2_gnn_W2"]]
            for k, w in enumerate(natural):
                if w is not None:
                    act.dma_start(NATW[:, k, :], w).then_inc(s_w, 16)
            for h in range(2):
                act.dma_start(NATW[:, W1, h * NG:(h + 1) * NG], io["L1_gnn_W1"]).then_inc(s_w, 16)
            for n, at in (("L2_gnn_W_ih", IH), ("L2_gnn_W_hh", HH)):
                act.dma_start(NATW[:, at:at + 3, :], io[n].rearrange("(c p) d -> p c d", p=128)).then_inc(s_w, 16)
            act.dma_start(W0[:, :], io["L0_gnn_W"]).then_inc(s_w, 16)
            act.dma_start(W3N[:, :, :], io["L3_gnn_W"].rearrange("(c p) d -> p c d", p=128)).then_inc(s_w, 16)
            for k, n in enumerate(("L0_gnn_b", "L1_gnn_bd2", "L3_gnn_b", "L2_gnn_b2")):
                act.dma_start(ROWN[0:1, k * 128:(k + 1) * 128],
                             io[n].rearrange("(a n) -> a n", a=1)).then_inc(s_w, 16)
            for k, n in enumerate(("L1_gnn_b1", "L1_gnn_b2", "L1_gnn_bd1", "L2_gnn_b1")):
                act.dma_start(COLB[:, k:k + 1], io[n].rearrange("(p a) -> p a", a=1)).then_inc(s_w, 16)
            for k in range(3):
                for n, at in (("L2_gnn_b_ih", 4), ("L2_gnn_b_hh", 7)):
                    act.dma_start(COLB[:, at + k:at + k + 1],
                                 io[n][k * 128:(k + 1) * 128].rearrange("(p a) -> p a", a=1)).then_inc(s_w, 16)

            for k in range(4):
                act.dma_start(X[:, k * 4 * GC:(k + 1) * 4 * GC].rearrange("p (b n) -> p b n", n=D),
                              io["x"][k * 4 * GB:(k + 1) * 4 * GB].rearrange("b n d -> n b d")).then_inc(s_x, 16)

            def store_at(t, u):
                if active(t, G):
                    act.wait_ge(s_tp, due(t + 1))
                    nc.scalar.copy(AT[:, gsl(t)], bank(u)).then_inc(s_at, 1)
            group_steps(act, store_at, 0)
            for k in range(0, NW, GB):
                n = min(GB, NW - k)
                act.wait_ge(s_wt, k // GB + 1)
                nc.scalar.copy(WT[:, k:k + n, :], bank(4 + k // GB)[:, 0:n * 128]
                               .rearrange("p (w n) -> p w n", w=n)).then_inc(s_wtc, 1)
            act.wait_ge(s_rowb, 1)
            nc.scalar.copy(ROWB[:, :, :], bank(0).rearrange("p (w n) -> p w n", w=4)).then_inc(s_wtc, 1)

            act.drain().then_inc(s_phase, 1)
            act.wait_ge(s_phase, 5)

            def ln_apply(layer, t, u, free_sem, per):
                act.wait_ge(s_hu, due(t + 1, layer * G))
                act.wait_ge(free_sem, due((t - 1) * per))
                for q in range(GB):
                    last = nc.scalar.activation(
                        HB[u][:, q * D:(q + 1) * D], X[:, bass.ds(t * GC + q * D, D)], ACT.Relu,
                        bias=LNB[:, bass.ds(t * GB + q, 1)], scale=LNS[:, bass.ds(t * GB + q, 1)])
                last.then_inc(s_h, 1)

            def layer0(t, u):
                if active(t - 1, G):
                    ln_apply(0, t - 1, 1 - u, s_p2[0], 1)
                h = t - 2
                if active(h, G):
                    act.wait_ge(s_p2[0], due(h + 1))
                    act.wait_ge(s_p2[2], due(h - 1))
                    nc.scalar.copy(TB[u], bank(u)).then_inc(s_p2[1], 1)
            group_steps(act, layer0, 2)
            act.drain().then_inc(s_phase, 1)
            act.wait_ge(s_phase, 10)

            def into1(t, u):
                if active(t - 1, G):
                    ln_apply(1, t - 1, 1 - u, s_p3[0], 1)
                h = t - 2
                if active(h, G):
                    act.wait_ge(s_p3[0], due(h + 1))
                    act.wait_ge(s_p3[2], due(h - 1))
                    nc.scalar.copy(TB[u], bank(u)).then_inc(s_p3[1], 1)
                e = t - 3
                if active(e, G):
                    act.wait_ge(s_p3[2], due(e + 1))
                    nc.scalar.copy(R[:, gsl(e)], bank(2 + (1 - u))).then_inc(s_p3[3], 1)
            group_steps(act, into1, 3)
            act.drain().then_inc(s_phase, 1)
            act.wait_ge(s_phase, 15)

            def edges1(base):
                def step(m, k, t):
                    h = t - 1
                    if active(h, STEPS):
                        u = (k - 1) % 2
                        act.wait_ge(s_z, due(h + 1, base))
                        act.wait_ge(s_acd, due(h * 16, base * 16))
                        nc.scalar.copy(ZC, bank(0)).then_inc(s_zc, 1)
                        act.wait_ge(s_pre, due(h - 1, base))
                        nc.scalar.activation(GA[u], bank(0), ACT.Square, bias=offc).then_inc(s_sq, 1)
                        act.wait_ge(s_sq, due(h + 1, base))
                        nc.scalar.activation(GA[u], GA[u], ACT.Exp, scale=COEFF).then_inc(s_g, 1)
                    e = t - 2
                    if active(e, STEPS):
                        v = k % 2
                        act.wait_ge(s_hm, due(e - 1, base))
                        act.wait_ge(s_gp2, due(2 * e + 1, base * 2))
                        nc.scalar.copy(GS[v][:, 0:HC], bank(1)).then_inc(s_gc, 1)
                        act.wait_ge(s_pre, due(e + 1, base))
                        act.wait_ge(s_wf, due(e - 1, base))
                        nc.scalar.activation(SP[v], bank(2 if v == 0 else 6, 2), ACT.Exp, bias=b1c).then_inc(s_ex, 1)
                        act.wait_ge(s_min, due(e + 1, base))
                        nc.scalar.activation(SP[v], SP[v], ACT.Ln, bias=1.0).then_inc(s_ln, 1)
                        act.wait_ge(s_gp2, due(2 * e + 2, base * 2))
                        nc.scalar.copy(GS[v][:, HC:CC], bank(1)).then_inc(s_gc, 1)
                return step
            chunk_steps(act, edges1(0), 3)
            act.drain().then_inc(s_phase, 1)
            act.wait_ge(s_phase, 20)
            general_rounds(act, lambda r: chunk_steps(act, edges1(r * STEPS), 3))
            act.drain().then_inc(s_phase, 1)
            act.wait_ge(s_phase, 25)

            def nodes1(t, u):
                if active(t, G):
                    act.wait_ge(s_p5[1], due(t + 1))
                    nc.scalar.activation(TB[u], TB[u], ACT.Exp).then_inc(s_p5[2], 1)
                    act.wait_ge(s_p5[2], due(t + 1))
                    nc.scalar.activation(TB[u], TB[u], ACT.Ln, bias=1.0).then_inc(s_p5[3], 1)
            group_steps(act, nodes1, 0)
            act.drain().then_inc(s_phase, 1)
            act.wait_ge(s_phase, 30)

            def messages(t, u):
                v = 1 - u
                if active(t - 1, G):
                    ln_apply(2, t - 1, v, s_p6[0], 1)
                h = t - 2
                if active(h, G):
                    act.wait_ge(s_p6[0], due(h + 1))
                    nc.scalar.copy(R[:, gsl(h)], bank(u)).then_inc(s_p6[1], 1)
                h = t - 3
                if active(h, G):
                    act.wait_ge(s_p6[2], due(h + 1))
                    act.wait_ge(s_p6[4], due(h - 1))
                    nc.scalar.activation(TB[v], bank(2 + v), ACT.Relu, bias=m1c).then_inc(s_p6[3], 1)
                h = t - 5
                if active(h, G):
                    act.wait_ge(s_p6[6], due(h + 1))
                    nc.scalar.activation(Y[:, gsl(h)], bank(6 + v), ACT.Relu).then_inc(s_p6[7], 1)
            group_steps(act, messages, 5, head=8)
            act.drain().then_inc(s_phase, 1)
            act.wait_ge(s_phase, 35)

            def gates(t, u):
                if active(t, G):
                    act.wait_ge(s_p8[0], due(t + 1))
                    act.wait_ge(s_p8[8], due(t - 1))
                    for k in range(2):
                        last = nc.scalar.activation(RZ[u][:, k * GC:(k + 1) * GC], bank(k), ACT.Sigmoid,
                                                    bias=brz[:, k:k + 1])
                    last.then_inc(s_p8[2], 1)
                    act.wait_ge(s_p8[4], due(t + 1))
                    nc.scalar.activation(NB_[u], VB[u], ACT.Tanh, bias=bin_).then_inc(s_p8[5], 1)
            group_steps(act, gates, 0)
            act.drain().then_inc(s_phase, 1)
            act.wait_ge(s_phase, 40)

            def into3(t, u):
                if active(t - 1, G):
                    ln_apply(3, t - 1, 1 - u, s_p9[0], 1)
                h = t - 2
                if active(h, G):
                    act.wait_ge(s_p9[0], due(h + 1))
                    act.wait_ge(s_p9[2], due(h - 1))
                    nc.scalar.copy(TB[u], bank(u)).then_inc(s_p9[1], 1)
                h = t - 3
                if active(h, G):
                    act.wait_ge(s_p9[3], due(h + 1))
                    pq = bank(4 if u else 6, 2).rearrange("p (b w n) -> p b w n", b=GB, w=2)
                    nc.scalar.copy(by4(R[:, gsl(h)]), pq[:, :, 1, :]).then_inc(s_p9[4], 1)
            group_steps(act, into3, 3)
            act.drain().then_inc(s_phase, 1)
            act.wait_ge(s_phase, 45)

            many = act.value_load(FLAG[0:1, 0:1], min_val=0, max_val=1)
            with act.If(many > 0):
                act.nop()
            with act.Else():
                def edges3(t, u):
                    if active(t, B):
                        act.wait_ge(s_l3["z"], due((t - 1) * BPG))
                        nc.scalar.copy(PARTS[u][:, 0], YR[:, :, gsl(t, 128)]).then_inc(s_l3["c1"], 1)
                    h = t - 1
                    for kb in range(BPG - 1):
                        if active(h, B):
                            v = 1 - u
                            act.wait_ge(s_l3["ac"], due(h + 1))
                            act.wait_ge(s_l3["z"], due(h * BPG + kb + 1))
                            act.wait_ge(s_l3["acc"], due((h - 1) * (BPG - 1)))
                            for q in range(4):
                                s = kb * 4 + q
                                last = nc.scalar.activation(MSG[v][kb][:, q, :], bank(kb)[:, q * D:(q + 1) * D],
                                                            ACT.Relu, scale=AC[v][:, s:s + 1])
                            last.then_inc(s_l3r, 1)
                        if kb == 1 and active(t, B):
                            act.wait_ge(s_l3["r1"], due(t + 1))
                            nc.scalar.copy(PARTS[u][:, 1], REM[u]).then_inc(s_l3["c2"], 1)
                graph_steps(act, edges3, 1)
            act.drain().then_inc(s_phase, 1)
            act.wait_ge(s_phase, 50)

        @block.tensor
        def _(pe):
            mm = nc.tensor.matmul
            pe.wait_ge(s_gp, 16)
            def ranks(t, u):
                if active(t, G):
                    pe.wait_ge(s_adj[u], (t - u) * 8 + 16)
                    pe.wait_ge(s_at, due(t - 1))
                    for q in range(GB):
                        last = nc.tensor.transpose(bank(u)[:, q * N:(q + 1) * N], ADJ[u][:, q * N:(q + 1) * N],
                                                   ident[:, :])
                    last.then_inc(s_tp, 1)
                h = t - 1
                if active(h, G):
                    v = 1 - u
                    pe.wait_ge(s_mask, due(h * 2 + 1))
                    pe.wait_ge(s_rks, due((h - 1) * 2))
                    mm(bank(2 + v), upto[:, :], MASK[v], start=True, stop=True).then_inc(s_rank, 1)
            group_steps(pe, ranks, 1)
            pe.wait_ge(s_w, 16 * LOADS)
            for k in range(0, NW, GB):
                for q in range(k, min(k + GB, NW)):
                    last = nc.tensor.transpose(bank(4 + k // GB)[:, (q - k) * 128:(q - k + 1) * 128],
                                               NATW[:, q, :], ident[:, :])
                last.then_inc(s_wt, 1)
            pe.wait_ge(s_at, G)
            pe.wait_ge(s_wtc, 2)
            pe.wait_ge(s_prep, 1)
            mm(bank(0), ONE[0:1, :], ROWN[0:1, :], start=True, stop=True, skip_group_check=True)
            mm(bank(0)[:, 128:256], MLN2, WT[:, WD2, :], start=False, stop=True, skip_group_check=True)\
                .then_inc(s_rowb, 1)
            pe.drain().then_inc(s_phase, 1)
            pe.wait_ge(s_phase, 5)

            def layer0(t, u):
                h = t - 2
                if active(h, G):
                    pe.wait_ge(s_h, due(h + 1))
                    pe.wait_ge(s_p2[1], due(h - 1))
                    for q in range(GB):
                        last = mm(bank(u)[:, q * N:(q + 1) * N], HB[u][:, q * D:(q + 1) * D],
                                  AT[:, bass.ds(h * GC + q * N, N)], start=(q == 0), stop=True, skip_group_check=True)
                    last.then_inc(s_p2[0], 1)
                e = t - 3
                if active(e, G):
                    v = 1 - u
                    pe.wait_ge(s_p2[1], due(e + 1))
                    pe.wait_ge(s_p2[3], due(e - 1))
                    for q in range(GB):
                        last = mm(bank(2 + v)[:, q * D:(q + 1) * D], TB[v][:, q * N:(q + 1) * N], W0[:, :],
                                  start=(q == 0), stop=True, skip_group_check=True)
                    last.then_inc(s_p2[2], 1)
            group_steps(pe, layer0, 3)
            pe.drain().then_inc(s_phase, 1)
            pe.wait_ge(s_phase, 10)

            def transpose_h(v, out, ready, count):
                for q in range(GB):
                    last = nc.tensor.transpose(out[:, q * N:(q + 1) * N], HB[v][:, q * D:(q + 1) * D], ident[:, :])
                last.then_inc(ready, 1)

            def into1(t, u):
                h = t - 2
                if active(h, G):
                    pe.wait_ge(s_h, due(h + 1, G))
                    pe.wait_ge(s_p3[1], due(h - 1))
                    transpose_h(u, bank(u), s_p3[0], 1)
                e = t - 3
                if active(e, G):
                    v = 1 - u
                    pe.wait_ge(s_p3[1], due(e + 1))
                    pe.wait_ge(s_p3[3], due(e - 1))
                    for q in range(GB):
                        last = mm(bank(2 + v)[:, q * D:(q + 1) * D], TB[v][:, q * N:(q + 1) * N], WT[:, WA, :],
                                  start=(q == 0), stop=True, skip_group_check=True)
                    last.then_inc(s_p3[2], 1)
            group_steps(pe, into1, 3)
            pe.drain().then_inc(s_phase, 1)
            pe.wait_ge(s_phase, 15)

            def edges1(base, rbase):
                def step(m, k, t):
                    h = t - 1
                    if active(h, STEPS):
                        u = (k - 1) % 2
                        pe.wait_ge(s_pa, due(h + 1, base))
                        pe.wait_ge(s_sq, due(h, base))
                        mm(PS[0:NG, 0:512], ones[:, :], PA[u][:, 0:HC], start=True, stop=True)
                        mm(PS[NG:128, 0:512], ones[:, :], PA[u][:, HC:CC], start=True, stop=True).then_inc(s_z, 1)
                    e = t - 2
                    if active(e, STEPS):
                        v = k % 2
                        ek = (k - 2) % UNROLL
                        b, slot, split = place(m if k >= 2 else m - 1, ek)
                        gq = 2 * ek // BPG

                        def gather(q):
                            nb, nq = (b + 1, gq + 1) if split and q else (b, gq)
                            if (slot == 0 and q == 0) or (split and q):
                                pe.wait_ge(s_rf, due(nb + 1, rbase))
                            pe.wait_ge(s_gc, due(2 * e + q, base * 2))
                            mm(bank(1), RF[nq % 2], PA2[v][:, q * HC:(q + 1) * HC], start=True, stop=True)\
                                .then_inc(s_gp2, 1)
                        pe.wait_ge(s_pa2, due(e + 1, base))
                        gather(0)
                        pe.wait_ge(s_g, due(e + 1, base))
                        pe.wait_ge(s_sp, due(e - 1, base))
                        for q in range(2):
                            last = mm(bank((2 if v == 0 else 6) + q), WT[q * NG:(q + 1) * NG, W1, :],
                                      GA[v][q * NG:(q + 1) * NG, :], start=True, stop=True)
                        last.then_inc(s_pre, 1)
                    f = t - 3

                    def filters(q):
                        return mm(bank(4 + q), WT[:, W2, :], SP[(k - 3) % 2][:, q * HC:(q + 1) * HC],
                                  start=True, stop=True)
                    if active(f, STEPS):
                        pe.wait_ge(s_sp, due(f + 1, base))
                        pe.wait_ge(s_hm, due(f, base))
                        filters(0)
                    if active(e, STEPS):
                        gather(1)
                    if active(f, STEPS):
                        filters(1).then_inc(s_wf, 1)
                return step
            chunk_steps(pe, edges1(0, 0), 3)
            pe.drain().then_inc(s_phase, 1)
            pe.wait_ge(s_phase, 20)
            general_rounds(pe, lambda r: chunk_steps(pe, edges1(r * STEPS, r * B), 3))
            pe.drain().then_inc(s_phase, 1)
            pe.wait_ge(s_phase, 25)

            def nodes1(t, u):
                if active(t, G):
                    pe.wait_ge(s_p5[4], due(t - 1))
                    mm(bank(u), WT[:, WD1, :], Y[:, gsl(t)], start=True, stop=True).then_inc(s_p5[0], 1)
                h = t - 2
                if active(h, G):
                    pe.wait_ge(s_p5[4], due(h + 1))
                    pe.wait_ge(s_p5[6], due(h - 1))
                    for q in range(GB):
                        last = mm(bank(2 + u)[:, q * D:(q + 1) * D], TB[u][:, q * N:(q + 1) * N], WT[:, WD2, :],
                                  start=(q == 0), stop=True, skip_group_check=True)
                    last.then_inc(s_p5[5], 1)
            group_steps(pe, nodes1, 2)
            pe.drain().then_inc(s_phase, 1)
            pe.wait_ge(s_phase, 30)

            def messages(t, u):
                v = 1 - u
                h = t - 2
                if active(h, G):
                    pe.wait_ge(s_h, due(h + 1, 2 * G))
                    pe.wait_ge(s_p6[1], due(h - 1))
                    transpose_h(u, bank(u), s_p6[0], 1)
                h = t - 3
                if active(h, G):
                    pe.wait_ge(s_p6[1], due(h + 1))
                    pe.wait_ge(s_p6[3], due(h - 1))
                    mm(bank(2 + v), WT[:, M1, :], R[:, gsl(h)], start=True, stop=True).then_inc(s_p6[2], 1)
                h = t - 4
                if active(h, G):
                    pe.wait_ge(s_p6[3], due(h + 1))
                    pe.wait_ge(s_p6[5], due(h - 1))
                    for q in range(GB):
                        mm(bank(4 + u)[:, q * D:(q + 1) * D], TB[u][:, q * N:(q + 1) * N], WT[:, M2, :],
                           start=(q == 0), stop=True, skip_group_check=True)
                    mm(bank(4 + u), ONE[0:1, :], ROWB[0:1, 3:4, :].to_broadcast([1, GB, 128]), start=False, stop=True,
                       skip_group_check=True).then_inc(s_p6[4], 1)
                h = t - 5
                if active(h, G):
                    pe.wait_ge(s_p6[5], due(h + 1))
                    pe.wait_ge(s_p6[7], due(h - 1))
                    for q in range(GB):
                        last = mm(bank(6 + v)[:, q * N:(q + 1) * N], UB[v][:, q * D:(q + 1) * D],
                                  AT[:, bass.ds(h * GC + q * N, N)], start=(q == 0), stop=True, skip_group_check=True)
                    last.then_inc(s_p6[6], 1)
            group_steps(pe, messages, 5, head=8)
            pe.drain().then_inc(s_phase, 1)
            pe.wait_ge(s_phase, 35)

            def gates(t, u):
                if active(t, G):
                    msg, ht = Y[:, gsl(t)], R[:, gsl(t)]
                    pe.wait_ge(s_p8[2], due(t))
                    for k in range(2):
                        mm(bank(k), WT[:, IH + k, :], msg, start=True, stop=False)
                        last = mm(bank(k), WT[:, HH + k, :], ht, start=False, stop=True)
                    last.then_inc(s_p8[0], 1)
                    pe.wait_ge(s_p8[4], due(t))
                    mm(bank(2), WT[:, IH + 2, :], msg, start=True, stop=True)
                    mm(bank(3), WT[:, HH + 2, :], ht, start=True, stop=True).then_inc(s_p8[1], 1)
                h = t - 1
                if active(h, G):
                    v = 1 - u
                    pe.wait_ge(s_p8[8], due(h + 1))
                    pe.wait_ge(s_p8[10], due(h - 1))
                    for q in range(GB):
                        last = nc.tensor.transpose(bank(4 + v)[:, q * N:(q + 1) * N],
                                                   UB[v][:, q * D:(q + 1) * D], ident[:, :])
                    last.then_inc(s_p8[9], 1)
            group_steps(pe, gates, 1)
            pe.drain().then_inc(s_phase, 1)
            pe.wait_ge(s_phase, 40)

            def into3(t, u):
                h = t - 2
                if active(h, G):
                    pe.wait_ge(s_h, due(h + 1, 3 * G))
                    pe.wait_ge(s_p9[1], due(h - 1))
                    transpose_h(u, bank(u), s_p9[0], 1)
                h = t - 3
                if active(h, G):
                    v = 1 - u
                    pe.wait_ge(s_p9[1], due(h + 1))
                    pe.wait_ge(s_p9[4], due(h - 1))
                    pq = bank(6 if v else 4, 2)
                    for q in range(GB):
                        last = mm(pq[:, q * 256:(q + 1) * 256], TB[v][:, q * N:(q + 1) * N], W3[:, :, :],
                                  start=(q % 2 == 0), stop=True, skip_group_check=True)
                    last.then_inc(s_p9[2], 1)
            group_steps(pe, into3, 3)
            pe.drain().then_inc(s_phase, 1)
            pe.wait_ge(s_phase, 45)

            def slots(parts, oh, zb, kb):
                for k in range(3):
                    mm(zb, identb[:, :], parts[:, k, 0:1, :].to_broadcast([128, 4, D]), start=(k == 0), stop=True,
                       skip_group_check=True)
                for q in range(4):
                    for k in range(3):
                        last = mm(zb[:, q * D:(q + 1) * D], oh[:, kb * 4 + q, :], parts[:, k, 1, :],
                                  start=False, stop=True, skip_group_check=True)
                return last

            many = pe.value_load(FLAG[0:1, 0:1], min_val=0, max_val=1)
            with pe.If(many > 0):
                with pe.Fori(0, B) as b:
                    with pe.Fori(0, NR) as r:
                        n = b * NR + r
                        pe.wait_ge(s_gl["ac"], due(n * 16 + 16))
                        pe.wait_ge(s_gl["acs"], due(n + 1))
                        pe.sem_inc(s_passed, 1)
                        nc.tensor.transpose(bank(6)[:, 0:NS], ACT_[0][0:NS, :], ident[0:NS, 0:NS])\
                            .then_inc(s_gl["act"], 1)
                        pe.wait_ge(s_gl["oh"], due(n + 1))
                        pe.wait_ge(s_gl["c3"], due(b + 1))
                        for kb in range(BPG):
                            pe.wait_ge(s_gl["acc"], due(n * BPG + max(kb - 1, 0) + 1))
                            slots(PARTS[0], OH3[0], bank(kb % 2), kb).then_inc(s_gl["z"], 1)
            with pe.Else():
                def edges3(t, u):
                    if active(t, B):
                        pe.wait_ge(s_l3[f"ac{u}"], (t - u) * 8 + 16)
                        pe.wait_ge(s_l3["ac"], due(t - 1))
                        pe.sem_inc(s_passed, 1)
                        nc.tensor.transpose(bank(6 + u)[:, 0:NS], ACT_[u][0:NS, :], ident[0:NS, 0:NS])\
                            .then_inc(s_l3["act"], 1)
                    h = t - 1
                    if active(h, B):
                        v = 1 - u
                        pe.wait_ge(s_l3["oh"], due(h + 1))
                        pe.wait_ge(s_l3["c3"], due(h + 1))
                        for kb in range(BPG):
                            if kb < BPG - 1:
                                pe.wait_ge(s_l3r, due((h - 1) * (BPG - 1) + kb + 1))
                            else:
                                pe.wait_ge(s_l3["acc"], due(h * (BPG - 1)))
                            slots(PARTS[v], OH3[v], bank(kb), kb).then_inc(s_l3["z"], 1)
                graph_steps(pe, edges3, 1)
            pe.drain().then_inc(s_phase, 1)
            pe.wait_ge(s_phase, 50)


_INS = ['x', 'adj', 'L0_gnn_W', 'L0_gnn_b', 'L1_gnn_W1', 'L1_gnn_b1', 'L1_gnn_W2', 'L1_gnn_b2', 'L1_gnn_Wa',
        'L1_gnn_Wd1', 'L1_gnn_bd1', 'L1_gnn_Wd2', 'L1_gnn_bd2', 'L2_gnn_W1', 'L2_gnn_b1', 'L2_gnn_W2',
        'L2_gnn_b2', 'L2_gnn_W_ih', 'L2_gnn_W_hh', 'L2_gnn_b_ih', 'L2_gnn_b_hh', 'L3_gnn_W', 'L3_gnn_b']


def kernel(**inputs):
    import concourse.bacc as bacc
    from concourse.bass_utils import run_bass_kernel_spmd

    nc = bacc.Bacc("TRN2", target_bir_lowering=False, num_devices=1, dynamic_dma_scratch_size=1024)
    arrays, io = {}, {}
    for name in _INS:
        a = np.ascontiguousarray(inputs[name])
        arrays[name + "_dram"] = a
        io[name] = nc.dram_tensor(name + "_dram", a.shape, mybir.dt.from_np(a.dtype), kind="ExternalInput").ap()
    io["out"] = nc.dram_tensor("out_dram", (B, N, D), F32, kind="ExternalOutput").ap()
    build(nc, io)
    r = run_bass_kernel_spmd(nc, [arrays], core_ids=[0])
    return r.results[0]["out_dram"]
```

```python
from contextlib import ExitStack

import numpy as np

import concourse.bass as bass
from concourse import mybir

F32 = mybir.dt.float32
BF16 = mybir.dt.bfloat16
I32 = mybir.dt.int32
ALU = mybir.AluOpType
ACT = mybir.ActivationFunctionType
AX = mybir.AxisListType

B, N, D = 64, 128, 128
NG = 64
GB = 4
G = B // GB
GC = GB * D
NS = 12
NS3 = 20
TOO_LONG = 256.0
LATE = NS3 - NS
NR = -(-N // NS)
BPG = NS // 4
BPG3 = NS3 // 4
CC = 2 * GC
HC = GC
UNROLL = GB * BPG // 2
STEPS = G * UNROLL
NO_SLOT = 200.0
CUTOFF = 5.0
WIDTH = np.float32(CUTOFF) / np.float32(NG - 1)
COEFF = float(np.float32(-0.5) / (WIDTH * WIDTH))
LN2 = float(np.log(2.0))
SOFT_MAX = 20.0
EXP_MAX = float(np.exp(SOFT_MAX))
LN_EPS = 1e-5
DEG_EPS = 1e-8
WA, W1, W2, WD1, WD2, M1, M2, IH, HH = 0, 1, 2, 3, 4, 5, 6, 7, 10
NW = 13
WORK_SIZE = 12900
LOADS = 26


def due(value, base=0):
    return 0 if isinstance(value, int) and value <= 0 else value + base


def active(h, n):
    return not isinstance(h, int) or 0 <= h < n


def group_steps(eng, body, depth, head=6):
    for t in range(head):
        body(t, t % 2)
    with eng.Fori(0, (G - head) // 2) as i:
        for u in range(2):
            body(i * 2 + (head + u), u)
    for t in range(G, G + depth):
        body(t, t % 2)


def chunk_steps(eng, step, depth):
    for k in range(UNROLL):
        step(0, k, k)
    with eng.Fori(1, G) as m:
        for k in range(UNROLL):
            step(m, k, m * UNROLL + k)
    for k in range(depth):
        step(G, k, STEPS + k)


def graph_steps(eng, body, depth):
    for t in range(4):
        body(t, t % 2)
    with eng.Fori(0, (B - 4) // 2) as i:
        for u in range(2):
            body(i * 2 + (4 + u), u)
    for t in range(B, B + depth):
        body(t, t % 2)


def ring_steps(eng, body, depth):
    for t in range(8):
        body(t, t % 2, t % 4)
    with eng.Fori(0, (G - 8) // 4) as i:
        for k in range(4):
            body(i * 4 + (8 + k), k % 2, k)
    for t in range(G, G + depth):
        body(t, t % 2, t % 4)


def place(m, k):
    j = 2 * k
    return m * GB + j // BPG, 4 * (j % BPG), j % BPG == BPG - 1


def carries():
    side = [None] * UNROLL
    for k in reversed(range(UNROLL)):
        _, slot, split = place(0, k)
        if slot or split:
            behind = side[k + 1] if k + 1 < UNROLL else None
            after_split = k > 0 and place(0, k - 1)[2]
            side[k] = 0 if split else 9 if behind == 0 or after_split else 0
    return side


CARRY = carries()


def build(nc, io):
    ctx = ExitStack()
    with ctx:
        def sb(name, shape, dt=F32):
            return ctx.enter_context(nc.sbuf_tensor(name, shape, dt))

        def sem(name):
            return ctx.enter_context(nc.semaphore(name))

        X = sb("X", [128, B * D])
        AT = sb("AT", [128, B * N])
        YR = sb("YR", [128, 2, B * N])
        Y, R = YR[:, 0, :], YR[:, 1, :]
        RANK = sb("RANK", [128, B * N], BF16)
        IOTA = sb("IOTA", [128, (NS + 4) * N], BF16)
        WT = sb("WT", [128, NW, 128])
        W0 = sb("W0", [128, 128])
        W3 = sb("W3", [128, 2, 128])
        ident = sb("ident", [128, 128])
        identb = sb("identb", [128, 128], BF16)
        upto = sb("upto", [128, 128], BF16)
        ones = sb("ones", [128, NG])
        onesb = sb("onesb", [128, 128], BF16)
        OV = sb("OV", [128, B])
        OVB = sb("OVB", [128, 2 * B], BF16)
        OFFE = sb("OFFE", [128, B])
        OFFI = sb("OFFI", [128, B])
        ACL = sb("ACL", [128, B * LATE])
        IOTAC = sb("IOTAC", [128, N])
        NEGC = sb("NEGC", [1, GC], BF16)
        CS = sb("CS", [128, LATE])
        B2R = sb("B2R", [128, N])
        ROWB = sb("ROWB", [128, 4, 128])
        COLB = sb("COLB", [128, 16])
        STAT = sb("STAT", [128, 3, B])
        STATB = sb("STATB", [128, 2, GB * 8 + 16])
        ONE = sb("ONE", [1, 128])
        MX = sb("MX", [1, 8])
        FLAG = sb("FLAG", [1, 8], I32)
        WORK = sb("WORK", [128, WORK_SIZE])
        PS = ctx.enter_context(nc.psum_tensor("PS", [128, 8 * 512], F32))
        acD = nc.dram_tensor("ac_slots", (NR * STEPS, 2, HC), F32, kind="Internal").ap()
        ac_rows = acD.rearrange("c h w -> (c h w)").rearrange("(g s i) -> g s i", s=NS, i=N)

        b1c, b2c, bd1c, m1c = (COLB[:, k:k + 1] for k in range(4))
        brz = COLB[:, 4:6]
        bin_, bhn = COLB[:, 6:7], COLB[:, 9:10]
        offc = COLB[:, 10:11]
        DEG, LNS, LNB = STAT[:, 0, :], STAT[:, 1, :], STAT[:, 2, :]

        def bank(k, n=1):
            return PS[:, k * 512:(k + n) * 512]

        class Carve:
            def __init__(self):
                self.at = 0

            def __call__(self, words, dt=F32):
                a = WORK[:, self.at:self.at + words]
                self.at += words
                assert self.at <= WORK_SIZE, self.at
                return a if dt == F32 else a.bitcast(dt)

        def gsl(t, k=GC):
            return bass.ds(t * k, k)

        def by4(ap):
            return ap.rearrange("p (b n) -> p b n", b=GB)

        s_passed = sem("wait_passed")
        s_phase = sem("phase")
        s_gen = sem("general_round")
        s_w = sem("weights_loaded")
        s_x = sem("x_loaded")
        s_gp = sem("gpsimd_constants")
        s_prep = sem("prep_dve")
        s_wt = sem("weights_transposed")
        s_wtc = sem("weights_copied")
        s_rowb = sem("row_biases_summed")
        s_adj = [sem(f"adj_loaded{k}") for k in range(4)]
        s_deg = sem("degrees_read")
        s_tp = sem("adj_transposed")
        s_at = sem("at_stored")
        s_mask = sem("mask_made")
        s_rank = sem("rank_counted")
        s_rks = sem("rank_stored")
        s_d0 = sem("degree_root")
        s_bn = sem("ln_stats")
        s_var = sem("ln_var")
        s_rs = sem("ln_scale")
        s_h = sem("h_ready")
        s_hu = sem("h_used")
        s_p2 = [sem(f"l0_{n}") for n in ("support", "support_copied", "out", "x", "xb")]
        s_p3 = [sem(f"l1in_{n}") for n in ("t", "tc", "rf", "rfc")]
        s_oh = sem("onehot_made")
        s_pa = sem("weighted_made")
        s_pa2 = sem("weighted2_made")
        s_rf = sem("rf_copied")
        s_z = sem("z_gathered")
        s_zc = sem("z_copied")
        s_sq = sem("square_made")
        s_g = sem("gauss_made")
        s_acd = sem("ac_saved")
        s_pre = sem("pre_made")
        s_min = sem("pre_capped")
        s_ex = sem("exp_made")
        s_ln = sem("log_made")
        s_sp = sem("softplus_made")
        s_gp2 = sem("gather_made")
        s_gc = sem("gather_copied")
        s_wf = sem("filter_made")
        s_hm = sem("message_made")
        s_red = sem("message_summed")
        s_fin = sem("first_graph_summed")
        s_ya = sem("general_added")
        s_io = sem("iota_moved")
        s_p5 = [sem(f"l1out_{n}") for n in ("t1", "cap", "exp", "log", "sp", "t2", "x", "xb")]
        s_p6 = [sem(f"l2m_{n}") for n in ("ht", "htc", "m1", "m1c", "m2", "m2c", "msg", "msgc", "m2b")]
        s_p8 = [sem(f"l2g_{n}") for n in ("rz", "n", "sig", "rh", "pre", "tanh", "dif", "zd", "new", "t", "x")]
        s_p9 = [sem(f"l3in_{n}") for n in ("t", "tc", "pq", "p", "q")]
        s_l3 = {n: sem(f"l3_{n}") for n in ("ac0", "ac1", "act", "ac", "oh", "c1", "r1", "c2", "c3",
                                            "z", "acc", "last", "fold", "x")}
        s_l3r = sem("l3_relu")
        s_gl = {n: sem(f"l3g_{n}") for n in ("ac", "act", "acs", "sh", "oh", "c1", "r1", "c2", "c3", "z",
                                             "acc", "fold", "x")}
        s_out = sem("out_stored")
        s_flag = sem("flag_made")
        s_off = sem("late_offsets")
        s_ladj = [sem("late_adj0"), sem("late_adj1")]
        s_late = {n: sem(f"late_{n}") for n in (
            "edge", "ri", "rio", "ag", "ags", "ma", "rk", "pa", "pa2", "z", "sm", "sq", "g", "rit", "ritc",
            "d1", "d", "pre", "gath", "acv", "acl", "ex", "mn", "ln", "sp", "wf", "m1", "m2", "y", "ya", "b2")}

        def leave_round(eng, r):
            eng.drain().then_inc(s_gen, 1)
            eng.wait_ge(s_gen, due(r * 5))
            eng.sem_inc(s_passed, 1)

        c = Carve()
        NATW = c(NW * 128).rearrange("p (w n) -> p w n", w=NW)
        W3N = c(256).rearrange("p (w n) -> p w n", w=2)
        ROWN = c(512)
        MLN2 = c(128)
        ADJ = [c(GC) for _ in range(4)]
        MASK = [c(GC // 2, BF16), c(GC // 2, BF16)]
        SUMW2 = c(1)
        MINUS_HALF = c(64)

        c = Carve()
        HB = [c(GC), c(GC)]
        TB = [c(GC), c(GC)]
        XB = [c(GC), c(GC)]
        UB = [c(GC), c(GC)]
        VB = [c(GC), c(GC)]
        RZ = [c(2 * GC), c(2 * GC)]
        NB_ = [c(GC), c(GC)]

        c = Carve()
        OH = [c(CC // 2, BF16), c(CC // 2, BF16)]
        PA = [c(CC), c(CC)]
        PA2 = [c(CC), c(CC)]
        ZC = c(HC)
        GA = [c(HC), c(HC)]
        SP = [c(CC), c(CC)]
        GS = [c(CC), c(CC)]
        HS = c(10 * N).rearrange("p (s i) -> p s i", i=N)
        YT = c(N)
        RF = [c(128) for _ in range(GB)]

        c = Carve()
        LADJ = [c(GC), c(GC)]
        RI = [c(GC) for _ in range(4)]
        RIT = [c(GC) for _ in range(4)]
        UPTO = c(GC)
        RIO = [c(GC // 2, BF16) for _ in range(4)]
        AGS = [c(GC), c(GC)]
        MA = [c(GC // 2, BF16) for _ in range(2)]
        LPA = [c(GC), c(GC)]
        LPA2 = [c(GC), c(GC)]
        LGA = c(GC)
        LSP = [c(GC), c(GC)]
        LM = c(GC)
        LD1 = c(GB * LATE)
        LD = [c(GB * LATE), c(GB * LATE)]

        c = Carve()
        OH3 = [c(NS3 * N // 2, BF16).rearrange("p (s i) -> p s i", i=N) for _ in range(2)]
        PARTS = [c(3 * D, BF16).rearrange("p (k w n) -> p k w n", k=3, w=2) for _ in range(2)]
        REM = [c(2 * D).rearrange("p (w n) -> p w n", w=2) for _ in range(2)]
        ACT_ = [c(N), c(N)]
        AC = [c(NS), c(NS)]
        ACC = [c(GC).rearrange("p (s o) -> p s o", o=D) for _ in range(2)]
        MSG = [[c(GC).rearrange("p (s o) -> p s o", o=D) for _ in range(BPG3 - 1)] for _ in range(2)]
        LAST = c(2 * D).rearrange("p (s o) -> p s o", o=D)
        SHR = c(N // 2, BF16)
        SHV = c(1)
        IOTA3 = c(NS3 * N // 2, BF16).rearrange("p (s i) -> p s i", i=N)

        def spread(ap, b, split):
            if split:
                return ap[:, bass.ds(b * N, 2 * N)].rearrange("p (g a i) -> p g a i", g=2, a=1)\
                    .to_broadcast([128, 2, 4, N])
            return ap[:, gsl(b, N)].rearrange("p (a i) -> p a i", a=1).to_broadcast([128, 8, N])

        def spread_rank(b):
            return RANK[:, gsl(b, N)].rearrange("p (a i) -> p a i", a=1).to_broadcast([128, NS3, N])

        def slots_of(ap, split):
            return ap.rearrange("p (g s i) -> p g s i", g=2, i=N) if split else \
                ap.rearrange("p (s i) -> p s i", i=N)

        def general_rounds(eng, one_round, late, last_dma=False):
            many = eng.value_load(FLAG[0:1, 0:1], min_val=0, max_val=1)
            with eng.If(many > 0):
                with eng.Fori(1, NR) as r:
                    one_round(r)
                    if last_dma:
                        eng.wait_ge(s_acd, due((r + 1) * (16 * STEPS)))
                        eng.sem_inc(s_passed, 1)
                    leave_round(eng, r)
            with eng.Else():
                ring_steps(eng, late, 6)

        def slot_adj(v, b, s):
            return AC[v][:, s:s + 1] if s < NS else ACL[:, bass.ds(b * LATE + (s - NS), 1)]

        def g4(ap, q):
            return ap[:, q * N:(q + 1) * N]

        block = ctx.enter_context(nc.Block())

        @block.sync
        def _(sp):
            def column(name, k=0):
                return io[name][k * 128:(k + 1) * 128].rearrange("(p a) -> p a", a=1)

            small = [(NATW[:, W1, h * NG:(h + 1) * NG], io["L1_gnn_W1"]) for h in range(2)]
            small += [(NATW[:, at:at + 3, :], io[n].rearrange("(c p) d -> p c d", p=128))
                      for n, at in (("L2_gnn_W_ih", IH), ("L2_gnn_W_hh", HH))]
            small += [(W0[:, :], io["L0_gnn_W"]),
                      (W3N[:, :, :], io["L3_gnn_W"].rearrange("(c p) d -> p c d", p=128))]
            small += [(ROWN[0:1, k * 128:(k + 1) * 128], io[n].rearrange("(a n) -> a n", a=1))
                      for k, n in enumerate(("L0_gnn_b", "L1_gnn_bd2", "L3_gnn_b", "L2_gnn_b2"))]
            small += [(COLB[:, k:k + 1], column(n))
                      for k, n in enumerate(("L1_gnn_b1", "L1_gnn_b2", "L1_gnn_bd1", "L2_gnn_b1"))]
            small += [(COLB[:, at + k:at + k + 1], column(n, k)) for k in range(3)
                      for n, at in (("L2_gnn_b_ih", 4), ("L2_gnn_b_hh", 7))]

            def load_adj(t, u, r4):
                if not active(t, G):
                    return
                sp.wait_ge(s_deg, due(t - 3))
                sp.wait_ge(s_tp, due(t - 3))
                sp.dma_start(by4(ADJ[r4]), io["adj"][bass.ds(t * GB, GB), :, :]
                             .rearrange("b i j -> i b j")).then_inc(s_adj[r4], 16)
                if isinstance(t, int) and 1 <= t < 6:
                    for dst, src in small[(t - 1) * 4:t * 4]:
                        sp.dma_start(dst, src).then_inc(s_w, 16)
            ring_steps(sp, load_adj, 0)
            sp.drain().then_inc(s_phase, 1)
            sp.wait_ge(s_phase, 5)
            sp.drain().then_inc(s_phase, 1)
            sp.wait_ge(s_phase, 10)
            sp.drain().then_inc(s_phase, 1)
            sp.wait_ge(s_phase, 15)

            def save_ac(base):
                def step(m, k, t):
                    h = t - 1
                    if not active(h, STEPS):
                        return
                    sp.wait_ge(s_zc, due(h + 1, base))
                    sp.dma_start(acD[bass.ds(h + base, 1)].rearrange("c h w -> (c h) w"),
                                 ZC[0:NG + 1:NG, :]).then_inc(s_acd, 16)
                return step
            chunk_steps(sp, save_ac(0), 1)
            sp.wait_ge(s_acd, 16 * STEPS)
            sp.drain().then_inc(s_phase, 1)
            sp.wait_ge(s_phase, 20)

            def late(t, u, r4):
                if active(t, G):
                    sp.wait_ge(s_late["ag"], due(t - 1))
                    sp.dma_start(by4(LADJ[u]), io["adj"][bass.ds(t * GB, GB), :, :]
                                 .rearrange("b i j -> i b j")).then_inc(s_ladj[u], 16)
            general_rounds(sp, lambda r: chunk_steps(sp, save_ac(r * STEPS), 1), late, last_dma=True)
            sp.drain().then_inc(s_phase, 1)
            sp.wait_ge(s_phase, 25)
            sp.drain().then_inc(s_phase, 1)
            sp.wait_ge(s_phase, 30)
            sp.drain().then_inc(s_phase, 1)
            sp.wait_ge(s_phase, 35)
            sp.drain().then_inc(s_phase, 1)
            sp.wait_ge(s_phase, 40)
            sp.drain().then_inc(s_phase, 1)
            sp.wait_ge(s_phase, 45)

            many = sp.value_load(FLAG[0:1, 0:1], min_val=0, max_val=1)
            with sp.If(many > 0):
                with sp.Fori(0, B) as b:
                    with sp.Fori(0, NR) as r:
                        sp.wait_ge(s_gl["act"], due(b * NR + r + 1))
                        sp.dma_start(ACT_[0][0:NS, :], ac_rows[bass.ds(r * B + b, 1)]
                                     .rearrange("a s i -> (a s) i")).then_inc(s_gl["ac"], 16)
                sp.wait_ge(s_gl["x"], B)
                for k in range(G):
                    sp.dma_start(io["out"][k * GB:(k + 1) * GB].rearrange("b n d -> n b d"),
                                 by4(X[:, k * GC:(k + 1) * GC])).then_inc(s_out, 16)
                sp.wait_ge(s_out, 16 * G)
            with sp.Else():
                def load_ac(t, u):
                    if active(t, B):
                        sp.wait_ge(s_l3["act"], due(t - 1))
                        sp.dma_start(ACT_[u][0:NS, :], ac_rows[bass.ds(t, 1)].rearrange("a s i -> (a s) i"))\
                          .then_inc(s_l3[f"ac{u}"], 16)
                    h = t - 4
                    if active(h, B):
                        sp.wait_ge(s_l3["x"], due(h + 1))
                        sp.dma_start(io["out"][bass.ds(h, 1)].rearrange("a n d -> (a n) d"), X[:, gsl(h, D)])\
                          .then_inc(s_out, 16)
                graph_steps(sp, load_ac, 4)
                sp.wait_ge(s_out, 16 * B)
            sp.drain().then_inc(s_phase, 1)
            sp.wait_ge(s_phase, 50)

        @block.gpsimd
        def _(pool):
            nc.gpsimd.memset(ident[:, :], 0.0).then_inc(s_gp, 1)
            nc.gpsimd.memset(identb[:, :], 0.0).then_inc(s_gp, 1)
            nc.gpsimd.memset(upto[:, :], 0.0).then_inc(s_gp, 1)
            nc.gpsimd.memset(ones[:, :], 1.0).then_inc(s_gp, 1)
            nc.gpsimd.memset(MLN2[:, :], -LN2).then_inc(s_gp, 1)
            nc.gpsimd.memset(MINUS_HALF[:, :], -0.5).then_inc(s_gp, 1)
            nc.gpsimd.memset(MX[0:1, :], 0.0).then_inc(s_gp, 1)
            nc.gpsimd.memset(COLB[:, 11:16], -0.5).then_inc(s_gp, 1)
            nc.gpsimd.memset(ONE[:, :], 1.0).then_inc(s_gp, 1)
            nc.gpsimd.memset(onesb[:, :], 1.0).then_inc(s_gp, 1)
            pool.wait_ge(s_gp, 10)
            nc.gpsimd.affine_select(out=ident[:, :], in_=ident[:, :], compare_op=ALU.not_equal, fill=1.0,
                                    base=0, pattern=[[-1, 128]], channel_multiplier=1).then_inc(s_gp, 1)
            nc.gpsimd.affine_select(out=identb[:, :], in_=identb[:, :], compare_op=ALU.not_equal, fill=1.0,
                                    base=0, pattern=[[-1, 128]], channel_multiplier=1).then_inc(s_gp, 1)
            nc.gpsimd.affine_select(out=upto[:, :], in_=upto[:, :], compare_op=ALU.is_gt, fill=1.0,
                                    base=0, pattern=[[1, 128]], channel_multiplier=-1).then_inc(s_gp, 1)
            for at, n in ((0, NS), (NS, 4)):
                nc.gpsimd.iota(IOTA[:, at * N:(at + n) * N].rearrange("p (s i) -> p s i", i=N),
                               pattern=[[1, n], [0, N]], base=1, channel_multiplier=0,
                               allow_small_or_imprecise_dtypes=True).then_inc(s_gp, 1)
            nc.gpsimd.iota(IOTAC[:, :], pattern=[[1, N]], base=1, channel_multiplier=0,
                           allow_small_or_imprecise_dtypes=True).then_inc(s_gp, 1)
            nc.gpsimd.iota(NEGC[0:1, :].rearrange("p (g c) -> p g c", g=GB), pattern=[[0, GB], [-1, N]],
                           base=-(NS + 1), channel_multiplier=0, allow_small_or_imprecise_dtypes=True)\
              .then_inc(s_gp, 1)
            nc.gpsimd.iota(CS[:, :], pattern=[[-1, LATE]], base=0, channel_multiplier=1,
                           allow_small_or_imprecise_dtypes=True).then_inc(s_gp, 1)
            for h in range(2):
                pool.wait_ge(s_gp, 18 + h)
                nc.gpsimd.iota(offc[h * NG:(h + 1) * NG, :], pattern=[[0, 1]], base=0, channel_multiplier=1,
                               allow_small_or_imprecise_dtypes=True).then_inc(s_gp, 1)
            pool.wait_ge(s_gp, 20)
            pool.wait_ge(s_d0, 1)
            nc.gpsimd.tensor_tensor(DEG, DEG, MINUS_HALF, ALU.pow).then_inc(s_d0, 1)
            pool.drain().then_inc(s_phase, 1)
            pool.wait_ge(s_phase, 5)

            def ln_root(layer, add_bias=None):
                base = layer * G

                def step(t, u):
                    if active(t, G):
                        pool.wait_ge(s_var, due(t + 1, base))
                        v = LNS[:, bass.ds(t * GB, GB)]
                        nc.gpsimd.tensor_tensor(v, v, COLB[:, 11:15], ALU.pow).then_inc(s_rs, 1)
                    if add_bias is not None:
                        add_bias(t, u)
                return step

            def xb0(t, u):
                h = t - 2
                if active(h, G):
                    pool.wait_ge(s_p2[3], due(h - 1))
                    nc.gpsimd.tensor_tensor(by4(XB[u]), by4(X[:, gsl(h)]),
                                            ROWB[:, 0:1, :].to_broadcast([128, GB, 128]), ALU.add)\
                      .then_inc(s_p2[4], 1)
            group_steps(pool, ln_root(0, xb0), 2)
            pool.drain().then_inc(s_phase, 1)
            pool.wait_ge(s_phase, 10)
            group_steps(pool, ln_root(1), 0)
            pool.drain().then_inc(s_phase, 1)
            pool.wait_ge(s_phase, 15)

            def weigh(base, rbase):
                def step(m, k, t):
                    if not active(t, STEPS):
                        return
                    u = k % 2
                    b, slot, split = place(m, k)
                    if slot == 0 or split:
                        b2, q = (b + 1, 2 * k // BPG + 1) if split else (b, 2 * k // BPG)
                        pool.wait_ge(s_gp2, due((b2 - 3) * BPG, base * 2))
                        pool.sem_inc(s_passed, 1)
                        nc.gpsimd.tensor_copy(RF[q], R[:, gsl(b2, 128)]).then_inc(s_rf, 1)
                    pool.wait_ge(s_oh, due(t + 1, base))
                    pool.wait_ge(s_z, due(t - 1, base))
                    pool.sem_inc(s_passed, 1)
                    nc.gpsimd.tensor_tensor(slots_of(PA[u], split), slots_of(OH[u], split),
                                            spread(AT, b, split), ALU.mult).then_inc(s_pa, 1)
                    pool.wait_ge(s_pa, due(t + 1, base))
                    pool.wait_ge(s_gp2, due(2 * (t - 1), base * 2))
                    nc.gpsimd.tensor_tensor(PA2[u], PA[u], PA[u], ALU.mult).then_inc(s_pa2, 1)
                return step
            chunk_steps(pool, weigh(0, 0), 0)
            pool.drain().then_inc(s_phase, 1)
            pool.wait_ge(s_phase, 20)

            def late(t, u, r4):
                h = t - 3
                if active(h, G):
                    v = 1 - u
                    pool.wait_ge(s_late["pa"], due(h + 1))
                    pool.wait_ge(s_late["gath"], due(h - 1))
                    nc.gpsimd.tensor_tensor(LPA2[v], LPA[v], LPA[v], ALU.mult).then_inc(s_late["pa2"], 1)
                if active(t, G):
                    pool.wait_ge(s_late["edge"], due(2 * (t + 1)))
                    nc.gpsimd.tensor_tensor(RI[r4], RI[r4], UPTO, ALU.mult).then_inc(s_late["ri"], 1)
                    pool.wait_ge(s_late["ri"], due(t + 1))
                    pool.wait_ge(s_late["sm"], due(t - 3))
                    nc.gpsimd.tensor_tensor(by4(RIO[r4]), by4(RI[r4]), OFFE[:, bass.ds(t * GB, GB)]
                                            .rearrange("p (g a) -> p g a", a=1).to_broadcast([128, GB, N]),
                                            ALU.mult).then_inc(s_late["rio"], 1)
            general_rounds(pool, lambda r: chunk_steps(pool, weigh(r * STEPS, r * B), 0), late)
            pool.drain().then_inc(s_phase, 1)
            pool.wait_ge(s_phase, 25)

            def xb1(t, u):
                if active(t, G):
                    pool.wait_ge(s_p5[6], due(t - 1))
                    nc.gpsimd.tensor_tensor(by4(XB[u]), by4(X[:, gsl(t)]),
                                            ROWB[:, 1:2, :].to_broadcast([128, GB, 128]), ALU.add)\
                      .then_inc(s_p5[7], 1)
            group_steps(pool, xb1, 0)
            pool.drain().then_inc(s_phase, 1)
            pool.wait_ge(s_phase, 30)
            group_steps(pool, ln_root(2), 0)
            pool.drain().then_inc(s_phase, 1)
            pool.wait_ge(s_phase, 35)

            def blend(t, u):
                h = t - 1
                if active(h, G):
                    v = 1 - u
                    ht = R[:, gsl(h)]
                    pool.wait_ge(s_p8[5], due(h + 1))
                    pool.wait_ge(s_p8[9], due(h - 1))
                    nc.gpsimd.tensor_tensor(UB[v], ht, NB_[v], ALU.subtract).then_inc(s_p8[6], 1)
                    pool.wait_ge(s_p8[6], due(h + 1))
                    nc.gpsimd.tensor_tensor(UB[v], UB[v], RZ[v][:, GC:2 * GC], ALU.mult).then_inc(s_p8[7], 1)
                    pool.wait_ge(s_p8[7], due(h + 1))
                    nc.gpsimd.tensor_tensor(UB[v], UB[v], NB_[v], ALU.add).then_inc(s_p8[8], 1)
            group_steps(pool, blend, 1)
            pool.drain().then_inc(s_phase, 1)
            pool.wait_ge(s_phase, 40)
            for at in range(0, NS3, 4):
                nc.gpsimd.iota(IOTA3[:, at:at + 4, :], pattern=[[1, 4], [0, N]], base=at + 1,
                               channel_multiplier=0, allow_small_or_imprecise_dtypes=True).then_inc(s_io, 1)
            group_steps(pool, ln_root(3), 0)
            pool.drain().then_inc(s_phase, 1)
            pool.wait_ge(s_phase, 45)

            many = pool.value_load(FLAG[0:1, 0:1], min_val=0, max_val=1)
            with pool.If(many > 0):
                pool.nop()
            with pool.Else():
                def remainders(t, u):
                    if active(t, B):
                        y2 = YR[:, :, gsl(t, 128)]
                        pool.wait_ge(s_l3["c1"], due(t + 1))
                        pool.wait_ge(s_l3["c2"], due(t - 1))
                        pool.sem_inc(s_passed, 1)
                        nc.gpsimd.tensor_tensor(REM[u], y2, PARTS[u][:, 0], ALU.subtract).then_inc(s_l3["r1"], 1)
                        pool.wait_ge(s_l3["c2"], due(t + 1))
                        nc.gpsimd.tensor_tensor(PARTS[u][:, 2], REM[u], PARTS[u][:, 1], ALU.subtract)\
                          .then_inc(s_l3["c3"], 1)
                    h = t - 2
                    if active(h, B):
                        pool.wait_ge(s_l3["fold"], due(h * 2 + 2))
                        pool.sem_inc(s_passed, 1)
                        nc.gpsimd.tensor_tensor(X[:, gsl(h, D)], X[:, gsl(h, D)], ACC[u][:, 0, :], ALU.add)\
                          .then_inc(s_l3["x"], 1)
                graph_steps(pool, remainders, 2)
            pool.drain().then_inc(s_phase, 1)
            pool.wait_ge(s_phase, 50)

        @block.vector
        def _(dve):
            dve.wait_ge(s_gp, 10)
            def ranks(t, u, r4):
                if active(t, G):
                    dve.wait_ge(s_adj[r4], (t - r4) * 4 + 16)
                    nc.vector.reduce_sum(DEG[:, bass.ds(t * GB, GB)], by4(ADJ[r4]), AX.X).then_inc(s_deg, 1)
                    dve.wait_ge(s_at, due(t + 1))
                    dve.wait_ge(s_rank, due(t - 1))
                    nc.vector.tensor_scalar(MASK[u], AT[:, gsl(t)], 0.0, None, ALU.not_equal).then_inc(s_mask, 1)
                    nc.vector.tensor_scalar(RANK[:, gsl(t)], AT[:, gsl(t)], 0.0, NO_SLOT,
                                            ALU.is_equal, ALU.mult).then_inc(s_mask, 1)
                h = t - 1
                if active(h, G):
                    dve.wait_ge(s_rank, due(h + 1))
                    dve.wait_ge(s_mask, due(h * 2 + 2))
                    nc.vector.tensor_tensor(RANK[:, gsl(h)], RANK[:, gsl(h)], bank(2 + (1 - u)), ALU.add)\
                      .then_inc(s_rks, 1)
                    nc.vector.tensor_scalar(OV[:, bass.ds(h * GB, GB)], bank(4 + (1 - u))[:, 0:GB], -float(NS), 0.0,
                                            ALU.add, ALU.max).then_inc(s_rks, 1)
            ring_steps(dve, ranks, 1)
            dve.wait_ge(s_gp, 20)
            nc.vector.tensor_scalar(offc, offc, -float(WIDTH), None, ALU.mult).then_inc(s_prep, 1)
            dve.wait_ge(s_w, 16 * LOADS)
            nc.vector.tensor_tensor(COLB[:, 4:6], COLB[:, 4:6], COLB[:, 7:9], ALU.add).then_inc(s_prep, 1)
            nc.vector.reduce_sum(SUMW2, NATW[:, W2, :], AX.X).then_inc(s_prep, 1)
            nc.vector.tensor_tensor(W3[:, 0, :], W3N[:, 0, :], W3N[:, 1, :], ALU.subtract).then_inc(s_prep, 1)
            nc.vector.tensor_copy(W3[:, 1, :], W3N[:, 1, :]).then_inc(s_prep, 1)
            dve.wait_ge(s_prep, 5)
            nc.vector.scalar_tensor_tensor(b2c, SUMW2, -LN2, b2c, ALU.mult, ALU.add).then_inc(s_prep, 1)
            dve.wait_ge(s_deg, G)
            nc.vector.tensor_scalar(DEG, DEG, DEG_EPS, None, ALU.add).then_inc(s_d0, 1)
            dve.wait_ge(s_rks, 2 * G)
            nc.vector.tensor_copy(OVB[:, 0:B], OV[:, :]).then_inc(s_off, 1)
            nc.vector.tensor_scalar(OVB[:, B:2 * B], OV[:, :], float(LATE) + 0.5, TOO_LONG, ALU.is_gt, ALU.mult)\
              .then_inc(s_off, 1)
            dve.wait_ge(s_off, 3)
            nc.vector.tensor_copy(OFFI[:, :], bank(7)[:, 0:B]).then_inc(s_off, 1)
            nc.vector.tensor_tensor(OFFE[:, :], bank(7)[:, 0:B], OV[:, :], ALU.subtract).then_inc(s_off, 1)
            nc.vector.reduce_max(MX[0:1, 0:1], bank(7)[0:1, 0:2 * B], AX.X).then_inc(s_flag, 1)
            dve.wait_ge(s_flag, 1)
            nc.vector.tensor_scalar(FLAG[0:1, 0:1], MX[0:1, 0:1], float(N) + 0.5, None, ALU.is_gt)\
              .then_inc(s_flag, 1)
            dve.drain().then_inc(s_phase, 1)
            dve.wait_ge(s_phase, 5)

            def ln_stats(layer, t, u):
                base = layer * G
                st = STATB[:, u, 0:GB * 6].rearrange("p (b k) -> p b k", k=6)
                mv = STATB[:, u, GB * 6:GB * 8].rearrange("p (b k) -> p b k", k=2)
                for q in range(GB):
                    nc.vector.bn_stats(st[:, q, :], X[:, bass.ds(t * GC + q * D, D)]).then_inc(s_bn, 1)
                dve.wait_ge(s_bn, due(t * (2 * GB + 1) + GB, layer * G * (2 * GB + 1)))
                dve.sem_inc(s_passed, 1)
                for q in range(GB):
                    nc.vector.bn_aggr(mv[:, q, :], st[:, q, :]).then_inc(s_bn, 1)
                dve.wait_ge(s_bn, due(t * (2 * GB + 1) + 2 * GB, layer * G * (2 * GB + 1)))
                v = LNS[:, bass.ds(t * GB, GB)]
                nc.vector.tensor_scalar(v, mv[:, :, 1], LN_EPS, None, ALU.add).then_inc(s_var, 1)
                nc.vector.tensor_scalar(LNB[:, bass.ds(t * GB, GB)], mv[:, :, 0], -1.0, None, ALU.mult)\
                  .then_inc(s_bn, 1)

            def ln_shift(layer, t):
                dve.wait_ge(s_rs, due(t + 1, layer * G))
                dve.wait_ge(s_bn, due((t + 1) * (2 * GB + 1), layer * G * (2 * GB + 1)))
                v, s = LNS[:, bass.ds(t * GB, GB)], LNB[:, bass.ds(t * GB, GB)]
                if layer == 0:
                    nc.vector.tensor_tensor(v, v, DEG[:, bass.ds(t * GB, GB)], ALU.mult).then_inc(s_prep, 1)
                    dve.wait_ge(s_prep, due(t + 7))
                nc.vector.tensor_tensor(s, s, v, ALU.mult).then_inc(s_hu, 1)

            dve.wait_ge(s_x, 16 * 4)

            def layer0(t, u):
                if active(t - 1, G):
                    ln_shift(0, t - 1)
                if active(t, G):
                    ln_stats(0, t, u)
                h = t - 3
                if active(h, G):
                    dve.wait_ge(s_p2[2], due(h + 1))
                    dve.wait_ge(s_p2[4], due(h + 1))
                    for q in range(GB):
                        last = nc.vector.scalar_tensor_tensor(
                            X[:, bass.ds(h * GC + q * D, D)], bank(2 + (1 - u))[:, q * D:(q + 1) * D],
                            DEG[:, bass.ds(h * GB + q, 1)], XB[1 - u][:, q * D:(q + 1) * D],
                            ALU.mult, ALU.add)
                    last.then_inc(s_p2[3], 1)
            group_steps(dve, layer0, 3)
            dve.drain().then_inc(s_phase, 1)
            dve.wait_ge(s_phase, 10)

            def norm1(t, u):
                if active(t, G):
                    ln_stats(1, t, u)
                if active(t - 1, G):
                    ln_shift(1, t - 1)
            group_steps(dve, norm1, 1)
            dve.drain().then_inc(s_phase, 1)
            dve.wait_ge(s_phase, 15)

            def sum_slots(dst, lo, hi):
                return nc.vector.reduce_sum(dst, HS[:, lo:hi, :].rearrange("p s i -> p i s"), AX.X)

            def edges1(base, rbase, general):
                def step(m, k, t):
                    u = k % 2
                    v = 1 - u
                    e = t - 5
                    if active(e, STEPS):
                        ek = (k - 5) % UNROLL
                        eb, eslot, esplit = place(m if k >= 5 else m - 1, ek)
                        dve.wait_ge(s_wf, due(e + 1, base))
                        dve.wait_ge(s_gc, due(2 * (e + 1), base * 2))
                        dve.wait_ge(s_red, due(e, base))
                        nc.vector.scalar_tensor_tensor(
                            HS[:, 1:9, :], bank(4, 2).rearrange("p (s i) -> p s i", i=N), b2c,
                            GS[v].rearrange("p (s i) -> p s i", i=N), ALU.add, ALU.mult).then_inc(s_hm, 1)
                        dve.wait_ge(s_hm, due(e + 1, base))
                        into, out = CARRY[ek], CARRY[ek + 1] if ek + 1 < UNROLL else None
                        whole = YT if general else Y[:, gsl(eb, N)]
                        lo, hi = (0 if into == 0 else 1), (10 if into == 9 else 9)
                        if esplit:
                            last = sum_slots(whole, lo, 5)
                            last.then_inc(s_fin, 1)
                            sum_slots(HS[:, out, :], 5, 9).then_inc(s_red, 1)
                        elif out is None or eslot + 8 == NS:
                            sum_slots(whole, lo, hi).then_inc(s_red, 1)
                        else:
                            sum_slots(HS[:, out, :], lo, hi).then_inc(s_red, 1)
                        if general and (esplit or eslot + 8 == NS):
                            dve.wait_ge(s_red, due(e + 1, base))
                            if esplit:
                                dve.wait_ge(s_fin, due(1 + 2 * (m if k >= 5 else m - 1) + (ek >= UNROLL // 2),
                                                       rbase))
                            nc.vector.tensor_tensor(Y[:, gsl(eb, N)], Y[:, gsl(eb, N)], YT, ALU.add)\
                              .then_inc(s_ya, 1)
                    h = t - 3
                    if active(h, STEPS):
                        pre = bank(2 if v == 0 else 6, 2)
                        dve.wait_ge(s_ex, due(h + 1, base))
                        nc.vector.tensor_scalar(SP[v], SP[v], EXP_MAX, None, ALU.min).then_inc(s_min, 1)
                    if active(t, STEPS):
                        b, slot, split = place(m, k)
                        dve.wait_ge(s_pa, due(t - 1, base))
                        nc.vector.tensor_tensor(slots_of(OH[u], split), spread(RANK, b, split),
                                                slots_of(IOTA[:, slot * N:(slot + 8) * N], split),
                                                ALU.is_equal).then_inc(s_oh, 1)
                    if active(h, STEPS):
                        dve.wait_ge(s_ln, due(h + 1, base))
                        nc.vector.scalar_tensor_tensor(SP[v], pre, b1c, SP[v], ALU.add, ALU.max)\
                          .then_inc(s_sp, 1)
                return step
            chunk_steps(dve, edges1(0, 0, False), 5)
            dve.drain().then_inc(s_phase, 1)
            dve.wait_ge(s_phase, 20)
            many = dve.value_load(FLAG[0:1, 0:1], min_val=0, max_val=1)
            with dve.If(many > 0):
                with dve.Fori(1, NR) as r:
                    nc.vector.tensor_scalar(IOTA[:, :], IOTA[:, :], float(NS), None, ALU.add).then_inc(s_io, 1)
                    dve.wait_ge(s_io, r)
                    chunk_steps(dve, edges1(r * STEPS, (r * 2) * G, True), 5)
                    leave_round(dve, r)
            with dve.Else():
                nc.vector.tensor_scalar(LM[:, 0:N], ident[:, :], b2c, None, ALU.mult).then_inc(s_late["b2"], 1)

                def late(t, u, r4):
                    v = 1 - u
                    h = t - 4
                    if active(h, G):
                        dve.wait_ge(s_late["ex"], due(h + 1))
                        nc.vector.tensor_scalar(LSP[u], LSP[u], EXP_MAX, None, ALU.min).then_inc(s_late["mn"], 1)
                    h = t - 6
                    if active(h, G):
                        dve.wait_ge(s_late["y"], due(h + 1))
                        nc.vector.tensor_tensor(Y[:, gsl(h)], Y[:, gsl(h)], bank(1), ALU.add)\
                          .then_inc(s_late["ya"], 1)
                    h = t - 5
                    if active(h, G):
                        dve.wait_ge(s_late["wf"], due(h + 1))
                        dve.wait_ge(s_late["b2"], 3)
                        dve.wait_ge(s_late["y"], due(h))
                        nc.vector.tensor_tensor(by4(LM), by4(bank(7)), B2R[:, :].rearrange("p (a n) -> p a n", a=1)
                                                .to_broadcast([128, GB, N]), ALU.add).then_inc(s_late["m1"], 1)
                        dve.wait_ge(s_late["m1"], due(h + 1))
                        dve.wait_ge(s_late["gath"], due(h + 1))
                        nc.vector.tensor_tensor(LM, LM, bank(6), ALU.mult).then_inc(s_late["m2"], 1)
                    h = t - 2
                    if active(h, G):
                        dve.wait_ge(s_late["rk"], due(h + 1))
                        dve.wait_ge(s_late["ags"], due(h + 1))
                        dve.wait_ge(s_late["z"], due(h - 1))
                        dve.wait_ge(s_late["sm"], due(h - 1))
                        dve.wait_ge(s_late["pa2"], due(h - 1))
                        nc.vector.scalar_tensor_tensor(LPA[u], bank(2), 0.0, AGS[u], ALU.is_equal, ALU.mult)\
                          .then_inc(s_late["pa"], 1)
                    h = t - 1
                    if active(h, G):
                        dve.wait_ge(s_late["ags"], due(h + 1))
                        dve.wait_ge(s_late["rk"], due(h - 1))
                        nc.vector.tensor_scalar(MA[v], AGS[v], 0.0, None, ALU.not_equal).then_inc(s_late["ma"], 1)
                    h = t - 4
                    if active(h, G):
                        dve.wait_ge(s_late["ln"], due(h + 1))
                        nc.vector.scalar_tensor_tensor(LSP[u], bank(4), b1c, LSP[u], ALU.add, ALU.max)\
                          .then_inc(s_late["sp"], 1)
                    h = t - 3
                    if active(h, G):
                        offs, adj_c = (bank(5)[:, k:k + GB].rearrange("p (g a) -> p g a", a=1)
                                       .to_broadcast([128, GB, LATE]) for k in (GB, 0))
                        d1, d = (a.rearrange("p (g s) -> p g s", g=GB) for a in (LD1, LD[v]))
                        dve.wait_ge(s_late["sm"], due(h + 1))
                        dve.wait_ge(s_late["d"], due(h))
                        nc.vector.tensor_tensor(d1, CS[:, :].rearrange("p (a s) -> p a s", a=1)
                                                .to_broadcast([128, GB, LATE]), offs, ALU.is_equal)\
                          .then_inc(s_late["d1"], 1)
                        dve.wait_ge(s_late["d1"], due(h + 1))
                        dve.wait_ge(s_late["acv"], due(h - 1))
                        nc.vector.tensor_tensor(d, d1, adj_c, ALU.mult).then_inc(s_late["d"], 1)
                    if active(t, G):
                        c_ = IOTAC[:, :].rearrange("p (a n) -> p a n", a=1).to_broadcast([128, GB, N])
                        lo, hi = (o[:, bass.ds(t * GB, GB)].rearrange("p (g a) -> p g a", a=1)
                                  .to_broadcast([128, GB, N]) for o in (OFFE, OFFI))
                        dve.wait_ge(s_late["rit"], due(t - 3))
                        nc.vector.tensor_tensor(by4(RI[r4]), c_, lo, ALU.is_gt).then_inc(s_late["edge"], 1)
                        dve.wait_ge(s_late["ri"], due(t))
                        nc.vector.tensor_tensor(by4(UPTO), c_, hi, ALU.is_le).then_inc(s_late["edge"], 1)
                ring_steps(dve, late, 6)
            dve.drain().then_inc(s_phase, 1)
            dve.wait_ge(s_phase, 25)

            def nodes1(t, u):
                h = t - 1
                if active(h, G):
                    v = 1 - u
                    dve.wait_ge(s_p5[3], due(h + 1))
                    nc.vector.scalar_tensor_tensor(TB[v], bank(v), bd1c, TB[v], ALU.add, ALU.max)\
                      .then_inc(s_p5[4], 1)
                if active(t, G):
                    dve.wait_ge(s_p5[0], due(t + 1))
                    dve.wait_ge(s_p5[5], due(t - 1))
                    nc.vector.tensor_scalar(TB[u], bank(u), bd1c, SOFT_MAX, ALU.add, ALU.min).then_inc(s_p5[1], 1)
                e = t - 2
                if active(e, G):
                    dve.wait_ge(s_p5[5], due(e + 1))
                    dve.wait_ge(s_p5[7], due(e + 1))
                    nc.vector.tensor_tensor(X[:, gsl(e)], bank(2 + u), XB[u], ALU.add).then_inc(s_p5[6], 1)
            group_steps(dve, nodes1, 2)
            dve.drain().then_inc(s_phase, 1)
            dve.wait_ge(s_phase, 30)

            def norm2(t, u):
                if active(t - 1, G):
                    ln_shift(2, t - 1)
                if active(t, G):
                    ln_stats(2, t, u)
                h = t - 4
                if active(h, G):
                    dve.wait_ge(s_p6[4], due(h + 1))
                    dve.wait_ge(s_p6[6], due(h - 1))
                    nc.vector.tensor_tensor(by4(UB[u]), by4(bank(4 + u)), ROWB[:, 3:4, :].to_broadcast([128, GB, 128]),
                                            ALU.add).then_inc(s_p6[8], 1)
                    dve.wait_ge(s_p6[8], due(h + 1))
                    nc.vector.tensor_scalar(UB[u], UB[u], 0.0, None, ALU.max).then_inc(s_p6[5], 1)
            group_steps(dve, norm2, 4)
            dve.drain().then_inc(s_phase, 1)
            dve.wait_ge(s_phase, 35)

            def gates(t, u):
                h = t - 2
                if active(t, G):
                    dve.wait_ge(s_p8[2], due(t + 1))
                    dve.wait_ge(s_p8[1], due(t + 1))
                    dve.wait_ge(s_p8[5], due(t - 1))
                    nc.vector.scalar_tensor_tensor(VB[u], bank(3), bhn, RZ[u][:, 0:GC], ALU.add, ALU.mult)\
                      .then_inc(s_p8[3], 1)
                    dve.wait_ge(s_p8[3], due(t + 1))
                    nc.vector.tensor_tensor(VB[u], VB[u], bank(2), ALU.add).then_inc(s_p8[4], 1)
                if active(h, G):
                    dve.wait_ge(s_p8[9], due(h + 1))
                    nc.vector.tensor_tensor(X[:, gsl(h)], bank(4 + u), X[:, gsl(h)], ALU.add)\
                      .then_inc(s_p8[10], 1)
            group_steps(dve, gates, 2)
            dve.drain().then_inc(s_phase, 1)
            dve.wait_ge(s_phase, 40)

            def norm3(t, u):
                if active(t - 1, G):
                    ln_shift(3, t - 1)
                if active(t, G):
                    ln_stats(3, t, u)
                h = t - 3
                if active(h, G):
                    dve.wait_ge(s_p9[2], due(h + 1))
                    pq = bank(4 if u else 6, 2).rearrange("p (b w n) -> p b w n", b=GB, w=2)
                    nc.vector.tensor_tensor(by4(Y[:, gsl(h)]), pq[:, :, 0, :],
                                            ROWB[:, 2:3, :].to_broadcast([128, GB, 128]), ALU.add)\
                      .then_inc(s_p9[3], 1)
            group_steps(dve, norm3, 3)
            dve.drain().then_inc(s_phase, 1)
            dve.wait_ge(s_phase, 45)

            many = dve.value_load(FLAG[0:1, 0:1], min_val=0, max_val=1)
            with dve.If(many > 0):
                for n in ("act", "acs", "z", "acc"):
                    dve.sem_inc(s_gl[n], 1)
                nc.vector.memset(SHV[:, :], -float(NS) * (NR - 1)).then_inc(s_gl["sh"], 1)
                nc.vector.tensor_scalar(IOTA[:, :], IOTA[:, :], -float(NS) * (NR - 1), None, ALU.add)\
                  .then_inc(s_gl["sh"], 1)
                with dve.Fori(0, B) as b:
                    dve.wait_ge(s_gl["sh"], due(b * (2 * NR + 1) + 2))
                    nc.vector.tensor_scalar(SHV[:, :], SHV[:, :], float(NS) * NR, None, ALU.add)\
                      .then_inc(s_gl["sh"], 1)
                    y2 = YR[:, :, gsl(b, 128)]
                    dve.wait_ge(s_gl["z"], due(b * (NR * BPG) + 1))
                    nc.vector.tensor_copy(PARTS[0][:, 0], y2).then_inc(s_gl["c1"], 1)
                    dve.wait_ge(s_gl["c1"], due(b + 1))
                    nc.vector.tensor_tensor(REM[0], y2, PARTS[0][:, 0], ALU.subtract).then_inc(s_gl["r1"], 1)
                    dve.wait_ge(s_gl["r1"], due(b + 1))
                    nc.vector.tensor_copy(PARTS[0][:, 1], REM[0]).then_inc(s_gl["c2"], 1)
                    dve.wait_ge(s_gl["c2"], due(b + 1))
                    nc.vector.tensor_tensor(PARTS[0][:, 2], REM[0], PARTS[0][:, 1], ALU.subtract)\
                      .then_inc(s_gl["c3"], 1)
                    nc.vector.memset(ACC[0], 0.0).then_inc(s_gl["fold"], 1)
                    with dve.Fori(0, NR) as r:
                        n = b * NR + r
                        dve.wait_ge(s_gl["sh"], due(b * (2 * NR + 1) + r * 2 + 3))
                        nc.vector.tensor_scalar(SHV[:, :], SHV[:, :], -float(NS), None, ALU.add)\
                          .then_inc(s_gl["sh"], 1)
                        dve.wait_ge(s_gl["sh"], due(b * (2 * NR + 1) + r * 2 + 4))
                        nc.vector.tensor_scalar(SHR[:, :], RANK[:, gsl(b, N)], SHV[:, 0:1], None, ALU.add)\
                          .then_inc(s_gl["sh"], 1)
                        dve.wait_ge(s_gl["sh"], due(b * (2 * NR + 1) + r * 2 + 5))
                        dve.wait_ge(s_gl["z"], due(n * BPG + 1))
                        nc.vector.tensor_tensor(
                            OH3[0][:, 0:NS, :], SHR[:, :].rearrange("p (a i) -> p a i", a=1).to_broadcast([128, NS, N]),
                            IOTA[:, 0:NS * N].rearrange("p (s i) -> p s i", i=N), ALU.is_equal)\
                          .then_inc(s_gl["oh"], 1)
                        dve.wait_ge(s_gl["act"], due(n + 2))
                        dve.wait_ge(s_gl["acc"], due(n * BPG + 1))
                        nc.vector.tensor_scalar(AC[0], bank(6)[:, 0:NS], 0.0, None, ALU.max)\
                          .then_inc(s_gl["acs"], 1)
                        dve.wait_ge(s_gl["acs"], due(n + 2))
                        dve.wait_ge(s_gl["fold"], due(b * 3 + 1))
                        for kb in range(BPG):
                            dve.wait_ge(s_gl["z"], due(n * BPG + kb + 2))
                            dve.wait_ge(s_gl["acc"], due(n * BPG + kb + 1))
                            for q in range(4):
                                s = kb * 4 + q
                                last = nc.vector.scalar_tensor_tensor(
                                    ACC[0][:, q, :], bank(kb % 2)[:, q * D:(q + 1) * D], AC[0][:, s:s + 1],
                                    ACC[0][:, q, :], ALU.mult, ALU.max)
                            last.then_inc(s_gl["acc"], 1)
                    dve.wait_ge(s_gl["acc"], due((b + 1) * (NR * BPG) + 1))
                    nc.vector.tensor_tensor(ACC[0][:, 0:2, :], ACC[0][:, 0:2, :], ACC[0][:, 2:4, :], ALU.max)\
                      .then_inc(s_gl["fold"], 1)
                    dve.wait_ge(s_gl["fold"], due(b * 3 + 2))
                    nc.vector.tensor_tensor(ACC[0][:, 0, :], ACC[0][:, 0, :], ACC[0][:, 1, :], ALU.max)\
                      .then_inc(s_gl["fold"], 1)
                    dve.wait_ge(s_gl["fold"], due(b * 3 + 3))
                    nc.vector.tensor_tensor(X[:, gsl(b, D)], X[:, gsl(b, D)], ACC[0][:, 0, :], ALU.add)\
                      .then_inc(s_gl["x"], 1)
            with dve.Else():
                def edges3(t, u):
                    if active(t, B):
                        dve.wait_ge(s_l3["z"], due((t - 1) * BPG3))
                        nc.vector.tensor_tensor(OH3[u], spread_rank(t), IOTA3, ALU.is_equal)\
                          .then_inc(s_l3["oh"], 1)
                        dve.wait_ge(s_l3["act"], due(t + 1))
                        dve.wait_ge(s_l3r, due((t - 1) * (BPG3 - 1)))
                        nc.vector.tensor_scalar(AC[u], bank(6 + u)[:, 0:NS], 0.0, None, ALU.max)\
                          .then_inc(s_l3["ac"], 1)
                    h = t - 1
                    if active(h, B):
                        v = 1 - u
                        a, msg = ACC[v], MSG[v]
                        for kb in range(1, BPG3 - 1):
                            dve.wait_ge(s_l3r, due(h * (BPG3 - 1) + kb + 1))
                            if kb == 1:
                                dve.wait_ge(s_l3["x"], due(h - 1))
                            else:
                                dve.wait_ge(s_l3["acc"], due(h * (BPG3 - 1) + kb - 1))
                            nc.vector.tensor_tensor(a, msg[0] if kb == 1 else a, msg[kb], ALU.max)\
                              .then_inc(s_l3["acc"], 1)
                        dve.wait_ge(s_l3["z"], due(h * BPG3 + BPG3))
                        nc.vector.tensor_tensor(LAST, bank(BPG3 - 1)[:, 2 * D:4 * D]
                                                .rearrange("p (s o) -> p s o", o=D),
                                                Y[:, gsl(h, D)].rearrange("p (a o) -> p a o", a=1)
                                                .to_broadcast([128, 2, D]), ALU.add).then_inc(s_l3["last"], 1)
                        dve.wait_ge(s_l3["acc"], due(h * (BPG3 - 1) + BPG3 - 2))
                        dve.wait_ge(s_l3["last"], due(h + 1))
                        for q in range(4):
                            s = (BPG3 - 1) * 4 + q
                            last = nc.vector.scalar_tensor_tensor(
                                a[:, q, :], bank(BPG3 - 1)[:, q * D:(q + 1) * D] if q < 2 else LAST[:, q - 2, :],
                                slot_adj(v, h, s), a[:, q, :],
                                ALU.mult, ALU.max)
                        last.then_inc(s_l3["acc"], 1)
                        dve.wait_ge(s_l3["acc"], due((h + 1) * (BPG3 - 1)))
                        nc.vector.tensor_tensor(a[:, 0:2, :], a[:, 0:2, :], a[:, 2:4, :], ALU.max)\
                          .then_inc(s_l3["fold"], 1)
                        dve.wait_ge(s_l3["fold"], due(h * 2 + 1))
                        nc.vector.tensor_tensor(a[:, 0, :], a[:, 0, :], a[:, 1, :], ALU.max)\
                          .then_inc(s_l3["fold"], 1)
                graph_steps(dve, edges3, 1)
            dve.drain().then_inc(s_phase, 1)
            dve.wait_ge(s_phase, 50)

        @block.scalar
        def _(act):
            nc.scalar.preload_act_table_set("natural_log_exp_and_others")
            natural = [io["L1_gnn_Wa"], None, io["L1_gnn_W2"], io["L1_gnn_Wd1"], io["L1_gnn_Wd2"],
                       io["L2_gnn_W1"], io["L2_gnn_W2"]]
            for k, w in enumerate(natural):
                if w is not None:
                    act.dma_start(NATW[:, k, :], w).then_inc(s_w, 16)
            for k in range(4):
                act.dma_start(X[:, k * 4 * GC:(k + 1) * 4 * GC].rearrange("p (b n) -> p b n", n=D),
                              io["x"][k * 4 * GB:(k + 1) * 4 * GB].rearrange("b n d -> n b d")).then_inc(s_x, 16)

            def store_at(t, u):
                if active(t, G):
                    act.wait_ge(s_tp, due(t + 1))
                    nc.scalar.copy(AT[:, gsl(t)], bank(u)).then_inc(s_at, 1)
            group_steps(act, store_at, 0)
            for k in range(0, NW, GB):
                n = min(GB, NW - k)
                act.wait_ge(s_wt, k // GB + 1)
                nc.scalar.copy(WT[:, k:k + n, :], bank(4 + k // GB)[:, 0:n * 128]
                               .rearrange("p (w n) -> p w n", w=n)).then_inc(s_wtc, 1)
            act.wait_ge(s_rowb, 1)
            nc.scalar.copy(ROWB[:, :, :], bank(0).rearrange("p (w n) -> p w n", w=4)).then_inc(s_wtc, 1)

            act.drain().then_inc(s_phase, 1)
            act.wait_ge(s_phase, 5)

            def ln_apply(layer, t, u, free_sem, per):
                act.wait_ge(s_hu, due(t + 1, layer * G))
                act.wait_ge(free_sem, due((t - 1) * per))
                for q in range(GB):
                    last = nc.scalar.activation(
                        HB[u][:, q * D:(q + 1) * D], X[:, bass.ds(t * GC + q * D, D)], ACT.Relu,
                        bias=LNB[:, bass.ds(t * GB + q, 1)], scale=LNS[:, bass.ds(t * GB + q, 1)])
                last.then_inc(s_h, 1)

            def layer0(t, u):
                if active(t - 1, G):
                    ln_apply(0, t - 1, 1 - u, s_p2[0], 1)
                h = t - 2
                if active(h, G):
                    act.wait_ge(s_p2[0], due(h + 1))
                    act.wait_ge(s_p2[2], due(h - 1))
                    nc.scalar.copy(TB[u], bank(u)).then_inc(s_p2[1], 1)
            group_steps(act, layer0, 2)
            act.drain().then_inc(s_phase, 1)
            act.wait_ge(s_phase, 10)

            def into1(t, u):
                if active(t - 1, G):
                    ln_apply(1, t - 1, 1 - u, s_p3[0], 1)
                h = t - 2
                if active(h, G):
                    act.wait_ge(s_p3[0], due(h + 1))
                    act.wait_ge(s_p3[2], due(h - 1))
                    nc.scalar.copy(TB[u], bank(u)).then_inc(s_p3[1], 1)
                e = t - 3
                if active(e, G):
                    act.wait_ge(s_p3[2], due(e + 1))
                    nc.scalar.copy(R[:, gsl(e)], bank(2 + (1 - u))).then_inc(s_p3[3], 1)
            group_steps(act, into1, 3)
            act.drain().then_inc(s_phase, 1)
            act.wait_ge(s_phase, 15)

            def edges1(base):
                def step(m, k, t):
                    h = t - 1
                    if active(h, STEPS):
                        u = (k - 1) % 2
                        act.wait_ge(s_z, due(h + 1, base))
                        act.wait_ge(s_acd, due(h * 16, base * 16))
                        nc.scalar.copy(ZC, bank(0)).then_inc(s_zc, 1)
                        act.wait_ge(s_pre, due(h - 1, base))
                        nc.scalar.activation(GA[u], bank(0), ACT.Square, bias=offc).then_inc(s_sq, 1)
                        act.wait_ge(s_sq, due(h + 1, base))
                        nc.scalar.activation(GA[u], GA[u], ACT.Exp, scale=COEFF).then_inc(s_g, 1)
                    e = t - 2
                    if active(e, STEPS):
                        v = k % 2
                        act.wait_ge(s_hm, due(e - 1, base))
                        act.wait_ge(s_gp2, due(2 * e + 1, base * 2))
                        nc.scalar.copy(GS[v][:, 0:HC], bank(1)).then_inc(s_gc, 1)
                        act.wait_ge(s_pre, due(e + 1, base))
                        act.wait_ge(s_wf, due(e - 1, base))
                        nc.scalar.activation(SP[v], bank(2 if v == 0 else 6, 2), ACT.Exp, bias=b1c).then_inc(s_ex, 1)
                        act.wait_ge(s_gp2, due(2 * e + 2, base * 2))
                        nc.scalar.copy(GS[v][:, HC:CC], bank(1)).then_inc(s_gc, 1)
                        act.wait_ge(s_min, due(e + 1, base))
                        nc.scalar.activation(SP[v], SP[v], ACT.Ln, bias=1.0).then_inc(s_ln, 1)
                return step
            chunk_steps(act, edges1(0), 3)
            act.drain().then_inc(s_phase, 1)
            act.wait_ge(s_phase, 20)

            def late(t, u, r4):
                v = 1 - u
                if isinstance(t, int) and t == 0:
                    act.wait_ge(s_late["b2"], 2)
                    nc.scalar.copy(B2R[:, :], bank(7)[:, 0:N]).then_inc(s_late["b2"], 1)
                h = t - 4
                if active(h, G):
                    act.wait_ge(s_late["pre"], due(h + 1))
                    act.wait_ge(s_late["wf"], due(h - 1))
                    nc.scalar.activation(LSP[u], bank(4), ACT.Exp, bias=b1c).then_inc(s_late["ex"], 1)
                h = t - 3
                if active(h, G):
                    act.wait_ge(s_late["z"], due(h + 1))
                    act.wait_ge(s_late["pre"], due(h))
                    nc.scalar.activation(LGA[0:NG, :], bank(3)[0:NG, :], ACT.Square, bias=offc[0:NG, :])\
                      .then_inc(s_late["sq"], 1)
                    act.wait_ge(s_late["sq"], due(h + 1))
                    nc.scalar.activation(LGA[0:NG, :], LGA[0:NG, :], ACT.Exp, scale=COEFF)\
                      .then_inc(s_late["g"], 1)
                h = t - 1
                if active(h, G):
                    act.wait_ge(s_late["ag"], due(h + 1))
                    act.wait_ge(s_late["pa"], due(h - 1))
                    nc.scalar.copy(AGS[v], bank(0)).then_inc(s_late["ags"], 1)
                h = t - 4
                if active(h, G):
                    act.wait_ge(s_late["mn"], due(h + 1))
                    nc.scalar.activation(LSP[u], LSP[u], ACT.Ln, bias=1.0).then_inc(s_late["ln"], 1)
                h = t - 3
                if active(h, G):
                    act.wait_ge(s_late["rit"], due(h + 1))
                    act.wait_ge(s_late["y"], due(h - 3))
                    nc.scalar.copy(RIT[(r4 - 3) % 4], bank(1)).then_inc(s_late["ritc"], 1)
                h = t - 4
                if active(h, G):
                    act.wait_ge(s_late["acv"], due(h + 1))
                    nc.scalar.activation(ACL[:, gsl(h, GB * LATE)], bank(5)[:, 16:16 + GB * LATE], ACT.Relu)\
                      .then_inc(s_late["acl"], 1)
            general_rounds(act, lambda r: chunk_steps(act, edges1(r * STEPS), 3), late)
            act.drain().then_inc(s_phase, 1)
            act.wait_ge(s_phase, 25)

            def nodes1(t, u):
                if active(t, G):
                    act.wait_ge(s_p5[1], due(t + 1))
                    nc.scalar.activation(TB[u], TB[u], ACT.Exp).then_inc(s_p5[2], 1)
                    act.wait_ge(s_p5[2], due(t + 1))
                    nc.scalar.activation(TB[u], TB[u], ACT.Ln, bias=1.0).then_inc(s_p5[3], 1)
            group_steps(act, nodes1, 0)
            act.drain().then_inc(s_phase, 1)
            act.wait_ge(s_phase, 30)

            def messages(t, u):
                v = 1 - u
                if active(t - 1, G):
                    ln_apply(2, t - 1, v, s_p6[0], 1)
                h = t - 2
                if active(h, G):
                    act.wait_ge(s_p6[0], due(h + 1))
                    nc.scalar.copy(R[:, gsl(h)], bank(u)).then_inc(s_p6[1], 1)
                h = t - 3
                if active(h, G):
                    act.wait_ge(s_p6[2], due(h + 1))
                    act.wait_ge(s_p6[4], due(h - 1))
                    nc.scalar.activation(TB[v], bank(2 + v), ACT.Relu, bias=m1c).then_inc(s_p6[3], 1)
                h = t - 5
                if active(h, G):
                    act.wait_ge(s_p6[6], due(h + 1))
                    nc.scalar.activation(Y[:, gsl(h)], bank(6 + v), ACT.Relu).then_inc(s_p6[7], 1)
            group_steps(act, messages, 5, head=8)
            act.drain().then_inc(s_phase, 1)
            act.wait_ge(s_phase, 35)

            def gates(t, u):
                if active(t, G):
                    act.wait_ge(s_p8[0], due(t + 1))
                    act.wait_ge(s_p8[8], due(t - 1))
                    for k in range(2):
                        last = nc.scalar.activation(RZ[u][:, k * GC:(k + 1) * GC], bank(6 * u + k), ACT.Sigmoid,
                                                    bias=brz[:, k:k + 1])
                    last.then_inc(s_p8[2], 1)
                    act.wait_ge(s_p8[4], due(t + 1))
                    nc.scalar.activation(NB_[u], VB[u], ACT.Tanh, bias=bin_).then_inc(s_p8[5], 1)
            group_steps(act, gates, 0)
            act.drain().then_inc(s_phase, 1)
            act.wait_ge(s_phase, 40)

            def into3(t, u):
                if active(t - 1, G):
                    ln_apply(3, t - 1, 1 - u, s_p9[0], 1)
                h = t - 2
                if active(h, G):
                    act.wait_ge(s_p9[0], due(h + 1))
                    act.wait_ge(s_p9[2], due(h - 1))
                    nc.scalar.copy(TB[u], bank(u)).then_inc(s_p9[1], 1)
                h = t - 3
                if active(h, G):
                    act.wait_ge(s_p9[3], due(h + 1))
                    pq = bank(4 if u else 6, 2).rearrange("p (b w n) -> p b w n", b=GB, w=2)
                    nc.scalar.copy(by4(R[:, gsl(h)]), pq[:, :, 1, :]).then_inc(s_p9[4], 1)
            group_steps(act, into3, 3)
            act.drain().then_inc(s_phase, 1)
            act.wait_ge(s_phase, 45)

            many = act.value_load(FLAG[0:1, 0:1], min_val=0, max_val=1)
            with act.If(many > 0):
                act.nop()
            with act.Else():
                def edges3(t, u):
                    if active(t, B):
                        act.wait_ge(s_l3["z"], due((t - 1) * BPG3))
                        nc.scalar.copy(PARTS[u][:, 0], YR[:, :, gsl(t, 128)]).then_inc(s_l3["c1"], 1)
                    h = t - 1
                    for kb in range(BPG3 - 1):
                        if active(h, B):
                            v = 1 - u
                            act.wait_ge(s_l3["ac"], due(h + 1))
                            act.wait_ge(s_l3["z"], due(h * BPG3 + kb + 1))
                            act.wait_ge(s_l3["acc"], due((h - 1) * (BPG3 - 1)))
                            for q in range(4):
                                s = kb * 4 + q
                                last = nc.scalar.activation(MSG[v][kb][:, q, :], bank(kb)[:, q * D:(q + 1) * D],
                                                            ACT.Relu, scale=slot_adj(v, h, s))
                            last.then_inc(s_l3r, 1)
                        if kb == 1 and active(t, B):
                            act.wait_ge(s_l3["r1"], due(t + 1))
                            nc.scalar.copy(PARTS[u][:, 1], REM[u]).then_inc(s_l3["c2"], 1)
                graph_steps(act, edges3, 1)
            act.drain().then_inc(s_phase, 1)
            act.wait_ge(s_phase, 50)

        @block.tensor
        def _(pe):
            mm = nc.tensor.matmul
            pe.wait_ge(s_gp, 13)
            def ranks(t, u, r4):
                if active(t, G):
                    pe.wait_ge(s_adj[r4], (t - r4) * 4 + 16)
                    pe.wait_ge(s_at, due(t - 1))
                    for q in range(GB):
                        last = nc.tensor.transpose(bank(u)[:, q * N:(q + 1) * N], g4(ADJ[r4], q),
                                                   ident[:, :])
                    last.then_inc(s_tp, 1)
                h = t - 1
                if active(h, G):
                    v = 1 - u
                    pe.wait_ge(s_mask, due(h * 2 + 1))
                    pe.wait_ge(s_rks, due((h - 1) * 2))
                    mm(bank(2 + v), upto[:, :], MASK[v], start=True, stop=True)
                    for q in range(GB):
                        last = mm(bank(4 + v)[:, q:q + 1], g4(MASK[v], q), onesb[:, 0:1], start=(q == 0), stop=True,
                                  skip_group_check=True)
                    last.then_inc(s_rank, 1)
            ring_steps(pe, ranks, 1)
            pe.wait_ge(s_off, 2)
            mm(bank(7)[:, 0:2 * B], upto[:, :], OVB[:, :], start=True, stop=True).then_inc(s_off, 1)
            pe.wait_ge(s_off, 5)
            pe.wait_ge(s_flag, 1)
            pe.wait_ge(s_w, 16 * LOADS)
            for k in range(0, NW, GB):
                for q in range(k, min(k + GB, NW)):
                    last = nc.tensor.transpose(bank(4 + k // GB)[:, (q - k) * 128:(q - k + 1) * 128],
                                               NATW[:, q, :], ident[:, :])
                last.then_inc(s_wt, 1)
            pe.wait_ge(s_at, G)
            pe.wait_ge(s_wtc, 2)
            pe.wait_ge(s_prep, 1)
            mm(bank(0), ONE[0:1, :], ROWN[0:1, :], start=True, stop=True, skip_group_check=True)
            mm(bank(0)[:, 128:256], MLN2, WT[:, WD2, :], start=False, stop=True, skip_group_check=True)\
                .then_inc(s_rowb, 1)
            pe.drain().then_inc(s_phase, 1)
            pe.wait_ge(s_phase, 5)

            def layer0(t, u):
                e = t - 3
                if active(e, G):
                    v = 1 - u
                    pe.wait_ge(s_p2[1], due(e + 1))
                    pe.wait_ge(s_p2[3], due(e - 1))
                    for q in range(GB):
                        last = mm(bank(2 + v)[:, q * D:(q + 1) * D], TB[v][:, q * N:(q + 1) * N], W0[:, :],
                                  start=(q == 0), stop=True, skip_group_check=True)
                    last.then_inc(s_p2[2], 1)
                h = t - 2
                if active(h, G):
                    pe.wait_ge(s_h, due(h + 1))
                    pe.wait_ge(s_p2[1], due(h - 1))
                    for q in range(GB):
                        last = mm(bank(u)[:, q * N:(q + 1) * N], HB[u][:, q * D:(q + 1) * D],
                                  AT[:, bass.ds(h * GC + q * N, N)], start=(q == 0), stop=True, skip_group_check=True)
                    last.then_inc(s_p2[0], 1)
            group_steps(pe, layer0, 3)
            pe.drain().then_inc(s_phase, 1)
            pe.wait_ge(s_phase, 10)

            def transpose_h(v, out, ready, count):
                for q in range(GB):
                    last = nc.tensor.transpose(out[:, q * N:(q + 1) * N], HB[v][:, q * D:(q + 1) * D], ident[:, :])
                last.then_inc(ready, 1)

            def into1(t, u):
                e = t - 3
                if active(e, G):
                    v = 1 - u
                    pe.wait_ge(s_p3[1], due(e + 1))
                    pe.wait_ge(s_p3[3], due(e - 1))
                    for q in range(GB):
                        last = mm(bank(2 + v)[:, q * D:(q + 1) * D], TB[v][:, q * N:(q + 1) * N], WT[:, WA, :],
                                  start=(q == 0), stop=True, skip_group_check=True)
                    last.then_inc(s_p3[2], 1)
                h = t - 2
                if active(h, G):
                    pe.wait_ge(s_h, due(h + 1, G))
                    pe.wait_ge(s_p3[1], due(h - 1))
                    transpose_h(u, bank(u), s_p3[0], 1)
            group_steps(pe, into1, 3)
            pe.drain().then_inc(s_phase, 1)
            pe.wait_ge(s_phase, 15)

            def edges1(base, rbase):
                def step(m, k, t):
                    h = t - 1
                    if active(h, STEPS):
                        u = (k - 1) % 2
                        pe.wait_ge(s_pa, due(h + 1, base))
                        pe.wait_ge(s_sq, due(h, base))
                        mm(PS[0:NG, 0:512], ones[:, :], PA[u][:, 0:HC], start=True, stop=True)
                        mm(PS[NG:128, 0:512], ones[:, :], PA[u][:, HC:CC], start=True, stop=True).then_inc(s_z, 1)
                    e = t - 2
                    if active(e, STEPS):
                        v = k % 2
                        ek = (k - 2) % UNROLL
                        b, slot, split = place(m if k >= 2 else m - 1, ek)
                        gq = 2 * ek // BPG

                        def gather(q):
                            nb, nq = (b + 1, gq + 1) if split and q else (b, gq)
                            if (slot == 0 and q == 0) or (split and q):
                                pe.wait_ge(s_rf, due(nb + 1, rbase))
                            pe.wait_ge(s_gc, due(2 * e + q, base * 2))
                            mm(bank(1), RF[nq % GB], PA2[v][:, q * HC:(q + 1) * HC], start=True, stop=True)\
                                .then_inc(s_gp2, 1)
                        pe.wait_ge(s_pa2, due(e + 1, base))
                        gather(0)
                        pe.wait_ge(s_g, due(e + 1, base))
                        pe.wait_ge(s_sp, due(e - 1, base))
                        for q in range(2):
                            last = mm(bank((2 if v == 0 else 6) + q), WT[q * NG:(q + 1) * NG, W1, :],
                                      GA[v][q * NG:(q + 1) * NG, :], start=True, stop=True)
                        last.then_inc(s_pre, 1)
                    f = t - 3

                    def filters(q):
                        return mm(bank(4 + q), WT[:, W2, :], SP[(k - 3) % 2][:, q * HC:(q + 1) * HC],
                                  start=True, stop=True)
                    if active(f, STEPS):
                        pe.wait_ge(s_sp, due(f + 1, base))
                        pe.wait_ge(s_hm, due(f, base))
                        filters(0)
                    if active(e, STEPS):
                        gather(1)
                    if active(f, STEPS):
                        filters(1).then_inc(s_wf, 1)
                return step
            chunk_steps(pe, edges1(0, 0), 3)
            pe.drain().then_inc(s_phase, 1)
            pe.wait_ge(s_phase, 20)

            def late(t, u, r4):
                v = 1 - u
                if isinstance(t, int) and t == 0:
                    pe.wait_ge(s_late["b2"], 1)
                    mm(PS[0:NG, 7 * 512:7 * 512 + N], ones[:, :], LM[:, 0:N], start=True, stop=True)
                    mm(PS[NG:128, 7 * 512:7 * 512 + N], ones[:, :], LM[:, 0:N], start=True, stop=True)\
                        .then_inc(s_late["b2"], 1)
                h = t - 4
                if active(h, G):
                    pe.wait_ge(s_late["g"], due(h + 1))
                    pe.wait_ge(s_late["sp"], due(h))
                    mm(bank(4), WT[0:NG, W1, :], LGA[0:NG, :], start=True, stop=True).then_inc(s_late["pre"], 1)
                h = t - 5
                if active(h, G):
                    pe.wait_ge(s_late["sp"], due(h + 1))
                    pe.wait_ge(s_late["b2"], 3)
                    pe.wait_ge(s_late["m1"], due(h))
                    for q in range(GB):
                        last = mm(g4(bank(7), q), g4(LSP[v], q), WT[:, W2, :], start=(q == 0), stop=True,
                                  skip_group_check=True)
                    last.then_inc(s_late["wf"], 1)
                h = t - 3
                if active(h, G):
                    pe.wait_ge(s_late["pa"], due(h + 1))
                    pe.wait_ge(s_late["sq"], due(h))
                    mm(PS[0:NG, 3 * 512:4 * 512], ones[:, :], LPA[v], start=True, stop=True).then_inc(s_late["z"], 1)
                h = t - 6
                if active(h, G):
                    pe.wait_ge(s_late["m2"], due(h + 1))
                    pe.wait_ge(s_late["ritc"], due(min(h + 3, G) if isinstance(t, int) else h + 3))
                    for q in range(GB):
                        last = mm(g4(bank(1), q), g4(LM, q), g4(RIT[(r4 - 6) % 4], q), start=(q == 0), stop=True,
                                  skip_group_check=True)
                    last.then_inc(s_late["y"], 1)
                h = t - 1
                if active(h, G):
                    pe.wait_ge(s_ladj[v], (h - v) * 8 + 16)
                    pe.wait_ge(s_late["ri"], due(h + 1))
                    pe.wait_ge(s_late["ags"], due(h))
                    for q in range(GB):
                        last = mm(g4(bank(0), q), g4(LADJ[v], q), g4(RI[(r4 - 1) % 4], q), start=(q == 0), stop=True,
                                  skip_group_check=True)
                    last.then_inc(s_late["ag"], 1)
                h = t - 2
                if active(h, G):
                    pe.wait_ge(s_late["ma"], due(h + 1))
                    pe.wait_ge(s_late["rio"], due(h + 1))
                    pe.wait_ge(s_late["pa"], due(h))
                    mm(bank(2), upto[:, :], MA[u], start=True, stop=True, skip_group_check=True)
                    mm(bank(2), onesb[0:1, :], NEGC[0:1, :], start=False, stop=True, skip_group_check=True)
                    mm(bank(2), onesb[:, :], RIO[(r4 - 2) % 4], start=False, stop=True, skip_group_check=True)\
                        .then_inc(s_late["rk"], 1)
                h = t - 3
                if active(h, G):
                    pe.wait_ge(s_late["d"], due(h))
                    pe.wait_ge(s_late["acl"], due(h - 1))
                    for q in range(GB):
                        mm(bank(5)[:, q:q + 1], g4(LPA[v], q), ones[:, 0:1], start=(q == 0), stop=True,
                           skip_group_check=True)
                    for q in range(GB):
                        last = mm(bank(5)[:, GB + q:GB + q + 1], g4(RIO[(r4 - 3) % 4], q), onesb[:, 0:1],
                                  start=False, stop=True, skip_group_check=True)
                    last.then_inc(s_late["sm"], 1)
                h = t - 4
                if active(h, G):
                    pe.wait_ge(s_late["pa2"], due(h + 1))
                    pe.wait_ge(s_late["m2"], due(h))
                    for q in range(GB):
                        last = mm(g4(bank(6), q), g4(LPA2[u], q), R[:, bass.ds(h * GC + q * D, D)], start=(q == 0),
                                  stop=True, skip_group_check=True)
                    last.then_inc(s_late["gath"], 1)
                h = t - 3
                if active(h, G):
                    pe.wait_ge(s_late["ya"], due(h - 2))
                    pe.wait_ge(s_late["ritc"], due(h))
                    for q in range(GB):
                        last = nc.tensor.transpose(g4(bank(1), q), g4(RI[(r4 - 3) % 4], q), ident[:, :])
                    last.then_inc(s_late["rit"], 1)
                h = t - 4
                if active(h, G):
                    pe.wait_ge(s_late["d"], due(min(h + 2, G) if isinstance(t, int) else h + 2))
                    pe.wait_ge(s_late["acl"], due(h))
                    pe.wait_ge(s_late["ritc"], due(h + 1))
                    for q in range(GB):
                        last = mm(bank(5)[:, 16 + q * LATE:16 + (q + 1) * LATE], g4(RIT[r4], q),
                                  LD[u][:, q * LATE:(q + 1) * LATE], start=(q == 0), stop=True, skip_group_check=True)
                    last.then_inc(s_late["acv"], 1)
            general_rounds(pe, lambda r: chunk_steps(pe, edges1(r * STEPS, r * B), 3), late)
            pe.drain().then_inc(s_phase, 1)
            pe.wait_ge(s_phase, 25)

            def nodes1(t, u):
                h = t - 2
                if active(h, G):
                    pe.wait_ge(s_p5[4], due(h + 1))
                    pe.wait_ge(s_p5[6], due(h - 1))
                    for q in range(GB):
                        last = mm(bank(2 + u)[:, q * D:(q + 1) * D], TB[u][:, q * N:(q + 1) * N], WT[:, WD2, :],
                                  start=(q == 0), stop=True, skip_group_check=True)
                    last.then_inc(s_p5[5], 1)
                if active(t, G):
                    pe.wait_ge(s_p5[4], due(t - 1))
                    mm(bank(u), WT[:, WD1, :], Y[:, gsl(t)], start=True, stop=True).then_inc(s_p5[0], 1)
            group_steps(pe, nodes1, 2)
            pe.drain().then_inc(s_phase, 1)
            pe.wait_ge(s_phase, 30)

            def messages(t, u):
                v = 1 - u
                h = t - 5
                if active(h, G):
                    pe.wait_ge(s_p6[5], due(h + 1))
                    pe.wait_ge(s_p6[7], due(h - 1))
                    for q in range(GB):
                        last = mm(bank(6 + v)[:, q * N:(q + 1) * N], UB[v][:, q * D:(q + 1) * D],
                                  AT[:, bass.ds(h * GC + q * N, N)], start=(q == 0), stop=True, skip_group_check=True)
                    last.then_inc(s_p6[6], 1)
                h = t - 4
                if active(h, G):
                    pe.wait_ge(s_p6[3], due(h + 1))
                    pe.wait_ge(s_p6[5], due(h - 1))
                    for q in range(GB):
                        last = mm(bank(4 + u)[:, q * D:(q + 1) * D], TB[u][:, q * N:(q + 1) * N], WT[:, M2, :],
                                  start=(q == 0), stop=True, skip_group_check=True)
                    last.then_inc(s_p6[4], 1)
                h = t - 3
                if active(h, G):
                    pe.wait_ge(s_p6[1], due(h + 1))
                    pe.wait_ge(s_p6[3], due(h - 1))
                    mm(bank(2 + v), WT[:, M1, :], R[:, gsl(h)], start=True, stop=True).then_inc(s_p6[2], 1)
                h = t - 2
                if active(h, G):
                    pe.wait_ge(s_h, due(h + 1, 2 * G))
                    pe.wait_ge(s_p6[1], due(h - 1))
                    transpose_h(u, bank(u), s_p6[0], 1)
            group_steps(pe, messages, 5, head=8)
            pe.drain().then_inc(s_phase, 1)
            pe.wait_ge(s_phase, 35)

            def gates(t, u):
                if active(t, G):
                    msg, ht = Y[:, gsl(t)], R[:, gsl(t)]
                    pe.wait_ge(s_p8[2], due(t - 1))
                    for k in range(2):
                        mm(bank(6 * u + k), WT[:, IH + k, :], msg, start=True, stop=False)
                        last = mm(bank(6 * u + k), WT[:, HH + k, :], ht, start=False, stop=True)
                    last.then_inc(s_p8[0], 1)
                    pe.wait_ge(s_p8[4], due(t))
                    mm(bank(2), WT[:, IH + 2, :], msg, start=True, stop=True)
                    mm(bank(3), WT[:, HH + 2, :], ht, start=True, stop=True).then_inc(s_p8[1], 1)
                h = t - 2
                if active(h, G):
                    pe.wait_ge(s_p8[8], due(h + 1))
                    pe.wait_ge(s_p8[10], due(h - 1))
                    for q in range(GB):
                        last = nc.tensor.transpose(bank(4 + u)[:, q * N:(q + 1) * N],
                                                   UB[u][:, q * D:(q + 1) * D], ident[:, :])
                    last.then_inc(s_p8[9], 1)
            group_steps(pe, gates, 2)
            pe.drain().then_inc(s_phase, 1)
            pe.wait_ge(s_phase, 40)

            def into3(t, u):
                h = t - 3
                if active(h, G):
                    v = 1 - u
                    pe.wait_ge(s_p9[1], due(h + 1))
                    pe.wait_ge(s_p9[4], due(h - 1))
                    pq = bank(6 if v else 4, 2)
                    for q in range(GB):
                        last = mm(pq[:, q * 256:(q + 1) * 256], TB[v][:, q * N:(q + 1) * N], W3[:, :, :],
                                  start=(q % 2 == 0), stop=True, skip_group_check=True)
                    last.then_inc(s_p9[2], 1)
                h = t - 2
                if active(h, G):
                    pe.wait_ge(s_h, due(h + 1, 3 * G))
                    pe.wait_ge(s_p9[1], due(h - 1))
                    transpose_h(u, bank(u), s_p9[0], 1)
            group_steps(pe, into3, 3)
            pe.drain().then_inc(s_phase, 1)
            pe.wait_ge(s_phase, 45)

            def slots(parts, oh, zb, kb, with_p=4):
                for k in range(3):
                    mm(zb[:, 0:with_p * D], identb[:, :], parts[:, k, 0:1, :].to_broadcast([128, with_p, D]),
                       start=(k == 0), stop=True, skip_group_check=True)
                for q in range(4):
                    for k in range(3):
                        last = mm(zb[:, q * D:(q + 1) * D], oh[:, kb * 4 + q, :], parts[:, k, 1, :],
                                  start=False, stop=True, skip_group_check=True)
                return last

            many = pe.value_load(FLAG[0:1, 0:1], min_val=0, max_val=1)
            with pe.If(many > 0):
                with pe.Fori(0, B) as b:
                    with pe.Fori(0, NR) as r:
                        n = b * NR + r
                        pe.wait_ge(s_gl["ac"], due(n * 16 + 16))
                        pe.wait_ge(s_gl["acs"], due(n + 1))
                        pe.sem_inc(s_passed, 1)
                        nc.tensor.transpose(bank(6)[:, 0:NS], ACT_[0][0:NS, :], ident[0:NS, 0:NS])\
                            .then_inc(s_gl["act"], 1)
                        pe.wait_ge(s_gl["oh"], due(n + 1))
                        pe.wait_ge(s_gl["c3"], due(b + 1))
                        for kb in range(BPG):
                            pe.wait_ge(s_gl["acc"], due(n * BPG + max(kb - 1, 0) + 1))
                            slots(PARTS[0], OH3[0], bank(kb % 2), kb).then_inc(s_gl["z"], 1)
            with pe.Else():
                def edges3(t, u):
                    if active(t, B):
                        pe.wait_ge(s_l3[f"ac{u}"], (t - u) * 8 + 16)
                        pe.wait_ge(s_l3["ac"], due(t - 1))
                        pe.sem_inc(s_passed, 1)
                        nc.tensor.transpose(bank(6 + u)[:, 0:NS], ACT_[u][0:NS, :], ident[0:NS, 0:NS])\
                            .then_inc(s_l3["act"], 1)
                    h = t - 1
                    if active(h, B):
                        v = 1 - u
                        pe.wait_ge(s_l3["oh"], due(h + 1))
                        pe.wait_ge(s_l3["c3"], due(h + 1))
                        for kb in range(BPG3):
                            if kb < BPG3 - 1:
                                pe.wait_ge(s_l3r, due((h - 1) * (BPG3 - 1) + kb + 1))
                            else:
                                pe.wait_ge(s_l3["acc"], due(h * (BPG3 - 1)))
                            slots(PARTS[v], OH3[v], bank(kb), kb, 4 if kb < BPG3 - 1 else 2).then_inc(s_l3["z"], 1)
                graph_steps(pe, edges3, 1)
            pe.drain().then_inc(s_phase, 1)
            pe.wait_ge(s_phase, 50)


_INS = ['x', 'adj', 'L0_gnn_W', 'L0_gnn_b', 'L1_gnn_W1', 'L1_gnn_b1', 'L1_gnn_W2', 'L1_gnn_b2', 'L1_gnn_Wa',
        'L1_gnn_Wd1', 'L1_gnn_bd1', 'L1_gnn_Wd2', 'L1_gnn_bd2', 'L2_gnn_W1', 'L2_gnn_b1', 'L2_gnn_W2',
        'L2_gnn_b2', 'L2_gnn_W_ih', 'L2_gnn_W_hh', 'L2_gnn_b_ih', 'L2_gnn_b_hh', 'L3_gnn_W', 'L3_gnn_b']


def kernel(**inputs):
    import concourse.bacc as bacc
    from concourse.bass_utils import run_bass_kernel_spmd

    nc = bacc.Bacc("TRN2", target_bir_lowering=False, num_devices=1, dynamic_dma_scratch_size=1024)
    arrays, io = {}, {}
    for name in _INS:
        a = np.ascontiguousarray(inputs[name])
        arrays[name + "_dram"] = a
        io[name] = nc.dram_tensor(name + "_dram", a.shape, mybir.dt.from_np(a.dtype), kind="ExternalInput").ap()
    io["out"] = nc.dram_tensor("out_dram", (B, N, D), F32, kind="ExternalOutput").ap()
    build(nc, io)
    r = run_bass_kernel_spmd(nc, [arrays], core_ids=[0])
    return r.results[0]["out_dram"]
```
